# Optimizing a Trainium2 kernel written in Bass

```python
import numpy as np
import jax
import jax.numpy as jnp

def _softmax(x, axis=-1):
    return jax.nn.softmax(x, axis=axis)

def _gelu(x):
    return jax.nn.gelu(x, approximate=True)

def _silu(x):
    return jax.nn.silu(x)

def _sigmoid(x):
    return jax.nn.sigmoid(x)

def _layernorm(x, axis=-1, eps=1e-05):
    m = jnp.mean(x, axis=axis, keepdims=True)
    v = jnp.var(x, axis=axis, keepdims=True)
    return (x - m) / jnp.sqrt(v + eps)

def _scatter_add(tgt, idx, src, axis=0):
    return tgt.at[idx].add(src)

def _segment_sum(src, seg, n):
    return jax.ops.segment_sum(src, seg, n)
kernel_name = 'mk_gps_d1_gnn_r32_b41e5e'

def setup_inputs(seed: int=0):
    np.random.seed(seed)
    _w = jnp.asarray

    def _rec_inputs():
        import jax
        import jax.numpy as jnp
        _gk = jax.random.key(seed)
        x = -0.0002117 + 1 * jax.random.normal(jax.random.fold_in(_gk, 1), (3125, 256), jnp.float32)
        src = jax.random.randint(jax.random.fold_in(_gk, 2), (50000,), 0, 3125, jnp.int32)
        dst = jax.random.randint(jax.random.fold_in(_gk, 3), (50000,), 0, 3125, jnp.int32)
        _o = jnp.argsort(dst, stable=True)
        src = src[_o]
        dst = dst[_o]
        return (x, src, dst)
    x, src, dst = _rec_inputs()

    def _L0_gnn_setup():
        import jax, jax.numpy as jnp
        import numpy as np
        N_NODES = 3125
        N_EDGES = 50000
        NUM_CLASSES = 256
        HIDDEN = 128

        def _gcn_norm(edge_index, num_nodes):
            src, dst = (edge_index[0], edge_index[1])
            loop = jnp.arange(num_nodes, dtype=src.dtype)
            src = jnp.concatenate([src, loop])
            dst = jnp.concatenate([dst, loop])
            deg = jax.ops.segment_sum(jnp.ones_like(dst, dtype=jnp.float32), dst, num_segments=num_nodes)
            deg_inv_sqrt = jnp.where(deg > 0, jax.lax.rsqrt(deg), 0.0)
            norm = deg_inv_sqrt[src] * deg_inv_sqrt[dst]
            return (src, dst, norm)

        def _gcn_conv(x, W, b, src, dst, norm, num_nodes):
            h = x @ W
            msgs = h[src] * norm[:, None]
            out = jax.ops.segment_sum(msgs, dst, num_segments=num_nodes)
            return out + b
        key = jax.random.key(seed)
        k1, k2, k3, k4 = jax.random.split(key, 4)
        x = jax.random.normal(k1, (N_NODES, NUM_CLASSES), dtype=jnp.float32)
        edge_index = jax.random.randint(k2, (2, N_EDGES), 0, N_NODES, dtype=jnp.int32)
        W1 = jax.random.normal(k3, (NUM_CLASSES, HIDDEN), dtype=jnp.float32) / np.sqrt(NUM_CLASSES)
        b1 = jnp.zeros((HIDDEN,), dtype=jnp.float32)
        W2 = jax.random.normal(k4, (HIDDEN, NUM_CLASSES), dtype=jnp.float32) / np.sqrt(HIDDEN)
        b2 = jnp.zeros((NUM_CLASSES,), dtype=jnp.float32)
        return {'x': x, 'edge_index': edge_index, 'W1': W1, 'b1': b1, 'W2': W2, 'b2': b2}
    _L0_gnn_all = _L0_gnn_setup()
    _L0_gnn_in = {k: v for k, v in _L0_gnn_all.items() if k in ('W1', 'b1', 'W2', 'b2')}
    del _L0_gnn_all

    def _L0_mix_setup():
        import jax, jax.numpy as jnp
        import numpy as np
        import math
        EMBED = 256
        HEADS = 4
        HEAD_DIM = EMBED // HEADS
        OUT_DIM = 256
        LN_EPS = 1e-05

        def _qkv_init(key):
            spread = math.sqrt(3.0 / EMBED)
            gain, delta = (0.01, 0.01)
            w = jax.random.uniform(key, (EMBED, EMBED), minval=-spread, maxval=spread) * gain
            return w + delta * jnp.eye(EMBED, dtype=w.dtype)

        def _layer_norm(x, g, b):
            mu = jnp.mean(x, axis=-1, keepdims=True)
            var = jnp.mean(jnp.square(x - mu), axis=-1, keepdims=True)
            return (x - mu) * jax.lax.rsqrt(var + LN_EPS) * g + b

        def _split_heads(x, B, S):
            return x.reshape(B, S, HEADS, HEAD_DIM).transpose(0, 2, 1, 3)
        key = jax.random.key(seed)
        ks = jax.random.split(key, 6)
        seq = jax.random.normal(ks[0], (4, 256, EMBED), dtype=jnp.float32)
        wq = _qkv_init(ks[1])
        wk = _qkv_init(ks[2])
        wv = _qkv_init(ks[3])
        bound = 1.0 / math.sqrt(EMBED)
        wo = jax.random.uniform(ks[4], (OUT_DIM, EMBED), minval=-bound, maxval=bound)
        bo = jax.random.uniform(ks[5], (OUT_DIM,), minval=-bound, maxval=bound)
        ln_k_g = jnp.ones((HEAD_DIM,), jnp.float32)
        ln_k_b = jnp.zeros((HEAD_DIM,), jnp.float32)
        ln_v_g = jnp.ones((HEAD_DIM,), jnp.float32)
        ln_v_b = jnp.zeros((HEAD_DIM,), jnp.float32)
        return {'seq': seq, 'wq': wq, 'wk': wk, 'wv': wv, 'wo': wo, 'bo': bo, 'ln_k_g': ln_k_g, 'ln_k_b': ln_k_b, 'ln_v_g': ln_v_g, 'ln_v_b': ln_v_b}
    _L0_mix_all = _L0_mix_setup()
    _L0_mix_in = {k: v for k, v in _L0_mix_all.items() if k in ('wq', 'wk', 'wv', 'wo', 'bo', 'ln_k_g', 'ln_k_b', 'ln_v_g', 'ln_v_b')}
    del _L0_mix_all

    def _L0_ffn_setup():
        import jax, jax.numpy as jnp
        import numpy as np
        DIM = 256
        H = 8
        D = 64
        G = 64
        INNER = H * D
        SCALE = D ** (-0.5)
        key = jax.random.key(seed)
        ks = jax.random.split(key, 12)
        B, N = (4, 512)
        x = jax.random.normal(ks[0], (B, N, DIM), dtype=jnp.float32)
        s = lambda fan_in: 1.0 / np.sqrt(fan_in)
        W_fx = jax.random.normal(ks[1], (DIM, INNER), dtype=jnp.float32) * s(DIM)
        b_fx = jnp.zeros((INNER,), dtype=jnp.float32)
        W_x = jax.random.normal(ks[2], (DIM, INNER), dtype=jnp.float32) * s(DIM)
        b_x = jnp.zeros((INNER,), dtype=jnp.float32)
        A = jax.random.normal(ks[3], (G, D), dtype=jnp.float32)
        Q, _ = jnp.linalg.qr(A.T)
        W_slice = Q[:, :G].astype(jnp.float32)
        b_slice = jnp.zeros((G,), dtype=jnp.float32)
        W_q = jax.random.normal(ks[4], (D, D), dtype=jnp.float32) * s(D)
        W_k = jax.random.normal(ks[5], (D, D), dtype=jnp.float32) * s(D)
        W_v = jax.random.normal(ks[6], (D, D), dtype=jnp.float32) * s(D)
        W_out = jax.random.normal(ks[7], (INNER, DIM), dtype=jnp.float32) * s(INNER)
        b_out = jnp.zeros((DIM,), dtype=jnp.float32)
        temperature = jnp.ones((1, H, 1, 1), dtype=jnp.float32) * 0.5
        return {'x': x, 'W_fx': W_fx, 'b_fx': b_fx, 'W_x': W_x, 'b_x': b_x, 'W_slice': W_slice, 'b_slice': b_slice, 'W_q': W_q, 'W_k': W_k, 'W_v': W_v, 'W_out': W_out, 'b_out': b_out, 'temperature': temperature}
    _L0_ffn_all = _L0_ffn_setup()
    _L0_ffn_in = {k: v for k, v in _L0_ffn_all.items() if k in ('W_fx', 'b_fx', 'W_x', 'b_x', 'W_slice', 'b_slice', 'W_q', 'W_k', 'W_v', 'W_out', 'b_out', 'temperature')}
    del _L0_ffn_all
    return {'x': x, 'src': src, 'dst': dst, 'L0_gnn_W1': _L0_gnn_in['W1'], 'L0_gnn_b1': _L0_gnn_in['b1'], 'L0_gnn_W2': _L0_gnn_in['W2'], 'L0_gnn_b2': _L0_gnn_in['b2'], 'L0_mix_wq': _L0_mix_in['wq'], 'L0_mix_wk': _L0_mix_in['wk'], 'L0_mix_wv': _L0_mix_in['wv'], 'L0_mix_wo': _L0_mix_in['wo'], 'L0_mix_bo': _L0_mix_in['bo'], 'L0_mix_ln_k_g': _L0_mix_in['ln_k_g'], 'L0_mix_ln_k_b': _L0_mix_in['ln_k_b'], 'L0_mix_ln_v_g': _L0_mix_in['ln_v_g'], 'L0_mix_ln_v_b': _L0_mix_in['ln_v_b'], 'L0_ffn_W_fx': _L0_ffn_in['W_fx'], 'L0_ffn_b_fx': _L0_ffn_in['b_fx'], 'L0_ffn_W_x': _L0_ffn_in['W_x'], 'L0_ffn_b_x': _L0_ffn_in['b_x'], 'L0_ffn_W_slice': _L0_ffn_in['W_slice'], 'L0_ffn_b_slice': _L0_ffn_in['b_slice'], 'L0_ffn_W_q': _L0_ffn_in['W_q'], 'L0_ffn_W_k': _L0_ffn_in['W_k'], 'L0_ffn_W_v': _L0_ffn_in['W_v'], 'L0_ffn_W_out': _L0_ffn_in['W_out'], 'L0_ffn_b_out': _L0_ffn_in['b_out'], 'L0_ffn_temperature': _L0_ffn_in['temperature']}

def reference(x, src, dst, L0_gnn_W1, L0_gnn_b1, L0_gnn_W2, L0_gnn_b2, L0_mix_wq, L0_mix_wk, L0_mix_wv, L0_mix_wo, L0_mix_bo, L0_mix_ln_k_g, L0_mix_ln_k_b, L0_mix_ln_v_g, L0_mix_ln_v_b, L0_ffn_W_fx, L0_ffn_b_fx, L0_ffn_W_x, L0_ffn_b_x, L0_ffn_W_slice, L0_ffn_b_slice, L0_ffn_W_q, L0_ffn_W_k, L0_ffn_W_v, L0_ffn_W_out, L0_ffn_b_out, L0_ffn_temperature):
    import jax
    import jax.numpy as jnp

    def _L0_gnn_ref(x, edge_index, W1, b1, W2, b2):
        import jax, jax.numpy as jnp
        import numpy as np
        N_NODES = 3125
        N_EDGES = 50000
        NUM_CLASSES = 256
        HIDDEN = 128

        def _gcn_norm(edge_index, num_nodes):
            src, dst = (edge_index[0], edge_index[1])
            loop = jnp.arange(num_nodes, dtype=src.dtype)
            src = jnp.concatenate([src, loop])
            dst = jnp.concatenate([dst, loop])
            deg = jax.ops.segment_sum(jnp.ones_like(dst, dtype=jnp.float32), dst, num_segments=num_nodes)
            deg_inv_sqrt = jnp.where(deg > 0, jax.lax.rsqrt(deg), 0.0)
            norm = deg_inv_sqrt[src] * deg_inv_sqrt[dst]
            return (src, dst, norm)

        def _gcn_conv(x, W, b, src, dst, norm, num_nodes):
            h = x @ W
            msgs = h[src] * norm[:, None]
            out = jax.ops.segment_sum(msgs, dst, num_segments=num_nodes)
            return out + b
        n = x.shape[0]
        src, dst, norm = _gcn_norm(edge_index, n)
        h = jax.nn.relu(_gcn_conv(x, W1, b1, src, dst, norm, n))
        out = _gcn_conv(h, W2, b2, src, dst, norm, n)
        return out

    def _L0_mix_ref(seq, wq, wk, wv, wo, bo, ln_k_g, ln_k_b, ln_v_g, ln_v_b):
        import jax, jax.numpy as jnp
        import numpy as np
        import math
        EMBED = 256
        HEADS = 4
        HEAD_DIM = EMBED // HEADS
        OUT_DIM = 256
        LN_EPS = 1e-05

        def _qkv_init(key):
            spread = math.sqrt(3.0 / EMBED)
            gain, delta = (0.01, 0.01)
            w = jax.random.uniform(key, (EMBED, EMBED), minval=-spread, maxval=spread) * gain
            return w + delta * jnp.eye(EMBED, dtype=w.dtype)

        def _layer_norm(x, g, b):
            mu = jnp.mean(x, axis=-1, keepdims=True)
            var = jnp.mean(jnp.square(x - mu), axis=-1, keepdims=True)
            return (x - mu) * jax.lax.rsqrt(var + LN_EPS) * g + b

        def _split_heads(x, B, S):
            return x.reshape(B, S, HEADS, HEAD_DIM).transpose(0, 2, 1, 3)
        B, S, _ = seq.shape
        q = _split_heads(seq @ wq.T, B, S)
        k = _split_heads(seq @ wk.T, B, S)
        v = _split_heads(seq @ wv.T, B, S)
        k = _layer_norm(k, ln_k_g, ln_k_b)
        v = _layer_norm(v, ln_v_g, ln_v_b)
        kv = jnp.einsum('bhsd,bhse->bhde', k, v) / S
        ga = jnp.einsum('bhsd,bhde->bhse', q, kv)
        ga = ga.transpose(0, 2, 1, 3).reshape(B, S, EMBED)
        return ga @ wo.T + bo

    def _L0_ffn_ref(x, W_fx, b_fx, W_x, b_x, W_slice, b_slice, W_q, W_k, W_v, W_out, b_out, temperature):
        import jax, jax.numpy as jnp
        import numpy as np
        DIM = 256
        H = 8
        D = 64
        G = 64
        INNER = H * D
        SCALE = D ** (-0.5)
        B, N, _ = x.shape
        fx_mid = (x @ W_fx + b_fx).reshape(B, N, H, D).transpose(0, 2, 1, 3)
        x_mid = (x @ W_x + b_x).reshape(B, N, H, D).transpose(0, 2, 1, 3)
        temp = jnp.clip(temperature, 0.1, 5.0)
        slice_weights = jax.nn.softmax((x_mid @ W_slice + b_slice) / temp, axis=-1)
        slice_norm = slice_weights.sum(axis=2)
        slice_token = jnp.einsum('bhnc,bhng->bhgc', fx_mid, slice_weights)
        slice_token = slice_token / (slice_norm[..., None] + 1e-05)
        q = slice_token @ W_q
        k = slice_token @ W_k
        v = slice_token @ W_v
        attn = jax.nn.softmax(jnp.einsum('bhgc,bhkc->bhgk', q, k) * SCALE, axis=-1)
        out_slice = jnp.einsum('bhgk,bhkc->bhgc', attn, v)
        out_x = jnp.einsum('bhgc,bhng->bhnc', out_slice, slice_weights)
        out_x = out_x.transpose(0, 2, 1, 3).reshape(B, N, INNER)
        return out_x @ W_out + b_out
    edge_index = jnp.stack([src, dst])
    xn = _layernorm(x, axis=-1)
    x = x + _L0_gnn_ref(xn, edge_index, L0_gnn_W1, L0_gnn_b1, L0_gnn_W2, L0_gnn_b2) + _L0_mix_ref(xn[None], L0_mix_wq, L0_mix_wk, L0_mix_wv, L0_mix_wo, L0_mix_bo, L0_mix_ln_k_g, L0_mix_ln_k_b, L0_mix_ln_v_g, L0_mix_ln_v_b)[0]
    x = x + _L0_ffn_ref(_layernorm(x, axis=-1)[None], L0_ffn_W_fx, L0_ffn_b_fx, L0_ffn_W_x, L0_ffn_b_x, L0_ffn_W_slice, L0_ffn_b_slice, L0_ffn_W_q, L0_ffn_W_k, L0_ffn_W_v, L0_ffn_W_out, L0_ffn_b_out, L0_ffn_temperature)[0]
    return x

_drawn_inputs = setup_inputs


def setup_inputs(seed=0):
    import zlib

    import numpy as np

    out = dict(_drawn_inputs(seed))
    spreads = {'L0_gnn_b1': (0.0, 0.1),
     'L0_gnn_b2': (0.0, 0.1),
     'L0_mix_ln_k_g': (1.0, 0.6),
     'L0_mix_ln_k_b': (0.0, 0.8),
     'L0_mix_ln_v_g': (1.0, 0.6),
     'L0_mix_ln_v_b': (0.0, 0.8),
     'L0_ffn_b_fx': (0.0, 0.1),
     'L0_ffn_b_x': (0.0, 0.8),
     'L0_ffn_b_slice': (0.0, 0.8),
     'L0_ffn_b_out': (0.0, 0.1),
     'L0_ffn_temperature': (0.5, 0.6)}
    factors = {'L0_mix_wq': 8.0,
     'L0_mix_wk': 8.0,
     'L0_mix_wv': 8.0,
     'L0_mix_wo': 8.0,
     'L0_ffn_W_x': 8.0,
     'L0_ffn_W_slice': 8.0,
     'L0_ffn_W_q': 8.0,
     'L0_ffn_W_k': 8.0}
    for name, (base, spread) in spreads.items():
        noise = np.random.default_rng([zlib.crc32(name.encode()), seed]).standard_normal(out[name].shape)
        drawn = base * np.exp(spread * noise) if base else spread * noise
        out[name] = jnp.asarray(drawn.astype(out[name].dtype))
    for name, factor in factors.items():
        out[name] = (out[name] * factor).astype(out[name].dtype)
    return out
```

```python
import concourse.bass as bass
from concourse import mybir
from contextlib import ExitStack

F32 = mybir.dt.float32
F16 = mybir.dt.float16
I32 = mybir.dt.int32
ALU = mybir.AluOpType
ACT = mybir.ActivationFunctionType
AX = mybir.AxisListType

N = 3125
E = 50000
D = 256
HID = 128
BL = 125
NB = N // BL
U = 5
IT = NB // U
KC = D // 128
W = 5
NW = N // W
WB = BL // W
NQ = NW // BL
SLOTS = 128
HEADS, HD = 4, 64
FH, G = 8, 64
INNER = FH * G
BANK = 512
EPS = 1e-5
ROUND = 12582912.0
LIMIT = 16384.0
CH = [4, 4, 4, 4, 3, 3, 3]
CBANK = [0, 1, 2, 0, 1, 2, 1]
GE = 416 * 128
GC = GE // 128


TWO = [0, 1, 0, 1, 0]
THREE = [0, 1, 2, 0, 1]


def at(i):
    return i + 1 + U


def semaphore(nc, s, name):
    s.phase_semaphores.append(nc.alloc_semaphore(name=name))
    return s.phase_semaphores[-1]


def hold(eng, held, *waits):
    for sem, value in waits:
        eng.wait_ge(sem, value)
    eng.sem_inc(held, 1)


def start_at(eng, sems, n=U):
    for x in sems:
        eng.sem_inc(x, n)


def pipelined(eng, *steps):
    assert max(lag for lag, _ in steps) < U
    for t in range(U):
        for lag, f in steps:
            if t >= lag:
                f(t - lag, (t - lag) % U, (t - lag) // U)
    with eng.Fori(1, IT) as it:
        for u in range(U):
            for lag, f in steps:
                f(it * U + (u - lag), (u - lag) % U, it + (u - lag) // U)
    for t in range(NB, NB + max(lag for lag, _ in steps)):
        for lag, f in steps:
            if t - lag < NB:
                f(t - lag, (t - lag) % U, (t - lag) // U)


def before(slots, u):
    n = len(slots)
    d = 1
    while slots[(u - d) % n] != slots[u]:
        d += 1
    return d


def bc(ap, n):
    return ap.unsqueeze(2).to_broadcast([ap.shape[0], ap.shape[1], n])


def blk(ap, i):
    return ap[:, bass.ds(i, 1), :].rearrange("p a c -> p (a c)")


def rows(dram, i):
    return dram.rearrange("(b p) c -> b p c", p=BL)[bass.ds(i, 1)].rearrange("a p c -> (a p) c")


class Store:
    pass


def build(nc, t, out):
    with ExitStack() as ctx:
        s = Store()
        s.t, s.out = t, out

        def sb(name, shape, dt=F32):
            return ctx.enter_context(nc.sbuf_tensor(name, shape, dt))

        def dram(name, shape, dt=F32):
            return nc.dram_tensor(name, shape, dt, kind="Internal").ap()

        s.xnT_d = dram("xnT_spill", (NB * 128, KC * BL))
        s.x1_d = dram("x1_spill", (N, D))
        s.table_d = dram("table_spill", (N, HID))
        s.adj = sb("adj", [128, NB * N + 1], F16)
        s.h1 = sb("h1_parts", [BL, NB, 2 * HID], F16)
        s.h2 = sb("h2_parts", [BL, NB, 2 * HID], F16)
        s.dinvB = sb("dinv_rows", [128, N])
        s.dinvN = sb("dinv_cols", [BL, NB])
        s.keyT = sb("keyT", [128, NW])
        s.loT = sb("loT", [128, NW])
        s.flag = sb("covered", [128, 1], I32)
        s.ident = sb("ident", [128, 128])
        s.ones = sb("ones", [128, 128])
        s.half = sb("minus_half", [128, 1])
        s.plus = sb("plus_half", [128, 1])
        s.ident16 = sb("ident16", [128, 128], F16)
        s.iota16 = sb("iota16", [128, BL], F16)
        s.W2 = sb("W2", [128, D])
        s.sb1 = sb("scaled_b1", [BL, HID])
        s.inv_s = sb("inv_scale", [128, 1])
        s.Wc = sb("W_logits", [128, KC, INNER])
        s.biasC = sb("bias_logits", [BL, INNER])
        s.PS = ctx.enter_context(nc.psum_tensor("PS", [128, 8 * BANK], F32))
        s.held = ctx.enter_context(nc.semaphore("held"))
        s.arena = s.adj[:, :].bitcast(F32)
        s.used = 0

        for phase in (constants, weights, windows, attention_stats, attention_out,
                      build_and_convolve, convolve_again, general, slices, tokens, output):
            s.phase_semaphores = []
            phase(nc, s)
            nc.clear_and_free_semaphores(s.phase_semaphores)
            nc.all_engine_barrier(sem_only=True)


def take(s, p, shape, dt=F32):
    n = 1
    for a in shape:
        n *= a
    words = n if dt != F16 else (n + 1) // 2
    v = s.arena[0:p, s.used:s.used + words]
    s.used += words
    assert s.used <= (NB * N + 1) // 2
    if dt != F32:
        v = v.bitcast(dt)[:, 0:n]
    if len(shape) == 2:
        v = v.rearrange("p (a b) -> p a b", b=shape[1])
    if len(shape) == 3:
        v = v.rearrange("p (a b c) -> p a b c", b=shape[1], c=shape[2])
    return v


def bank(s, b, p=128, a=0, n=BANK):
    return s.PS[0:p, b * BANK + a:b * BANK + a + n]


def constants(nc, s):
    with ExitStack() as ctx:
        made = semaphore(nc, s, "const_made")
        row_i = ctx.enter_context(nc.sbuf_tensor("row_i", [128, BL], I32))
        block = ctx.enter_context(nc.Block())

        @block.gpsimd
        def _(pool):
            pool.memset(s.ident[:, :], 0.0).then_inc(made, 1)
            pool.memset(s.ones[:, :], 1.0).then_inc(made, 1)
            pool.memset(s.half[:, :], -0.5).then_inc(made, 1)
            pool.memset(s.plus[:, :], 0.5).then_inc(made, 1)
            pool.iota(row_i[:, :], pattern=[[1, BL]], base=0, channel_multiplier=0).then_inc(made, 1)
            pool.wait_ge(made, 5)
            pool.affine_select(out=s.ident[:, :], in_=s.ident[:, :], compare_op=ALU.not_equal, fill=1.0, base=0,
                               pattern=[[-1, 128]], channel_multiplier=1).then_inc(made, 1)
            pool.tensor_copy(s.iota16[:, :], row_i[:, :]).then_inc(made, 1)
            pool.wait_ge(made, 7)
            pool.tensor_copy(s.ident16[:, :], s.ident[:, :]).then_inc(made, 1)
            pool.wait_ge(made, 8)


def weights(nc, s):
    t = s.t
    with ExitStack() as ctx:
        def sem(name):
            return semaphore(nc, s, "wt_" + name)

        s.used = 0
        s.Wkv = take(s, 128, [KC, 2 * D])
        s.W1 = take(s, 128, [KC, HID])
        s.X = take(s, HD + 1, [HEADS * D])
        s.Y = take(s, HD + 1, [HEADS * D])
        s.bsum = take(s, BL, [D])
        s.arena_keep = s.used
        sq = take(s, 128, [KC, HID])
        b1B = take(s, 128, [HID])
        B = take(s, 128, [HID])
        sc = take(s, 128, [HID])
        mean = take(s, 128, [KC, 2 * HEADS])
        wq = take(s, HD, [HEADS, D])
        woT = take(s, HD, [HEADS, D])
        ln = take(s, HD, [4])
        GkT = take(s, HD, [HD + 1])
        GvT = take(s, HD, [HD + 1])
        b2B = take(s, BL, [D])
        WxT = take(s, G, [FH, D])
        Wsl = take(s, G, [G])
        bx = take(s, G, [FH])
        bxB = take(s, G, [FH, 128])
        bslB = take(s, BL, [G])
        temp = take(s, 128, [FH])
        rtemp = take(s, 128, [FH])
        tmpb = take(s, BL, [INNER])
        absb = take(s, 128, [HID])

        loads = [
            ("kv", s.Wkv, t["wkvT"].rearrange("(k p) n -> p k n", p=128)),
            ("W1", s.W1, t["W1"].rearrange("(k p) n -> p k n", p=128)),
            ("b1", b1B, t["b1"].partition_broadcast(128)),
            ("wq", wq, t["wq"].rearrange("(h d) n -> d h n", d=HD)),
            ("wo", woT, t["woT"].rearrange("(h d) n -> d h n", d=HD)),
            ("ln", ln, t["ln"]),
            ("b2", b2B, t["b2"].partition_broadcast(BL)),
            ("bo", s.bsum, t["bo"].partition_broadcast(BL)),
            ("WxT", WxT, t["WxT"].rearrange("(h c) n -> c h n", c=G)),
            ("Wsl", Wsl, t["W_slice"]),
            ("bx", bx, t["bxT"]),
            ("bsl", bslB, t["b_slice"].partition_broadcast(BL)),
            ("temp", temp, t["temp"].partition_broadcast(128)),
            ("W2", s.W2[:, :], t["W2"]),
        ]
        got = {name: sem("in_" + name) for name, _, _ in loads}
        step = sem("dve_step")
        normed, scaled, gains, wx_ready, sc_ready = sem("w1_sq"), sem("w1_sum"), sem("gains"), sem("wx"), sem("sc")
        pooled, folded, columns, logits, biases = sem("pow"), sem("xy"), sem("col"), sem("wc"), sem("bcm")
        summed, kept = sem("sum"), sem("kept")
        block = ctx.enter_context(nc.Block())

        @block.sync
        def _(sp):
            for name, dst, src in loads:
                sp.dma_start(dst, src).then_inc(got[name], 16)
            sp.wait_ge(got["W2"], 16)

        @block.vector
        def _(dve):
            chain = [0]

            def link(ins):
                chain[0] += 1
                ins.then_inc(step, 1)
                dve.wait_ge(step, chain[0])

            dve.wait_ge(got["W1"], 16)
            dve.tensor_tensor(sq, s.W1, s.W1, ALU.mult).then_inc(normed, 1)
            dve.wait_ge(got["kv"], 16)
            kv3 = s.Wkv.rearrange("p k (h d) -> p (k h) d", d=HD)
            m3 = mean.rearrange("p k h -> p (k h)")
            link(dve.tensor_reduce(m3, kv3, AX.X, ALU.add))
            link(dve.tensor_scalar(m3, m3, -1.0 / HD, None, ALU.mult))
            link(dve.tensor_tensor(kv3, kv3, bc(m3, HD), ALU.add))
            dve.wait_ge(got["ln"], 16)
            for m, a in ((GkT, 0), (GvT, 2)):
                dve.tensor_scalar(m[:, 0:HD], s.ident[0:HD, 0:HD], ln[:, a:a + 1], None, ALU.mult).then_inc(gains, 1)
                dve.tensor_copy(m[:, HD:HD + 1], ln[:, a + 1:a + 2]).then_inc(gains, 1)
            dve.wait_ge(got["bx"], 16)
            dve.tensor_copy(bxB, bc(bx, 128)).then_inc(gains, 1)
            dve.wait_ge(got["temp"], 16)
            link(dve.tensor_scalar(temp, temp, 0.1, 5.0, ALU.max, ALU.min))
            link(dve.reciprocal(rtemp, temp))
            dve.wait_ge(got["b2"], 16)
            dve.wait_ge(got["bo"], 16)
            dve.tensor_tensor(s.bsum, s.bsum, b2B, ALU.add).then_inc(summed, 1)
            dve.wait_ge(got["b1"], 16)
            dve.wait_ge(pooled, 1)
            link(dve.tensor_scalar(absb, b1B, -1.0, None, ALU.mult))
            link(dve.tensor_tensor(absb, absb, b1B, ALU.max))
            link(dve.scalar_tensor_tensor(B, B, 16.0, absb, ALU.mult, ALU.add))
            link(dve.tensor_scalar(B, B, 1e-20, 1.0 / LIMIT, ALU.max, ALU.mult))
            link(dve.reciprocal(sc, B))
            dve.tensor_copy(absb, sc).then_inc(sc_ready, 1)
            dve.tensor_tensor(s.sb1[:, :], b1B[0:BL, :], sc[0:BL, :], ALU.mult).then_inc(kept, 1)
            for k in range(KC):
                dve.tensor_tensor(s.W1[:, k, :], s.W1[:, k, :], sc, ALU.mult).then_inc(kept, 1)
            dve.wait_ge(folded, 2)
            for dst, b in ((s.X, 0), (s.Y, 2)):
                dve.tensor_copy(dst, s.PS[0:HD + 1, b * BANK:(b + 2) * BANK]).then_inc(kept, 1)
            dve.wait_ge(logits, 1)
            for k in range(KC):
                dve.tensor_tensor(s.Wc[:, k, :].rearrange("p (h g) -> p h g", g=G),
                                  bank(s, 4 + k).rearrange("p (h g) -> p h g", g=G), bc(rtemp, G),
                                  ALU.mult).then_inc(kept, 1)
            dve.wait_ge(biases, 1)
            dve.wait_ge(got["bsl"], 16)
            tb = tmpb.rearrange("p (h g) -> p h g", g=G)
            link(dve.tensor_tensor(tb, bank(s, 6, BL).rearrange("p (h g) -> p h g", g=G),
                                   bslB.unsqueeze(1).to_broadcast([BL, FH, G]), ALU.add))
            dve.tensor_tensor(s.biasC[:, :].rearrange("p (h g) -> p h g", g=G), tb, bc(rtemp[0:BL, :], G),
                              ALU.mult).then_inc(kept, 1)
            dve.wait_ge(columns, 1)
            dve.tensor_scalar(s.inv_s[:, :], bank(s, 7, 128, 256, 1), 1.0, None, ALU.mult).then_inc(kept, 1)
            dve.wait_ge(kept, 9)
            dve.wait_ge(summed, 1)

        @block.gpsimd
        def _(pool):
            pool.wait_ge(scaled, 2)
            pool.tensor_tensor(B, B, s.plus[:, 0:1].to_broadcast([128, HID]), ALU.pow).then_inc(pooled, 1)

        @block.scalar
        def _(act):
            act.wait_ge(scaled, 1)
            act.activation(B, bank(s, 7, 128, 0, HID), ACT.Copy).then_inc(scaled, 1)

        @block.tensor
        def _(pe):
            pe.wait_ge(normed, 1)
            for k in range(KC):
                mm = pe.matmul(bank(s, 7, 128, 0, HID), s.ones[:, :], sq[:, k, :], start=(k == 0), stop=(k == KC - 1))
            mm.then_inc(scaled, 1)
            pe.wait_ge(gains, 5)
            pe.wait_ge(got["wq"], 16)
            pe.wait_ge(got["wo"], 16)
            for m, src, b in ((GkT, wq, 0), (GvT, woT, 2)):
                flat = src.rearrange("p h n -> p (h n)")
                for c in range(2):
                    mm = pe.matmul(bank(s, b + c, HD + 1), m, flat[:, c * BANK:(c + 1) * BANK], start=True, stop=True)
                mm.then_inc(folded, 1)
            pe.wait_ge(got["WxT"], 16)
            pe.wait_ge(got["Wsl"], 16)
            for k in range(KC):
                for h in range(FH):
                    mm = pe.matmul(bank(s, 4 + k, 128, h * G, G), WxT[:, h, k * 128:(k + 1) * 128], Wsl,
                                   start=True, stop=True)
            mm.then_inc(logits, 1)
            for h in range(FH):
                mm = pe.matmul(bank(s, 6, BL, h * G, G), bxB[:, h, 0:BL], Wsl, start=True, stop=True)
            mm.then_inc(biases, 1)
            pe.wait_ge(sc_ready, 1)
            pe.matmul(bank(s, 7, 128, 256, 1), B[0:1, :], s.ones[0:1, 0:1], start=True, stop=True).then_inc(columns, 1)


def windows(nc, s):
    t = s.t
    with ExitStack() as ctx:
        def sem(name):
            return semaphore(nc, s, "wi_" + name)

        s.used = s.arena_keep
        FC = E // BL
        first_i = take(s, BL, [FC], I32)
        first = take(s, BL, [FC])
        t5_i = take(s, BL, [NQ], I32)
        t5 = take(s, BL, [NQ])
        junk = take(s, BL, [FC])
        n1 = take(s, BL, [NQ])
        rowf = take(s, BL, [NQ])
        row_i = take(s, BL, [NQ], I32)
        R = take(s, BL, [NQ, BL], I32)
        n2 = take(s, BL, [NQ])
        at = take(s, BL, [NQ])
        at_i = take(s, BL, [NQ], I32)
        EW = take(s, BL, [NQ, SLOTS * 2], I32)
        C = NQ * SLOTS
        src = take(s, BL, [C])
        loc = take(s, BL, [C])
        hi = take(s, BL, [C])
        lo = take(s, BL, [C])
        valid = take(s, BL, [C])
        locm = take(s, BL, [C])
        keym = take(s, BL, [C])
        vsum = take(s, BL, [1])
        locT = take(s, 128, [NW])
        L = take(s, 128, [NW, W], F16)
        iota5 = s.iota16[:, 0:W]
        ones16 = take(s, 128, [128], F16)
        step, thr, in_f, rows_at, rows_in = sem("dve"), sem("thr"), sem("first"), sem("rowat"), [sem(f"r{q}") for q in range(NQ)]
        edges_at, edges_in, masked, turned = sem("edgeat"), [sem(f"e{q}") for q in range(NQ)], sem("mask"), sem("turn")
        hot, deg_mm, deg_sb, deg_pow, cols, counted, ones_r = sem("hot"), sem("degmm"), sem("degsb"), sem("degpow"), sem("cols"), sem("cnt"), sem("ones")
        diag = take(s, BL, [NB, BL])
        diag_r, flag_mm, kept = sem("diag"), sem("flag"), sem("kept")
        block = ctx.enter_context(nc.Block())
        NC7 = [(c * 500, min(500, N - c * 500)) for c in range(7)]

        @block.sync
        def _(sp):
            sp.dma_start(first_i, t["firsts"].partition_broadcast(BL)).then_inc(in_f, 16)

        @block.gpsimd
        def _(pool):
            pool.iota(t5_i, pattern=[[W * BL, NQ]], base=0, channel_multiplier=W).then_inc(thr, 1)
            pool.memset(ones16, 1.0).then_inc(ones_r, 1)
            pool.wait_ge(rows_at, 1)
            for q in range(NQ):
                pool.indirect_dma_start(out=R[:, q, :], out_offset=None, in_=t["dst"].rearrange("(a b) -> a b", b=BL),
                                        in_offset=bass.IndirectOffsetOnAxis(ap=row_i[:, q:q + 1], axis=0)
                                        ).then_inc(rows_in[q], 16)
            pool.wait_ge(edges_at, 1)
            for q in range(NQ):
                pool.indirect_dma_start(out=EW[:, q, :], out_offset=None, in_=t["edges"].rearrange("(a b) -> a b", a=1),
                                        in_offset=bass.IndirectOffsetOnAxis(ap=at_i[:, q:q + 1], axis=1)
                                        ).then_inc(edges_in[q], 16)
            pool.wait_ge(deg_sb, 1)
            pool.tensor_tensor(s.dinvN[:, :], s.dinvN[:, :], s.half[0:BL, 0:1].to_broadcast([BL, NB]),
                               ALU.pow).then_inc(deg_pow, 1)

        @block.vector
        def _(dve):
            chain = [0]

            def link(ins):
                chain[0] += 1
                ins.then_inc(step, 1)
                dve.wait_ge(step, chain[0])

            dve.wait_ge(thr, 1)
            link(dve.tensor_copy(t5, t5_i))
            dve.wait_ge(in_f, 16)
            link(dve.tensor_copy(first, first_i))
            for q in range(NQ):
                link(dve.tensor_scalar(junk, first, t5[:, q:q + 1], 0.0, ALU.is_lt, ALU.add, accum_out=n1[:, q:q + 1]))
            link(dve.tensor_scalar(rowf, n1, 1.0, 0.0, ALU.subtract, ALU.max))
            dve.tensor_copy(row_i, rowf).then_inc(rows_at, 1)
            for q in range(NQ):
                dve.wait_ge(rows_in[q], 16)
                link(dve.tensor_scalar(junk[:, 0:BL], R[:, q, :], t5[:, q:q + 1], 0.0, ALU.is_lt, ALU.add,
                                       accum_out=n2[:, q:q + 1]))
            link(dve.scalar_tensor_tensor(at, rowf, float(BL), n2, ALU.mult, ALU.add))
            dve.tensor_scalar(at_i, at, float(E - SLOTS), 2.0, ALU.min, ALU.mult).then_inc(edges_at, 1)
            for q in range(NQ):
                dve.wait_ge(edges_in[q], 16)
                pair = EW[:, q, :].rearrange("p (e k) -> p e k", k=2)
                dve.tensor_copy(src[:, q * SLOTS:(q + 1) * SLOTS], pair[:, :, 0])
                link(dve.tensor_scalar(loc[:, q * SLOTS:(q + 1) * SLOTS], pair[:, :, 1], t5[:, q:q + 1], None,
                                       ALU.subtract))
            link(dve.tensor_scalar(hi, loc, 0.0, None, ALU.is_ge))
            link(dve.scalar_tensor_tensor(valid, loc, float(W), hi, ALU.is_lt, ALU.mult))
            dve.tensor_reduce(vsum, valid, AX.X, ALU.add).then_inc(counted, 1)
            link(dve.tensor_scalar(hi, src, 0.5, 1.0 / BL, ALU.add, ALU.mult))
            link(dve.tensor_scalar(hi, hi, 0.5, ROUND, ALU.subtract, ALU.add))
            link(dve.tensor_scalar(hi, hi, ROUND, None, ALU.subtract))
            dve.scalar_tensor_tensor(lo, hi, -float(BL), src, ALU.mult, ALU.add).then_inc(masked, 1)
            link(dve.scalar_tensor_tensor(keym, hi, float(W), loc, ALU.mult, ALU.add))
            link(dve.scalar_tensor_tensor(keym, keym, 1.0, valid, ALU.add, ALU.mult))
            dve.tensor_scalar(keym, keym, 1.0, None, ALU.subtract).then_inc(masked, 1)
            link(dve.scalar_tensor_tensor(locm, loc, 1.0, valid, ALU.add, ALU.mult))
            dve.tensor_scalar(locm, locm, 1.0, None, ALU.subtract).then_inc(masked, 1)
            for i, (m, b) in enumerate(((s.loT[:, :], 0), (s.keyT[:, :], 2), (locT, 4))):
                dve.wait_ge(turned, i + 1)
                dve.tensor_copy(m[:, 0:500], bank(s, b, 128, 0, 500))
                link(dve.tensor_copy(m[:, 500:NW], bank(s, b + 1, 128, 0, 125)))
            link(dve.tensor_tensor(L, bc(locT, W), iota5.unsqueeze(1).to_broadcast([128, NW, W]), ALU.is_equal))
            dve.wait_ge(flag_mm, 1)
            link(dve.tensor_copy(s.flag[:, :], bank(s, 7, 128, 0, 1)))
            dve.sem_inc(hot, 1)
            dve.wait_ge(deg_mm, 1)
            dve.tensor_scalar(s.dinvN[:, :], bank(s, 7, BL, 8, NB), 1.0, None, ALU.add).then_inc(deg_sb, 1)
            dve.wait_ge(deg_pow, 1)
            dve.tensor_tensor(diag, bc(s.dinvN[:, :], BL), s.ident[0:BL, 0:BL].unsqueeze(1).to_broadcast([BL, NB, BL]),
                              ALU.mult).then_inc(diag_r, 1)
            for c, (a, n) in enumerate(NC7):
                dve.wait_ge(cols, c + 1)
                dve.tensor_copy(s.dinvB[:, a:a + n], bank(s, c, 128, 0, n)).then_inc(kept, 1)
            dve.wait_ge(kept, 7)

        @block.tensor
        def _(pe):
            for i, (m, b) in enumerate(((lo, 0), (keym, 2), (locm, 4))):
                pe.wait_ge(masked, i + 1)
                for q in range(NQ):
                    mm = pe.transpose(bank(s, b + (q == 4), 128, (q % 4) * BL, BL), m[:, q * SLOTS:(q + 1) * SLOTS],
                                      s.ident[0:BL, 0:BL])
                mm.then_inc(turned, 1)
            pe.wait_ge(counted, 1)
            pe.matmul(bank(s, 7, 128, 0, 1), s.ones[0:BL, :], vsum, start=True, stop=True).then_inc(flag_mm, 1)
            pe.wait_ge(hot, 1)
            pe.wait_ge(ones_r, 1)
            flat = L.rearrange("p k j -> p (k j)")
            for b in range(NB):
                mm = pe.matmul(bank(s, 7, BL, 8 + b, 1), flat[:, b * BL:(b + 1) * BL], ones16[:, 0:1], start=True,
                               stop=True)
            mm.then_inc(deg_mm, 1)
            pe.wait_ge(diag_r, 1)
            for c, (a, n) in enumerate(NC7):
                pe.matmul(bank(s, c, 128, 0, n), s.ones[0:BL, :], diag.rearrange("p b d -> p (b d)")[:, a:a + n],
                          start=True, stop=True).then_inc(cols, 1)


def attention_stats(nc, s):
    t = s.t
    with ExitStack() as ctx:
        def sem(name):
            return semaphore(nc, s, "st_" + name)

        s.used = s.arena_keep
        A1 = HD + 1
        xin = take(s, BL, [U, D])
        xn = take(s, BL, [U, D])
        xnT = take(s, 128, [U, KC * BL])
        st = take(s, BL, [U, 6])
        mv = take(s, BL, [U, 2])
        ve = take(s, BL, [U])
        rstd = take(s, BL, [U])
        sq = take(s, BL, [2, INNER])
        ss = take(s, BL, [U, 2 * HEADS])
        se = take(s, BL, [U, 2 * HEADS])
        rs = take(s, BL, [U, 2 * HEADS])
        kv = take(s, BL, [U * 2 * HEADS, A1])
        TP, KV, HB, AC = [0, 1], [2, 3, 7], [4, 5], 6
        loaded, spilled = [sem(f"x{u}") for u in range(U)], [sem(f"sp{u}") for u in range(U)]
        stats, aggr, ve_r, rstd_r, xn_r = sem("stats"), sem("aggr"), sem("ve"), sem("rstd"), sem("xn")
        tp_r, xnT_r, mm_r, h_hi, h_out = sem("tp"), sem("xnT"), sem("mm"), sem("hhi"), sem("hout")
        sq_r, ss_r, se_r, rs_r, kv_r, acc_r, ready = (sem(x) for x in ("sq", "ss", "se", "rs", "kv", "acc", "rdy"))
        block = ctx.enter_context(nc.Block())

        @block.sync
        def _(sp):
            start_at(sp, [xn_r])

            def load(i, u, r):
                sp.wait_ge(xn_r, at(i) - U)
                sp.dma_start(xin[:, u, :], rows(t["x"], i)).then_inc(loaded[u], 16)

            def spill(i, u, r):
                sp.wait_ge(xnT_r, at(i))
                sp.dma_start(s.xnT_d.rearrange("(b p) c -> b p c", p=128)[bass.ds(i, 1)]
                             .rearrange("a p c -> (a p) c"), xnT[:, u, :]).then_inc(spilled[u], 16)

            pipelined(sp, (0, load), (4, spill))
            for u in range(U):
                sp.wait_ge(spilled[u], 16 * IT + 16)

        @block.vector
        def _(dve):
            start_at(dve, [stats, aggr, ss_r, kv_r, h_out])
            dve.memset(kv, 1.0).then_inc(ready, 1)
            dve.wait_ge(ready, 1)

            def statistics(i, u, r):
                dve.wait_ge(loaded[u], r * 16 + 16)
                dve.bn_stats(st[:, u, :], xin[:, u, :]).then_inc(stats, 1)

            def aggregate(i, u, r):
                hold(dve, s.held, (stats, at(i)), (xn_r, at(i) - U))
                dve.bn_aggr(mv[:, u, :], st[:, u, :]).then_inc(aggr, 1)

            def square_sums(i, u, r):
                dve.wait_ge(sq_r, at(i))
                dve.wait_ge(se_r, at(i) - U)
                dve.tensor_reduce(ss[:, u, :], sq[:, TWO[u], :].rearrange("p (h d) -> p h d", d=HD), AX.X,
                                  ALU.add).then_inc(ss_r, 1)

            def low_part(i, u, r):
                dve.wait_ge(h_hi, at(i))
                dve.scalar_tensor_tensor(blk(s.h1[:, :, HID:2 * HID], i), bank(s, HB[TWO[u]], BL, 0, HID),
                                         s.dinvN[:, bass.ds(i, 1)], blk(s.h1[:, :, 0:HID], i),
                                         ALU.mult, ALU.subtract).then_inc(h_out, 1)

            def normalise(i, u, r):
                dve.wait_ge(rs_r, at(i))
                dve.wait_ge(acc_r, at(i) - U)
                dve.tensor_tensor(kv[:, u * 2 * HEADS:(u + 1) * 2 * HEADS, 0:HD],
                                  bank(s, KV[THREE[u]], BL).rearrange("p (h d) -> p h d", d=HD),
                                  bc(rs[:, u, :], HD), ALU.mult).then_inc(kv_r, 1)

            pipelined(dve, (4, normalise), (0, statistics), (0, aggregate), (3, square_sums), (3, low_part))

        @block.gpsimd
        def _(pool):
            start_at(pool, [ve_r, rstd_r, se_r, rs_r])

            def norm(i, u, r):
                hold(pool, s.held, (aggr, at(i)))
                pool.tensor_scalar(ve[:, u:u + 1], mv[:, u, 1:2], EPS, None, ALU.add).then_inc(ve_r, 1)
                pool.wait_ge(ve_r, at(i))
                pool.tensor_tensor(rstd[:, u:u + 1], ve[:, u:u + 1], s.half[0:BL, 0:1], ALU.pow).then_inc(rstd_r, 1)
                hold(pool, s.held, (rstd_r, at(i)), (tp_r, at(i) - U))
                pool.tensor_scalar(xn[:, u, :], xin[:, u, :], mv[:, u, 0:1], rstd[:, u:u + 1], ALU.subtract,
                                   ALU.mult).then_inc(xn_r, 1)

            def head_norm(i, u, r):
                hold(pool, s.held, (ss_r, at(i)))
                pool.tensor_scalar(se[:, u, :], ss[:, u, :], 1.0 / HD, EPS, ALU.mult, ALU.add).then_inc(se_r, 1)
                pool.wait_ge(se_r, at(i))
                pool.wait_ge(kv_r, at(i) - U)
                pool.tensor_tensor(rs[:, u, :], se[:, u, :], s.half[0:BL, 0:1].to_broadcast([BL, 2 * HEADS]),
                                   ALU.pow).then_inc(rs_r, 1)

            pipelined(pool, (0, norm), (3, head_norm))

        @block.scalar
        def _(act):
            start_at(act, [xnT_r, sq_r, h_hi])
            start_at(act, spilled, 16)

            def turned(i, u, r):
                act.wait_ge(tp_r, at(i))
                act.wait_ge(mm_r, at(i) - U)
                act.wait_ge(spilled[u], r * 16 + 16)
                act.activation(xnT[:, u, :], bank(s, TP[TWO[u]], 128, 0, KC * BL), ACT.Copy).then_inc(xnT_r, 1)

            def squares(i, u, r):
                act.wait_ge(mm_r, at(i))
                act.wait_ge(ss_r, at(i) - before(TWO, u))
                act.activation(sq[:, TWO[u], :], bank(s, KV[THREE[u]], BL), ACT.Square).then_inc(sq_r, 1)
                act.activation(blk(s.h1[:, :, 0:HID], i), bank(s, HB[TWO[u]], BL, 0, HID), ACT.Copy,
                               scale=s.dinvN[:, bass.ds(i, 1)]).then_inc(h_hi, 1)

            pipelined(act, (0, turned), (1, squares))

        @block.tensor
        def _(pe):
            start_at(pe, [tp_r, mm_r, acc_r])
            acc = bank(s, AC, A1, 0, HEADS * A1)

            def turn(i, u, r):
                pe.wait_ge(xn_r, at(i))
                pe.wait_ge(xnT_r, at(i) - before(TWO, u))
                for k in range(KC):
                    mm = pe.transpose(bank(s, TP[TWO[u]], 128, k * BL, BL), xn[:, u, k * 128:(k + 1) * 128],
                                      s.ident[0:BL, 0:BL])
                mm.then_inc(tp_r, 1)

            def project(i, u, r):
                pe.wait_ge(xnT_r, at(i))
                pe.wait_ge(kv_r, at(i) - before(THREE, u))
                for k in range(KC):
                    pe.matmul(bank(s, KV[THREE[u]], BL), xnT[:, u, k * BL:(k + 1) * BL], s.Wkv[:, k, :],
                              start=(k == 0), stop=(k == KC - 1))
                pe.wait_ge(h_out, at(i) - before(TWO, u))
                for k in range(KC):
                    mm = pe.matmul(bank(s, HB[TWO[u]], BL, 0, HID), xnT[:, u, k * BL:(k + 1) * BL], s.W1[:, k, :],
                                   start=(k == 0), stop=(k == KC - 1))
                mm.then_inc(mm_r, 1)

            def head_sums(i, u, r):
                pe.wait_ge(kv_r, at(i))
                for h in range(HEADS):
                    mm = pe.matmul(acc[:, h * A1:(h + 1) * A1], kv[:, u * 2 * HEADS + h, :],
                                   kv[:, u * 2 * HEADS + HEADS + h, :],
                                   start=isinstance(i, int) and i == 0 and h == 0,
                                   stop=isinstance(i, int) and i == NB - 1, skip_group_check=True)
                mm.then_inc(acc_r, 1)

            pipelined(pe, (0, turn), (1, project), (3, head_sums))


def attention_out(nc, s):
    t = s.t
    with ExitStack() as ctx:
        def sem(name):
            return semaphore(nc, s, "ao_" + name)

        s.used = s.arena_keep
        A1 = HD + 1
        K = take(s, A1, [HEADS * A1])
        KX = take(s, A1, [HEADS * D])
        M = take(s, 128, [KC, D])
        xnT = take(s, 128, [U, KC * BL])
        xin = take(s, BL, [U, D])
        x1 = take(s, BL, [U, D])
        MB = [4, 5]
        k_r, kx_mm, kx_r, m_mm, m_r = sem("k"), sem("kxmm"), sem("kx"), sem("mmm"), sem("m")
        in_t, in_x, sent = ([sem(f"{x}_{u}") for u in range(U)] for x in ("int", "inx", "sent"))
        xb_r, mix, x1_r = sem("xb"), sem("mix"), sem("x1")
        block = ctx.enter_context(nc.Block())

        @block.sync
        def _(sp):
            def load(i, u, r):
                sp.wait_ge(mix, at(i) - U)
                sp.dma_start(xnT[:, u, :], s.xnT_d.rearrange("(b p) c -> b p c", p=128)[bass.ds(i, 1)]
                             .rearrange("a p c -> (a p) c")).then_inc(in_t[u], 16)
                sp.wait_ge(x1_r, at(i) - U)
                sp.dma_start(xin[:, u, :], rows(t["x"], i)).then_inc(in_x[u], 16)

            pipelined(sp, (0, load))

        @block.gpsimd
        def _(pool):
            start_at(pool, [xb_r])

            def add_biases(i, u, r):
                pool.wait_ge(in_x[u], r * 16 + 16)
                pool.tensor_tensor(xin[:, u, :], xin[:, u, :], s.bsum, ALU.add).then_inc(xb_r, 1)

            pipelined(pool, (0, add_biases))

        @block.scalar
        def _(act):
            act.activation(K, bank(s, 6, A1, 0, HEADS * A1), ACT.Copy, scale=1.0 / N).then_inc(k_r, 1)
            act.wait_ge(kx_mm, 1)
            act.activation(KX, s.PS[0:A1, 0:2 * BANK], ACT.Copy).then_inc(kx_r, 1)
            act.wait_ge(m_mm, 1)
            act.activation(M.rearrange("p k n -> p (k n)"), bank(s, 2), ACT.Copy).then_inc(m_r, 1)

            def send(i, u, r):
                act.wait_ge(x1_r, at(i))
                act.dma_start(rows(s.x1_d, i), x1[:, u, :]).then_inc(sent[u], 16)

            pipelined(act, (0, send))
            for u in range(U):
                act.wait_ge(sent[u], 16 * IT + 16)

        @block.vector
        def _(dve):
            start_at(dve, [x1_r])
            start_at(dve, sent, 16)

            def add(i, u, r):
                dve.wait_ge(xb_r, at(i))
                dve.wait_ge(mix, at(i))
                dve.wait_ge(sent[u], r * 16 + 16)
                dve.tensor_tensor(x1[:, u, :], bank(s, MB[TWO[u]], BL, 0, D), xin[:, u, :], ALU.add).then_inc(x1_r, 1)

            pipelined(dve, (0, add))

        @block.tensor
        def _(pe):
            start_at(pe, [mix])
            pe.wait_ge(k_r, 1)
            for h in range(HEADS):
                mm = pe.matmul(s.PS[0:A1, h * D:(h + 1) * D], K[:, h * A1:(h + 1) * A1], s.X[:, h * D:(h + 1) * D],
                               start=True, stop=True)
            mm.then_inc(kx_mm, 1)
            pe.wait_ge(kx_r, 1)
            for k in range(KC):
                for h in range(HEADS):
                    mm = pe.matmul(bank(s, 2, 128, k * D, D), KX[:, h * D + k * 128:h * D + (k + 1) * 128],
                                   s.Y[:, h * D:(h + 1) * D], start=(h == 0), stop=(h == HEADS - 1))
            mm.then_inc(m_mm, 1)
            pe.wait_ge(m_r, 1)

            def mixed(i, u, r):
                pe.wait_ge(in_t[u], r * 16 + 16)
                pe.wait_ge(x1_r, at(i) - before(TWO, u))
                for k in range(KC):
                    mm = pe.matmul(bank(s, MB[TWO[u]], BL, 0, D), xnT[:, u, k * BL:(k + 1) * BL], M[:, k, :],
                                   start=(k == 0), stop=(k == KC - 1))
                mm.then_inc(mix, 1)

            pipelined(pe, (0, mixed))


def build_and_convolve(nc, s):
    with ExitStack() as ctx:
        def sem(name):
            return semaphore(nc, s, "bc_" + name)

        def sb(name, shape, dt=F32):
            return ctx.enter_context(nc.sbuf_tensor(name, shape, dt))

        R = 5
        hot_lo = sb("hot_lo", [128, R, BL], F16)
        hot_key = sb("hot_key", [128, R, BL], F16)
        low = sb("conv_low", [BL, HID])
        z = sb("conv_z", [BL, HID])
        hot, used, copied, conv, low_r = sem("hot"), sem("used"), sem("copied"), sem("conv"), sem("low")
        summed, biased, scaled, hi_r, lo_r = sem("summed"), sem("biased"), sem("scaled"), sem("hi"), sem("lo")
        NCH = len(CH)
        START = [sum(CH[:c]) for c in range(NCH)]
        CONV = 3
        block = ctx.enter_context(nc.Block())

        def turns(eng, turn):
            turn(0, True, False, False)
            turn(1, True, True, False)
            with eng.Fori(2, NB) as t:
                turn(t, True, True, True)
            turn(NB, False, True, True)
            turn(NB + 1, False, False, True)

        @block.vector
        def _(dve):
            covered = dve.value_load(s.flag[0:1, 0:1])
            with dve.If(covered == E):
                start_at(dve, [used], R)
                start_at(dve, [summed, lo_r], 1)

                def finish(j, part):
                    if part == 0:
                        dve.wait_ge(lo_r, j + 1)
                        dve.wait_ge(low_r, j + 1)
                        dve.tensor_tensor(z[:, :], bank(s, CONV, BL, 0, HID), low[:, :], ALU.add).then_inc(summed, 1)
                    if part == 1:
                        dve.wait_ge(summed, j + 2)
                        dve.scalar_tensor_tensor(z[:, :], z[:, :], s.dinvN[:, bass.ds(j, 1)], s.sb1[:, :], ALU.mult,
                                                 ALU.add).then_inc(biased, 1)
                    if part == 2:
                        dve.wait_ge(biased, j + 1)
                        dve.tensor_scalar(z[:, :], z[:, :], 0.0, s.dinvN[:, bass.ds(j, 1)], ALU.max,
                                          ALU.mult).then_inc(scaled, 1)
                    if part == 3:
                        dve.wait_ge(hi_r, j + 1)
                        dve.tensor_tensor(blk(s.h2[:, :, HID:2 * HID], j), z[:, :], blk(s.h2[:, :, 0:HID], j),
                                          ALU.subtract).then_inc(lo_r, 1)

                WHEN = {2: 0, 5: 1, 8: 2, 14: 3}

                def turn(t, build, convolve, fin):
                    for w in range(WB):
                        if build:
                            dve.wait_ge(used, t * WB + w + 1)
                            dve.tensor_scalar(hot_lo[:, w % R, :], s.iota16[:, :], s.loT[:, bass.ds(t * WB + w, 1)], None,
                                              ALU.is_equal)
                            dve.tensor_scalar(hot_key[:, w % R, :], s.iota16[:, :], s.keyT[:, bass.ds(t * WB + w, 1)],
                                              None, ALU.is_equal).then_inc(hot, 1)
                        if fin and w in WHEN:
                            finish(t - 2, WHEN[w])

                turns(dve, turn)
                dve.wait_ge(lo_r, NB + 1)
            dve.end_ifs()

        @block.scalar
        def _(act):
            covered = act.value_load(s.flag[0:1, 0:1])
            with act.If(covered == E):
                start_at(act, [copied], NCH)

                def turn(t, build, convolve, fin):
                    for c in range(NCH):
                        if fin and c == 0:
                            act.wait_ge(conv, t - 1)
                            act.wait_ge(summed, t - 1)
                            act.activation(low[:, :], bank(s, CONV, BL, HID, HID), ACT.Copy).then_inc(low_r, 1)
                        if build:
                            act.wait_ge(used, t * WB + START[c] + CH[c] + R)
                            src = bank(s, CBANK[c], BL, 0, CH[c] * BL).rearrange("p (n h w) -> p h n w", n=CH[c], w=W)
                            dst = s.adj[0:BL, bass.ds(t * N, N)].rearrange("p (h d) -> p h d", d=BL)
                            dst = dst[:, :, START[c] * W:(START[c] + CH[c]) * W].rearrange("p h (n w) -> p h n w", w=W)
                            act.activation(dst, src, ACT.Copy).then_inc(copied, 1)
                        if fin and c == 2:
                            act.wait_ge(scaled, t - 1)
                            act.activation(blk(s.h2[:, :, 0:HID], t - 2), z[:, :], ACT.Copy).then_inc(hi_r, 1)

                turns(act, turn)
                act.wait_ge(hi_r, NB)
            act.end_ifs()

        @block.tensor
        def _(pe):
            covered = pe.value_load(s.flag[0:1, 0:1])
            with pe.If(covered == E):
                dst = bank(s, CONV, BL, 0, 2 * HID)

                def turn(t, build, convolve, fin):
                    h = 0
                    for c in range(NCH):
                        if build:
                            pe.wait_ge(copied, t * NCH + c + 1 + NCH - before(CBANK, c))
                            for n in range(CH[c]):
                                w = START[c] + n
                                pe.wait_ge(hot, t * WB + w + 1)
                                pe.matmul(bank(s, CBANK[c], BL, n * BL, BL), hot_lo[:, w % R, :], hot_key[:, w % R, :],
                                          start=True, stop=True).then_inc(used, 1)
                        if convolve and c == 0:
                            pe.wait_ge(copied, t * NCH + NCH)
                            pe.wait_ge(summed, t)
                        if convolve:
                            while h * NCH < (c + 1) * NB:
                                pe.matmul(dst, s.adj[0:BL, bass.ds((t - 1) * N + h * BL, BL)], s.h1[:, h, :],
                                          start=(h == 0), stop=False, skip_group_check=True)
                                h += 1
                    if convolve:
                        pe.matmul(dst, s.ident16[0:BL, 0:BL], blk(s.h1[:, :, :], t - 1), start=False, stop=True,
                                  skip_group_check=True).then_inc(conv, 1)

                turns(pe, turn)
            pe.end_ifs()


def convolve_again(nc, s):
    with ExitStack() as ctx:
        def sem(name):
            return semaphore(nc, s, "ca_" + name)

        conv, scaled = sem("conv"), sem("scaled")
        adj = s.adj[0:BL, 0:NB * N].rearrange("p (j h d) -> p j h d", j=NB, d=BL)
        block = ctx.enter_context(nc.Block())

        @block.vector
        def _(dve):
            covered = dve.value_load(s.flag[0:1, 0:1])
            with dve.If(covered == E):
                start_at(dve, [scaled], 2)

                def scale(c, b, n):
                    dve.wait_ge(conv, c + 1)
                    v = s.dinvB[:, bass.ds(c * 4 * BL, n * BL)]
                    dve.scalar_tensor_tensor(v, bank(s, b, 128, 0, n * BL), s.inv_s[:, 0:1], v, ALU.mult,
                                             ALU.mult).then_inc(scaled, 1)

                with dve.Fori(0, 3) as r:
                    scale(2 * r, 0, 4)
                    scale(2 * r + 1, 1, 4)
                scale(6, 0, 1)
                dve.wait_ge(scaled, 9)
            dve.end_ifs()

        @block.tensor
        def _(pe):
            covered = pe.value_load(s.flag[0:1, 0:1])
            with pe.If(covered == E):
                def sums(c, b, n):
                    pe.wait_ge(scaled, c + 1)
                    for h in range(NB):
                        rhs = adj[:, bass.ds(c * 4, n), h, :] if n > 1 else s.adj[0:BL, (4 * c) * N + h * BL:
                                                                                 (4 * c) * N + (h + 1) * BL]
                        for p in range(2):
                            pe.matmul(bank(s, b, 128, 0, n * BL), s.h2[:, h, p * HID:(p + 1) * HID], rhs,
                                      start=(h == 0 and p == 0), stop=False, skip_group_check=True)
                    for k in range(n):
                        for p in range(2):
                            mm = pe.matmul(bank(s, b, 128, k * BL, BL), blk(s.h2[:, :, p * HID:(p + 1) * HID], c * 4 + k),
                                           s.ident16[0:BL, 0:BL], start=False, stop=(k == n - 1 and p == 1),
                                           skip_group_check=True)
                    mm.then_inc(conv, 1)

                with pe.Fori(0, 3) as r:
                    sums(2 * r, 0, 4)
                    sums(2 * r + 1, 1, 4)
                sums(6, 0, 1)
            pe.end_ifs()


def general(nc, s):
    t = s.t
    with ExitStack() as ctx:
        def sem(name):
            return semaphore(nc, s, "ge_" + name)

        s.used = 0
        src = take(s, 128, [GC], I32)
        dst_i = take(s, 128, [GC], I32)
        dst = take(s, 128, [GC])
        iota_i = take(s, 128, [N], I32)
        iota = take(s, 128, [N])
        hot = take(s, 128, [N])
        idx = take(s, 128, [1], I32)
        got = take(s, 128, [HID])
        ratio = take(s, BL, [NB])
        dinv = take(s, BL, [NB])
        rowsT = take(s, 128, [N])
        table = take(s, BL, [NB, HID])
        zeros = take(s, 128, [128])
        CN = [(c * 500, min(500, N - c * 500)) for c in range(7)]
        in_s, iota_r, step, idx_r, got_r = sem("in"), sem("iota"), sem("step"), sem("idx"), sem("got")
        hot_r, mm_r, sums_r, pow_r, cols_r = sem("hot"), sem("mm"), sem("sums"), sem("pow"), sem("cols")
        rows_r, tr_r, table_r, table_d, read, ready = (sem(x) for x in ("rows", "tr", "table", "tabled", "read", "ready"))
        block = ctx.enter_context(nc.Block())

        @block.sync
        def _(sp):
            covered = sp.value_load(s.flag[0:1, 0:1])
            with sp.If(covered != E):
                sp.dma_start(src, t["src_all"]).then_inc(in_s, 16)
                sp.wait_ge(in_s, 16)
                sp.dma_start(dst_i, t["dst_all"]).then_inc(in_s, 16)
                for p in range(2):
                    sp.wait_ge(table_r, p + 1)
                    sp.dma_start(s.table_d.rearrange("(b p) c -> p b c", p=BL), table).then_inc(table_d, 16)
                sp.wait_ge(table_d, 32)
            sp.end_ifs()

        @block.gpsimd
        def _(pool):
            covered = pool.value_load(s.flag[0:1, 0:1])
            with pool.If(covered != E):
                pool.iota(iota_i, pattern=[[1, N]], base=0, channel_multiplier=0).then_inc(iota_r, 1)
                pool.wait_ge(sums_r, 1)
                pool.tensor_tensor(s.dinvB[:, :], s.dinvB[:, :], s.half[:, 0:1].to_broadcast([128, N]),
                                   ALU.pow).then_inc(pow_r, 1)
                for p in range(2):
                    pool.wait_ge(table_d, 16 * (p + 1))
                    with pool.Fori(0, GC) as c:
                        pool.wait_ge(mm_r, c + 1 + (p + 1) * (GC + 1))
                        pool.tensor_copy(idx, src[:, bass.ds(c, 1)]).then_inc(idx_r, 1)
                        hold(pool, s.held, (idx_r, c + 1 + p * GC))
                        pool.indirect_dma_start(out=got, out_offset=None, in_=s.table_d,
                                                in_offset=bass.IndirectOffsetOnAxis(ap=idx, axis=0)
                                                ).then_inc(got_r, 16)
                        pool.wait_ge(got_r, 16 * (c + 1 + p * GC))
            pool.end_ifs()

        @block.vector
        def _(dve):
            covered = dve.value_load(s.flag[0:1, 0:1])
            with dve.If(covered != E):
                chain = [0]

                def link(ins):
                    chain[0] += 1
                    ins.then_inc(step, 1)
                    dve.wait_ge(step, chain[0])

                dve.wait_ge(in_s, 32)
                dve.wait_ge(iota_r, 1)
                link(dve.tensor_copy(dst, dst_i))
                link(dve.memset(zeros, 0.0))
                link(dve.tensor_copy(iota, iota_i))
                dve.sem_inc(ready, 1)
                for p in range(3):
                    with dve.Fori(0, GC) as c:
                        dve.wait_ge(mm_r, c + 1 + p * (GC + 1))
                        dve.tensor_scalar(hot, iota, dst[:, bass.ds(c, 1)], None, ALU.is_equal).then_inc(hot_r, 1)
                    dve.wait_ge(mm_r, (p + 1) * (GC + 1))
                    if p == 0:
                        for c, (a, n) in enumerate(CN):
                            link(dve.tensor_copy(s.dinvB[:, a:a + n], bank(s, c, 128, 0, n)))
                        dve.sem_inc(sums_r, 1)
                        dve.wait_ge(cols_r, 1)
                        link(dve.tensor_copy(dinv, bank(s, 7, BL, 0, NB)))
                        link(dve.reciprocal(ratio, s.dinvN[:, :]))
                        link(dve.tensor_tensor(ratio, ratio, dinv, ALU.mult))
                        link(dve.tensor_tensor(table, s.h1[:, :, 0:HID], s.h1[:, :, HID:2 * HID], ALU.add))
                        link(dve.tensor_tensor(table, table, bc(ratio, HID), ALU.mult))
                        dve.sem_inc(table_r, 1)
                        dve.sem_inc(mm_r, 1)
                    if p == 1:
                        for c, (a, n) in enumerate(CN):
                            link(dve.tensor_copy(rowsT[:, a:a + n], bank(s, c, 128, 0, n)))
                        dve.sem_inc(rows_r, 1)
                        dve.wait_ge(table_d, 16)
                        for b in range(NB):
                            dve.wait_ge(tr_r, b + 1)
                            v = table[:, b, :]
                            link(dve.scalar_tensor_tensor(v, bank(s, 7, BL, 0, HID), dinv[:, b:b + 1], s.sb1[:, :],
                                                          ALU.mult, ALU.add))
                            dve.sem_inc(read, 1)
                            link(dve.tensor_scalar(v, v, 0.0, dinv[:, b:b + 1], ALU.max, ALU.mult))
                        dve.sem_inc(table_r, 1)
                        dve.sem_inc(mm_r, 1)
                    if p == 2:
                        for c, (a, n) in enumerate(CN):
                            v = s.dinvB[:, a:a + n]
                            link(dve.scalar_tensor_tensor(v, bank(s, c, 128, 0, n), s.inv_s[:, 0:1], v, ALU.mult, ALU.mult))
            dve.end_ifs()

        @block.tensor
        def _(pe):
            covered = pe.value_load(s.flag[0:1, 0:1])
            with pe.If(covered != E):
                pe.wait_ge(ready, 1)
                pe.sem_inc(mm_r, 1)
                for p in range(3):
                    lhsT = s.ones[:, :] if p == 0 else got
                    if p:
                        pe.wait_ge(mm_r, p * (GC + 1) + 1)
                    for c, (a, n) in enumerate(CN):
                        pe.matmul(bank(s, c, 128, 0, n), zeros, iota[:, a:a + n], start=True, stop=False,
                                  skip_group_check=True)
                    with pe.Fori(0, GC) as k:
                        pe.wait_ge(hot_r, k + 1 + p * GC)
                        if p:
                            pe.wait_ge(got_r, 16 * (k + 1 + (p - 1) * GC))
                        for c, (a, n) in enumerate(CN):
                            mm = pe.matmul(bank(s, c, 128, 0, n), lhsT, hot[:, a:a + n], start=False, stop=False,
                                           skip_group_check=True)
                        mm.then_inc(mm_r, 1)
                    if p == 0:
                        pe.wait_ge(pow_r, 1)
                        for b in range(NB):
                            mm = pe.matmul(bank(s, 7, BL, b, 1), s.dinvB[0:1, b * BL:(b + 1) * BL], s.ones[0:1, 0:1],
                                           start=True, stop=True)
                        mm.then_inc(cols_r, 1)
                    if p == 1:
                        pe.wait_ge(rows_r, 1)
                        for b in range(NB):
                            if b:
                                pe.wait_ge(read, b)
                            pe.transpose(bank(s, 7, BL, 0, HID), rowsT[:, b * BL:(b + 1) * BL],
                                         s.ident[:, :]).then_inc(tr_r, 1)
            pe.end_ifs()


def slices(nc, s):
    t = s.t
    with ExitStack() as ctx:
        def sem(name):
            return semaphore(nc, s, "sl_" + name)

        s.used = 0
        s.x2 = take(s, BL, [NB, D])
        s.swT = take(s, 128, [NB, INNER // 128 * BL])
        s.wsum = take(s, BL, [INNER])
        s.UT = take(s, 128, [KC, INNER])
        s.keep = s.used
        agg = take(s, 128, [U, BL])
        x1 = take(s, BL, [U, D])
        st = take(s, BL, [U, 6])
        mv = take(s, BL, [U, 2])
        ve = take(s, BL, [U])
        rstd = take(s, BL, [U])
        y = take(s, BL, [U, D])
        yT = take(s, 128, [U, KC * BL])
        lg = take(s, BL, [U, INNER])
        mx = take(s, BL, [U, FH])
        sm = take(s, BL, [U, FH])
        rc = take(s, BL, [U, FH])
        G2, TP, LG, UTB, SWT = 0, [1, 2], [3, 4], 5, 7
        names = ("agg", "w2", "x2", "st", "mv", "ve", "rstd", "y", "tp", "yT", "lgmm", "lg", "mx", "sub", "ex", "sm", "rc",
                 "sw", "swt", "swT", "ut", "acc", "kept")
        (agg_r, w2_r, x2_r, st_r, mv_r, ve_r, rstd_r, y_r, tp_r, yT_r, lgmm_r, lg_r, mx_r, sub_r, ex_r, sm_r, rc_r,
         sw_r, swt_r, swT_r, ut_r, acc_r, x2_kept) = sems = [sem(x) for x in names]
        loaded = [sem(f"x1_{u}") for u in range(U)]
        zeroed, ut_kept = sem("zeroed"), sem("utkept")
        block = ctx.enter_context(nc.Block())

        def heads(ap):
            return ap.rearrange("p (h g) -> p h g", g=G)

        @block.sync
        def _(sp):
            start_at(sp, sems)

            def load(i, u, r):
                sp.wait_ge(x2_kept, at(i) - U)
                sp.wait_ge(st_r, at(i) - U)
                sp.dma_start(x1[:, u, :], rows(s.x1_d, i)).then_inc(loaded[u], 16)

            pipelined(sp, (0, load))

        @block.scalar
        def _(act):
            def static(i, u, r):
                act.wait_ge(w2_r, at(i) - U)
                act.activation(agg[:, u, :], s.dinvB[:, bass.ds(i * BL, BL)], ACT.Copy).then_inc(agg_r, 1)

            def turned(i, u, r):
                act.wait_ge(tp_r, at(i))
                act.wait_ge(lgmm_r, at(i) - U)
                act.activation(yT[:, u, :], bank(s, TP[TWO[u]], 128, 0, KC * BL), ACT.Copy).then_inc(yT_r, 1)

            def exponent(i, u, r):
                act.wait_ge(sub_r, at(i))
                act.activation(lg[:, u, :], lg[:, u, :], ACT.Exp).then_inc(ex_r, 1)

            def weights_turned(i, u, r):
                act.wait_ge(swt_r, at(i))
                act.activation(blk(s.swT, i), bank(s, SWT, 128, 0, 4 * BL), ACT.Copy).then_inc(swT_r, 1)

            pipelined(act, (0, static), (1, turned), (3, exponent), (4, weights_turned))
            act.wait_ge(acc_r, NB + U)
            act.activation(s.UT.rearrange("p k n -> p (k n)"), s.PS[:, UTB * BANK:(UTB + 2) * BANK],
                           ACT.Copy).then_inc(ut_kept, 1)
            act.wait_ge(ut_kept, 1)

        @block.vector
        def _(dve):
            def residual(i, u, r):
                dve.wait_ge(w2_r, at(i))
                dve.wait_ge(loaded[u], r * 16 + 16)
                dve.tensor_tensor(x1[:, u, :], bank(s, G2, BL, 0, D), x1[:, u, :], ALU.add).then_inc(x2_r, 1)
                dve.wait_ge(x2_r, at(i))
                dve.bn_stats(st[:, u, :], x1[:, u, :]).then_inc(st_r, 1)
                hold(dve, s.held, (st_r, at(i)), (y_r, at(i) - U))
                dve.bn_aggr(mv[:, u, :], st[:, u, :]).then_inc(mv_r, 1)

            def logits(i, u, r):
                dve.wait_ge(lgmm_r, at(i))
                dve.wait_ge(ut_r, at(i) - U)
                dve.wait_ge(acc_r, at(i) - U)
                dve.wait_ge(swt_r, at(i) - U)
                dve.tensor_tensor(lg[:, u, :], bank(s, LG[TWO[u]], BL), s.biasC[:, :], ALU.add).then_inc(lg_r, 1)
                dve.wait_ge(lg_r, at(i))
                dve.tensor_reduce(mx[:, u, :], heads(lg[:, u, :]), AX.X, ALU.max).then_inc(mx_r, 1)
                dve.wait_ge(mx_r, at(i))
                dve.tensor_tensor(heads(lg[:, u, :]), heads(lg[:, u, :]), bc(mx[:, u, :], G),
                                  ALU.subtract).then_inc(sub_r, 1)

            def weigh(i, u, r):
                dve.wait_ge(ex_r, at(i))
                dve.tensor_reduce(sm[:, u, :], heads(lg[:, u, :]), AX.X, ALU.add).then_inc(sm_r, 1)
                dve.wait_ge(sm_r, at(i))
                dve.reciprocal(rc[:, u, :], sm[:, u, :]).then_inc(rc_r, 1)
                dve.wait_ge(rc_r, at(i))
                dve.tensor_tensor(heads(lg[:, u, :]), heads(lg[:, u, :]), bc(rc[:, u, :], G),
                                  ALU.mult).then_inc(sw_r, 1)

            pipelined(dve, (0, residual), (2, logits), (3, weigh))

        @block.gpsimd
        def _(pool):
            pool.memset(s.wsum, 0.0).then_inc(zeroed, 1)
            pool.wait_ge(zeroed, 1)

            def norm(i, u, r):
                hold(pool, s.held, (mv_r, at(i)))
                pool.tensor_scalar(ve[:, u:u + 1], mv[:, u, 1:2], EPS, None, ALU.add).then_inc(ve_r, 1)
                pool.wait_ge(ve_r, at(i))
                pool.tensor_tensor(rstd[:, u:u + 1], ve[:, u:u + 1], s.half[0:BL, 0:1], ALU.pow).then_inc(rstd_r, 1)
                hold(pool, s.held, (rstd_r, at(i)), (acc_r, at(i) - U))
                pool.tensor_scalar(y[:, u, :], x1[:, u, :], mv[:, u, 0:1], rstd[:, u:u + 1], ALU.subtract,
                                   ALU.mult).then_inc(y_r, 1)
                pool.tensor_copy(blk(s.x2, i), x1[:, u, :]).then_inc(x2_kept, 1)

            def total(i, u, r):
                pool.wait_ge(sw_r, at(i))
                pool.wait_ge(ut_r, at(i) - 1)
                pool.tensor_tensor(s.wsum, s.wsum, lg[:, u, :], ALU.add).then_inc(ut_r, 1)

            pipelined(pool, (0, norm), (4, total))

        @block.tensor
        def _(pe):
            def gcn_out(i, u, r):
                pe.wait_ge(agg_r, at(i))
                pe.wait_ge(x2_r, at(i) - 1)
                pe.matmul(bank(s, G2, BL, 0, D), agg[:, u, :], s.W2[:, :], start=True, stop=True).then_inc(w2_r, 1)

            def turn(i, u, r):
                pe.wait_ge(y_r, at(i))
                pe.wait_ge(yT_r, at(i) - before(TWO, u))
                for k in range(KC):
                    mm = pe.transpose(bank(s, TP[TWO[u]], 128, k * BL, BL), y[:, u, k * 128:(k + 1) * 128],
                                      s.ident[0:BL, 0:BL])
                mm.then_inc(tp_r, 1)

            def logits(i, u, r):
                pe.wait_ge(yT_r, at(i))
                pe.wait_ge(lg_r, at(i) - before(TWO, u))
                for k in range(KC):
                    mm = pe.matmul(bank(s, LG[TWO[u]], BL), yT[:, u, k * BL:(k + 1) * BL], s.Wc[:, k, :],
                                   start=(k == 0), stop=(k == KC - 1))
                mm.then_inc(lgmm_r, 1)

            def sums(i, u, r):
                pe.wait_ge(sw_r, at(i))
                pe.wait_ge(swT_r, at(i) - 1)
                for c in range(4):
                    mm = pe.transpose(bank(s, SWT, 128, c * BL, BL), lg[:, u, c * 128:(c + 1) * 128],
                                      s.ident[0:BL, 0:BL])
                mm.then_inc(swt_r, 1)
                for k in range(KC):
                    mm = pe.matmul(bank(s, UTB + k), y[:, u, k * 128:(k + 1) * 128], lg[:, u, :],
                                   start=isinstance(i, int) and i == 0, stop=isinstance(i, int) and i == NB - 1,
                                   skip_group_check=True)
                mm.then_inc(acc_r, 1)

            pipelined(pe, (0, gcn_out), (1, turn), (2, logits), (4, sums))


def tokens(nc, s):
    t = s.t
    with ExitStack() as ctx:
        def sem(name):
            return semaphore(nc, s, "to_" + name)

        s.used = s.keep
        s.T = take(s, 128, [4, D])
        s.keep = s.used
        Wfx = take(s, 128, [KC, INNER])
        Wq, Wk, Wv = (take(s, G, [G]) for _ in range(3))
        Wout = take(s, G, [FH, D])
        bfx = take(s, G, [FH])
        nrm = take(s, G, [INNER])
        rn = take(s, G, [INNER])
        tok = take(s, G, [INNER])
        qT, kT, vT = (take(s, G, [INNER]) for _ in range(3))
        sc = take(s, G, [INNER])
        mx = take(s, G, [FH])
        sm = take(s, G, [FH])
        aT = take(s, G, [INNER])
        vW = take(s, G, [FH * D])
        Th = take(s, G, [FH, D])
        loads = [("fx", Wfx, t["W_fx"].rearrange("(k p) n -> p k n", p=128)), ("q", Wq, t["W_q"]), ("k", Wk, t["W_k"]),
                 ("v", Wv, t["W_v"]), ("out", Wout, t["W_out"].rearrange("(h c) n -> c h n", c=G)), ("bfx", bfx, t["bfxT"])]
        got = {n: sem("in" + n) for n, _, _ in loads}
        step, tok_r, qkv_r, ex_r, attn_r, aT_r, vW_r, Th_r = (sem(x) for x in ("s", "tok", "qkv", "ex", "at", "aT", "vW", "Th"))
        m_n, m_t, m_q, m_s, m_a, m_v, m_T, moved = (sem(x) for x in ("mn", "mt", "mq", "ms", "ma", "mv", "mT", "moved"))
        sub_r = sem("sub")
        block = ctx.enter_context(nc.Block())

        def heads(ap):
            return ap.rearrange("p (h g) -> p h g", g=G)

        @block.sync
        def _(sp):
            for n, d, src in loads:
                sp.dma_start(d, src).then_inc(got[n], 16)
            sp.wait_ge(Th_r, 1)
            pairs = Th.rearrange("p (c a) n -> p a c n", a=2)
            for a in range(2):
                sp.dma_start(s.T[a * G:(a + 1) * G, :, :], pairs[:, a, :, :]).then_inc(moved, 16)
            sp.wait_ge(moved, 32)

        @block.vector
        def _(dve):
            chain = [0]

            def link(ins):
                chain[0] += 1
                ins.then_inc(step, 1)
                dve.wait_ge(step, chain[0])

            dve.wait_ge(m_n, 1)
            link(dve.tensor_scalar(rn, bank(s, 0, G), EPS, None, ALU.add))
            link(dve.reciprocal(rn, rn))
            dve.wait_ge(got["bfx"], 16)
            link(dve.tensor_tensor(heads(nrm), heads(bank(s, 0, G)), bc(bfx, G), ALU.mult))
            dve.wait_ge(m_t, 1)
            link(dve.tensor_tensor(nrm, nrm, bank(s, 1, G), ALU.add))
            dve.tensor_tensor(tok, nrm, rn, ALU.mult).then_inc(tok_r, 1)
            dve.wait_ge(m_q, 1)
            for n, d in enumerate((qT, kT, vT)):
                link(dve.tensor_copy(d, bank(s, 2 + n, G)))
            dve.sem_inc(qkv_r, 1)
            dve.wait_ge(m_s, 1)
            link(dve.tensor_scalar(sc, bank(s, 5, G), G ** -0.5, None, ALU.mult))
            link(dve.tensor_reduce(mx, heads(sc), AX.X, ALU.max))
            dve.tensor_tensor(heads(sc), heads(sc), bc(mx, G), ALU.subtract).then_inc(sub_r, 1)
            dve.wait_ge(ex_r, 1)
            link(dve.tensor_reduce(sm, heads(sc), AX.X, ALU.add))
            link(dve.reciprocal(mx, sm))
            dve.tensor_tensor(heads(sc), heads(sc), bc(mx, G), ALU.mult).then_inc(attn_r, 1)
            dve.wait_ge(m_a, 1)
            dve.tensor_copy(aT, bank(s, 6, G)).then_inc(aT_r, 1)

        @block.scalar
        def _(act):
            act.wait_ge(sub_r, 1)
            act.activation(sc, sc, ACT.Exp).then_inc(ex_r, 1)
            act.wait_ge(m_v, 1)
            act.activation(vW, s.PS[0:G, 0:4 * BANK], ACT.Copy).then_inc(vW_r, 1)
            act.wait_ge(m_T, 1)
            act.activation(Th.rearrange("p h n -> p (h n)"), s.PS[0:G, 0:4 * BANK], ACT.Copy).then_inc(Th_r, 1)

        @block.tensor
        def _(pe):
            pe.matmul(bank(s, 0, G), s.ones[0:BL, 0:G], s.wsum, start=True, stop=True).then_inc(m_n, 1)
            pe.wait_ge(got["fx"], 16)
            for h in range(FH):
                for k in range(KC):
                    mm = pe.matmul(bank(s, 1, G, h * G, G), Wfx[:, k, h * G:(h + 1) * G], s.UT[:, k, h * G:(h + 1) * G],
                                   start=(k == 0), stop=(k == KC - 1))
            mm.then_inc(m_t, 1)
            pe.wait_ge(tok_r, 1)
            for n, (w, m) in enumerate((("q", Wq), ("k", Wk), ("v", Wv))):
                pe.wait_ge(got[w], 16)
                mm = pe.matmul(bank(s, 2 + n, G), m, tok, start=True, stop=True)
            mm.then_inc(m_q, 1)
            pe.wait_ge(qkv_r, 1)
            for h in range(FH):
                mm = pe.matmul(bank(s, 5, G, h * G, G), qT[:, h * G:(h + 1) * G], kT[:, h * G:(h + 1) * G],
                               start=True, stop=True)
            mm.then_inc(m_s, 1)
            pe.wait_ge(got["out"], 16)
            for h in range(FH):
                mm = pe.matmul(s.PS[0:G, h * D:(h + 1) * D], vT[:, h * G:(h + 1) * G], Wout[:, h, :],
                               start=True, stop=True)
            mm.then_inc(m_v, 1)
            pe.wait_ge(attn_r, 1)
            for h in range(FH):
                mm = pe.transpose(bank(s, 6, G, h * G, G), sc[:, h * G:(h + 1) * G], s.ident[0:G, 0:G])
            mm.then_inc(m_a, 1)
            pe.wait_ge(aT_r, 1)
            pe.wait_ge(vW_r, 1)
            for h in range(FH):
                mm = pe.matmul(s.PS[0:G, h * D:(h + 1) * D], aT[:, h * G:(h + 1) * G], vW[:, h * D:(h + 1) * D],
                               start=True, stop=True)
            mm.then_inc(m_T, 1)


def output(nc, s):
    with ExitStack() as ctx:
        def sem(name):
            return semaphore(nc, s, "ou_" + name)

        s.used = s.keep
        sw = take(s, 128, [U, 4 * BL])
        o = take(s, BL, [U, D])
        bout = take(s, BL, [D])
        in_b = sem("bout")
        OB = [0, 1]
        mm_r, o_r, xb_r = sem("mm"), sem("o"), sem("xb")
        moved, sent = [sem(f"m{u}") for u in range(U)], [sem(f"s{u}") for u in range(U)]
        block = ctx.enter_context(nc.Block())

        @block.sync
        def _(sp):
            start_at(sp, [mm_r, o_r, xb_r])
            sp.dma_start(bout, s.t["b_out"].partition_broadcast(BL)).then_inc(in_b, 16)
            start_at(sp, sent, 16)

            def static(i, u, r):
                sp.wait_ge(mm_r, at(i) - U)
                sp.dma_start(sw[:, u, :], blk(s.swT, i)).then_inc(moved[u], 16)

            pipelined(sp, (0, static))

        @block.gpsimd
        def _(pool):
            pool.wait_ge(in_b, 16)

            def add_bias(i, u, r):
                pool.tensor_tensor(blk(s.x2, i), blk(s.x2, i), bout, ALU.add).then_inc(xb_r, 1)

            pipelined(pool, (0, add_bias))

        @block.scalar
        def _(act):
            def send(i, u, r):
                act.wait_ge(o_r, at(i))
                act.dma_start(rows(s.out, i), o[:, u, :]).then_inc(sent[u], 16)

            pipelined(act, (0, send))
            for u in range(U):
                act.wait_ge(sent[u], 16 * IT + 16)

        @block.vector
        def _(dve):
            def add(i, u, r):
                dve.wait_ge(mm_r, at(i))
                dve.wait_ge(xb_r, at(i))
                dve.wait_ge(sent[u], r * 16 + 16)
                dve.tensor_tensor(o[:, u, :], bank(s, OB[TWO[u]], BL, 0, D), blk(s.x2, i), ALU.add).then_inc(o_r, 1)

            pipelined(dve, (0, add))

        @block.tensor
        def _(pe):
            def mix(i, u, r):
                pe.wait_ge(moved[u], r * 16 + 16)
                pe.wait_ge(o_r, at(i) - before(TWO, u))
                for c in range(4):
                    mm = pe.matmul(bank(s, OB[TWO[u]], BL, 0, D), sw[:, u, c * BL:(c + 1) * BL], s.T[:, c, :],
                                   start=(c == 0), stop=(c == 3))
                mm.then_inc(mm_r, 1)

            pipelined(pe, (0, mix))


def kernel(x, src, dst, L0_gnn_W1, L0_gnn_b1, L0_gnn_W2, L0_gnn_b2, L0_mix_wq, L0_mix_wk, L0_mix_wv, L0_mix_wo, L0_mix_bo,
           L0_mix_ln_k_g, L0_mix_ln_k_b, L0_mix_ln_v_g, L0_mix_ln_v_b, L0_ffn_W_fx, L0_ffn_b_fx, L0_ffn_W_x, L0_ffn_b_x,
           L0_ffn_W_slice, L0_ffn_b_slice, L0_ffn_W_q, L0_ffn_W_k, L0_ffn_W_v, L0_ffn_W_out, L0_ffn_b_out,
           L0_ffn_temperature):
    import numpy as np
    import concourse.bacc as bacc
    from concourse.bass_utils import run_bass_kernel_spmd

    src, dst = np.asarray(src), np.asarray(dst)
    loops = np.arange(N, dtype=src.dtype)
    pad = np.zeros(GE - E - N, dtype=src.dtype)
    laid = {
        "x": x, "dst": dst,
        "edges": np.stack([src, dst], axis=1).reshape(-1),
        "firsts": dst[::BL],
        "src_all": np.concatenate([src, loops, pad]).reshape(128, GC),
        "dst_all": np.concatenate([dst, loops, pad - 1]).reshape(128, GC),
        "W1": L0_gnn_W1, "b1": L0_gnn_b1, "W2": L0_gnn_W2, "b2": L0_gnn_b2,
        "wq": L0_mix_wq, "wkvT": np.concatenate([np.asarray(L0_mix_wk).T, np.asarray(L0_mix_wv).T], axis=1),
        "woT": np.asarray(L0_mix_wo).T, "bo": L0_mix_bo,
        "ln": np.stack([L0_mix_ln_k_g, L0_mix_ln_k_b, L0_mix_ln_v_g, L0_mix_ln_v_b], axis=1),
        "W_fx": L0_ffn_W_fx, "bfxT": np.asarray(L0_ffn_b_fx).reshape(FH, G).T, "WxT": np.asarray(L0_ffn_W_x).T,
        "bxT": np.asarray(L0_ffn_b_x).reshape(FH, G).T, "W_slice": L0_ffn_W_slice, "b_slice": L0_ffn_b_slice,
        "W_q": L0_ffn_W_q, "W_k": L0_ffn_W_k, "W_v": L0_ffn_W_v, "W_out": L0_ffn_W_out, "b_out": L0_ffn_b_out,
        "temp": np.asarray(L0_ffn_temperature).reshape(FH),
    }
    nc = bacc.Bacc("TRN2", target_bir_lowering=False, num_devices=1)
    arrays, t = {}, {}
    for name, a in laid.items():
        a = np.ascontiguousarray(a)
        arrays["in_" + name] = a
        t[name] = nc.dram_tensor("in_" + name, a.shape, mybir.dt.from_np(a.dtype), kind="ExternalInput").ap()
    out = nc.dram_tensor("out_0", (N, D), F32, kind="ExternalOutput").ap()
    build(nc, t, out)
    return run_bass_kernel_spmd(nc, [arrays], core_ids=[0]).results[0]["out_0"]
```

```python
import concourse.bass as bass
from concourse import mybir
from contextlib import ExitStack

F32 = mybir.dt.float32
F16 = mybir.dt.float16
I32 = mybir.dt.int32
ALU = mybir.AluOpType
ACT = mybir.ActivationFunctionType
AX = mybir.AxisListType

N = 3125
E = 50000
D = 256
HID = 128
BL = 125
NB = N // BL
U = 5
IT = NB // U
KC = D // 128
W = 5
NW = N // W
WB = BL // W
NQ = NW // BL
SLOTS = 128
HEADS, HD = 4, 64
FH, G = 8, 64
INNER = FH * G
BANK = 512
EPS = 1e-5
ROUND = 12582912.0
LIMIT = 16384.0
CH = [4, 4, 4, 4, 3, 3, 3]
GROUPS = WB // W
TAIL = (KC + 2) * INNER + 2 * FH
GE = 416 * 128
GC = GE // 128


TWO = [0, 1, 0, 1, 0]
THREE = [0, 1, 2, 0, 1]


def at(i):
    return i + 1 + U


def semaphore(nc, s, name):
    s.phase_semaphores.append(nc.alloc_semaphore(name=name))
    return s.phase_semaphores[-1]


def hold(eng, held, *waits):
    for sem, value in waits:
        eng.wait_ge(sem, value)
    eng.sem_inc(held, 1)


def start_at(eng, sems, n=U):
    for x in sems:
        eng.sem_inc(x, n)


def pipelined(eng, *steps):
    assert max(lag for lag, _ in steps) < U
    for t in range(U):
        for lag, f in steps:
            if t >= lag:
                f(t - lag, (t - lag) % U, (t - lag) // U)
    with eng.Fori(1, IT) as it:
        for u in range(U):
            for lag, f in steps:
                f(it * U + (u - lag), (u - lag) % U, it + (u - lag) // U)
    for t in range(NB, NB + max(lag for lag, _ in steps)):
        for lag, f in steps:
            if t - lag < NB:
                f(t - lag, (t - lag) % U, (t - lag) // U)


def before(slots, u):
    n = len(slots)
    d = 1
    while slots[(u - d) % n] != slots[u]:
        d += 1
    return d


def bc(ap, n):
    return ap.unsqueeze(2).to_broadcast([ap.shape[0], ap.shape[1], n])


def blk(ap, i):
    return ap[:, bass.ds(i, 1), :].rearrange("p a c -> p (a c)")


def rows(dram, i):
    return dram.rearrange("(b p) c -> b p c", p=BL)[bass.ds(i, 1)].rearrange("a p c -> (a p) c")


class Store:
    pass


def build(nc, t, out):
    with ExitStack() as ctx:
        s = Store()
        s.t, s.out = t, out

        def sb(name, shape, dt=F32):
            return ctx.enter_context(nc.sbuf_tensor(name, shape, dt))

        def dram(name, shape, dt=F32):
            return nc.dram_tensor(name, shape, dt, kind="Internal").ap()

        s.xnT_d = dram("xnT_spill", (NB * 128, KC * BL))
        s.table_d = dram("table_spill", (N, HID))
        s.adj = sb("adj", [128, NB * N + 1], F16)
        s.h1_flat = sb("h1_parts", [BL, NB * 2 * HID], F16)
        s.h1 = s.h1_flat[:, :].rearrange("p (b c) -> p b c", b=NB)
        s.h2 = sb("h2_parts", [BL, NB, 2 * HID], F16)
        s.aggT = sb("agg_rows", [128, N])
        s.dinvN = sb("dinv_cols", [BL, NB])
        s.keyT = sb("keyT", [128, NW], F16)
        s.loT = sb("loT", [128, NW], F16)
        s.flag = sb("covered", [128, 1], I32)
        s.ident = sb("ident", [128, 128])
        s.ones = sb("ones", [128, 128])
        s.half = sb("minus_half", [128, 1])
        s.plus = sb("plus_half", [128, 1])
        s.ident16 = sb("ident16", [128, 128], F16)
        s.iotaW = sb("iotaW", [128, BL, W], F16)
        s.sb1 = sb("scaled_b1", [BL, HID])
        s.inv_s = sb("inv_scale", [128, 1])
        s.M = sb("M", [128, KC, D])
        s.bsum = sb("b2_bo", [BL, D])
        s.tail = sb("tail", [128, TAIL])
        s.PS = ctx.enter_context(nc.psum_tensor("PS", [128, 8 * BANK], F32))
        s.held = ctx.enter_context(nc.semaphore("held"))
        s.arena = s.adj[:, :].bitcast(F32)
        s.used = 0

        for phase in (prepare, attention_stats, attention_out,
                      build_and_convolve, general, convolve_again, slices, tokens, output):
            s.phase_semaphores = []
            phase(nc, s)
            nc.clear_and_free_semaphores(s.phase_semaphores)
            nc.all_engine_barrier(sem_only=True)


def take(s, p, shape, dt=F32):
    n = 1
    for a in shape:
        n *= a
    words = n if dt != F16 else (n + 1) // 2
    s.used += words
    assert s.used <= (NB * N + 1) // 2
    return view(s.arena[0:p, s.used - words:s.used], shape, dt)


def view(v, shape, dt=F32):
    n = 1
    for a in shape:
        n *= a
    if dt != F32:
        v = v.bitcast(dt)[:, 0:n]
    if len(shape) == 2:
        v = v.rearrange("p (a b) -> p a b", b=shape[1])
    if len(shape) == 3:
        v = v.rearrange("p (a b c) -> p a b c", b=shape[1], c=shape[2])
    return v


def bank(s, b, p=128, a=0, n=BANK):
    return s.PS[0:p, b * BANK + a:b * BANK + a + n]


def prepare(nc, s):
    t = s.t
    with ExitStack() as ctx:
        def sem(name):
            return semaphore(nc, s, "pr_" + name)

        s.used = 0
        s.Wkv = take(s, 128, [KC, 2 * D])
        s.W1 = take(s, 128, [KC, HID])
        s.X = take(s, HD + 1, [HEADS * D])
        s.Y = take(s, HD + 1, [HEADS * D])
        s.arena_keep = s.used
        sq = take(s, 128, [KC, HID])
        b1B = take(s, BL, [HID])
        b1c = take(s, 128, [1])
        absb = take(s, 128, [1])
        norm = take(s, 128, [1])
        sc = take(s, 128, [1])
        mean = take(s, 128, [KC, 2 * HEADS])
        wq = take(s, HD, [HEADS, D])
        woT = take(s, HD, [HEADS, D])
        ln = take(s, HD, [4])
        GkT = take(s, HD, [HD + 1])
        GvT = take(s, HD, [HD + 1])
        b2B = take(s, BL, [D])
        FC = E // BL
        C = NQ * SLOTS
        row0 = take(s, 128, [BL * W], I32)
        first_i = take(s, BL, [FC], I32)
        first = take(s, BL, [FC])
        t5_i = take(s, BL, [NQ], I32)
        t5 = take(s, BL, [NQ])
        junk = take(s, BL, [FC])
        n1 = take(s, BL, [NQ])
        rowf = take(s, BL, [NQ])
        row_i = take(s, BL, [NQ], I32)
        R = take(s, BL, [NQ, BL], I32)
        n2 = take(s, BL, [NQ])
        at = take(s, BL, [NQ])
        at_i = take(s, BL, [NQ], I32)
        EW = take(s, BL, [NQ, SLOTS * 2], I32)
        src = take(s, BL, [C])
        loc = take(s, BL, [C])
        hi = take(s, BL, [C])
        low_ok = take(s, BL, [C])
        lo = take(s, BL, [C])
        valid = take(s, BL, [C])
        locm = take(s, BL, [C])
        keym = take(s, BL, [C])
        vsum = take(s, BL, [1])
        locT = take(s, 128, [NW], F16)
        L = take(s, 128, [NW, W], F16)
        ones16 = take(s, 128, [128], F16)

        loads = [
            ("first", first_i, t["firsts"].partition_broadcast(BL)),
            ("W1", s.W1, t["W1"].rearrange("(k p) n -> p k n", p=128)),
            ("kv", s.Wkv, t["wkvT"].rearrange("(k p) n -> p k n", p=128)),
            ("ln", ln, t["ln"]),
            ("b1c", b1c, t["b1"].rearrange("(p a) -> p a", a=1)),
            ("wq", wq, t["wq"].rearrange("(h d) n -> d h n", d=HD)),
            ("wo", woT, t["woT"].rearrange("(h d) n -> d h n", d=HD)),
            ("b1", b1B, t["b1"].partition_broadcast(BL)),
            ("b2", b2B, t["b2"].partition_broadcast(BL)),
            ("bo", s.bsum[:, :], t["bo"].partition_broadcast(BL)),
        ]
        got = {name: sem("in_" + name) for name, _, _ in loads}
        thr, zeros, consts, ident_r, spread = sem("thr"), sem("zeros"), sem("consts"), sem("ident"), sem("spread")
        step, squared, norm_mm, norm_sb, norm_pow, sc_r = (sem(x) for x in ("step", "sq", "nmm", "nsb", "npow", "sc"))
        sc_row, gains, folded, xy_kept, kept = sem("scrow"), sem("gains"), sem("folded"), sem("xy"), sem("kept")
        rows_at, rows_in = sem("rowat"), [sem(f"r{q}") for q in range(NQ)]
        edges_at, edges_in = sem("edgeat"), [sem(f"e{q}") for q in range(NQ)]
        divided, masked, turned, counted, flag_mm = sem("div"), sem("mask"), sem("turn"), sem("cnt"), sem("flag")
        hot, deg_mm, deg_sb, deg_pow = sem("hot"), sem("degmm"), sem("degsb"), sem("degpow")
        SC, DEG = 6, 7
        block = ctx.enter_context(nc.Block())

        @block.sync
        def _(sp):
            for name, dst, src_ in loads:
                sp.dma_start(dst, src_).then_inc(got[name], 16)

        @block.gpsimd
        def _(pool):
            pool.iota(t5_i, pattern=[[W * BL, NQ]], base=0, channel_multiplier=W).then_inc(thr, 1)
            pool.memset(s.ident[:, :], 0.0).then_inc(zeros, 1)
            pool.memset(s.ones[:, :], 1.0).then_inc(consts, 1)
            pool.memset(s.half[:, :], -0.5).then_inc(consts, 1)
            pool.memset(s.plus[:, :], 0.5).then_inc(consts, 1)
            pool.memset(ones16, 1.0).then_inc(consts, 1)
            pool.wait_ge(zeros, 1)
            pool.affine_select(out=s.ident[:, :], in_=s.ident[:, :], compare_op=ALU.not_equal, fill=1.0, base=0,
                               pattern=[[-1, 128]], channel_multiplier=1).then_inc(ident_r, 1)
            pool.iota(row0, pattern=[[1, BL], [0, W]], base=0, channel_multiplier=0).then_inc(ident_r, 1)
            pool.wait_ge(consts, 4)
            pool.wait_ge(rows_at, 1)
            for q in range(NQ):
                pool.indirect_dma_start(out=R[:, q, :], out_offset=None, in_=t["dst"].rearrange("(a b) -> a b", b=BL),
                                        in_offset=bass.IndirectOffsetOnAxis(ap=row_i[:, q:q + 1], axis=0)
                                        ).then_inc(rows_in[q], 16)
            pool.wait_ge(norm_sb, 1)
            pool.tensor_tensor(norm, norm, s.plus[:, 0:1], ALU.pow).then_inc(norm_pow, 1)
            pool.wait_ge(edges_at, 1)
            for q in range(NQ):
                pool.indirect_dma_start(out=EW[:, q, :], out_offset=None, in_=t["edges"].rearrange("(a b) -> a b", a=1),
                                        in_offset=bass.IndirectOffsetOnAxis(ap=at_i[:, q:q + 1], axis=1)
                                        ).then_inc(edges_in[q], 16)
            pool.wait_ge(deg_sb, 1)
            pool.tensor_tensor(s.dinvN[:, :], s.dinvN[:, :], s.half[0:BL, 0:1].to_broadcast([BL, NB]),
                               ALU.pow).then_inc(deg_pow, 1)
            pool.wait_ge(deg_pow, 1)

        @block.vector
        def _(dve):
            chain = [0]

            def link(ins):
                chain[0] += 1
                ins.then_inc(step, 1)
                dve.wait_ge(step, chain[0])

            dve.wait_ge(thr, 1)
            link(dve.tensor_copy(t5, t5_i))
            dve.wait_ge(got["first"], 16)
            link(dve.tensor_copy(first, first_i))
            for q in range(NQ):
                link(dve.tensor_scalar(junk, first, t5[:, q:q + 1], 0.0, ALU.is_lt, ALU.add, accum_out=n1[:, q:q + 1]))
            link(dve.tensor_scalar(rowf, n1, 1.0, 0.0, ALU.subtract, ALU.max))
            dve.tensor_copy(row_i, rowf).then_inc(rows_at, 1)

            dve.wait_ge(got["W1"], 16)
            dve.tensor_tensor(sq, s.W1, s.W1, ALU.mult).then_inc(squared, 1)
            dve.wait_ge(got["ln"], 16)
            dve.wait_ge(ident_r, 1)
            for m, a in ((GkT, 0), (GvT, 2)):
                dve.tensor_scalar(m[:, 0:HD], s.ident[0:HD, 0:HD], ln[:, a:a + 1], None, ALU.mult).then_inc(gains, 1)
                dve.tensor_copy(m[:, HD:HD + 1], ln[:, a + 1:a + 2]).then_inc(gains, 1)
            dve.wait_ge(got["kv"], 16)
            kv3 = s.Wkv.rearrange("p k (h d) -> p (k h) d", d=HD)
            m3 = mean.rearrange("p k h -> p (k h)")
            link(dve.tensor_reduce(m3, kv3, AX.X, ALU.add))

            for q in range(NQ):
                dve.wait_ge(rows_in[q], 16)
                link(dve.tensor_scalar(junk[:, 0:BL], R[:, q, :], t5[:, q:q + 1], 0.0, ALU.is_lt, ALU.add,
                                       accum_out=n2[:, q:q + 1]))
            link(dve.scalar_tensor_tensor(at, rowf, float(BL), n2, ALU.mult, ALU.add))
            dve.tensor_scalar(at_i, at, float(E - SLOTS), 2.0, ALU.min, ALU.mult).then_inc(edges_at, 1)

            link(dve.tensor_scalar(m3, m3, -1.0 / HD, None, ALU.mult))
            dve.tensor_tensor(kv3, kv3, bc(m3, HD), ALU.add).then_inc(kept, 1)
            dve.wait_ge(got["b1c"], 16)
            link(dve.tensor_scalar(absb, b1c, -1.0, None, ALU.mult))
            link(dve.tensor_tensor(absb, absb, b1c, ALU.max))
            dve.wait_ge(norm_pow, 1)
            link(dve.scalar_tensor_tensor(norm, norm, 16.0, absb, ALU.mult, ALU.add))
            link(dve.tensor_scalar(s.inv_s[:, :], norm, 1e-20, 1.0 / LIMIT, ALU.max, ALU.mult))
            dve.reciprocal(sc, s.inv_s[:, :]).then_inc(sc_r, 1)
            dve.wait_ge(got["b2"], 16)
            dve.wait_ge(got["bo"], 16)
            dve.tensor_tensor(s.bsum[:, :], s.bsum[:, :], b2B, ALU.add).then_inc(kept, 1)
            dve.wait_ge(sc_row, 1)
            dve.wait_ge(got["b1"], 16)
            dve.tensor_tensor(s.sb1[:, :], b1B, bank(s, SC, BL, 128, HID), ALU.mult).then_inc(kept, 1)
            for k in range(KC):
                dve.tensor_tensor(s.W1[:, k, :], s.W1[:, k, :], bank(s, SC, 128, 128, HID), ALU.mult).then_inc(kept, 1)

            for q in range(NQ):
                dve.wait_ge(edges_in[q], 16)
                pair = EW[:, q, :].rearrange("p (e k) -> p e k", k=2)
                cols = slice(q * SLOTS, (q + 1) * SLOTS)
                dve.tensor_copy(src[:, cols], pair[:, :, 0]).then_inc(divided, 1)
                link(dve.tensor_scalar(loc[:, cols], pair[:, :, 1], t5[:, q:q + 1], None, ALU.subtract))
            link(dve.tensor_scalar(low_ok, loc, 0.0, None, ALU.is_ge))
            link(dve.scalar_tensor_tensor(valid, loc, float(W), low_ok, ALU.is_lt, ALU.mult))
            dve.tensor_reduce(vsum, valid, AX.X, ALU.add).then_inc(counted, 1)
            dve.wait_ge(divided, NQ + 1)
            link(dve.tensor_scalar(hi, hi, ROUND, None, ALU.add))
            link(dve.tensor_scalar(hi, hi, ROUND, None, ALU.subtract))
            dve.scalar_tensor_tensor(lo, hi, -float(BL), src, ALU.mult, ALU.add).then_inc(masked, 1)
            link(dve.scalar_tensor_tensor(locm, loc, 1.0, valid, ALU.add, ALU.mult))
            dve.tensor_scalar(locm, locm, 1.0, None, ALU.subtract).then_inc(masked, 1)
            link(dve.scalar_tensor_tensor(keym, hi, float(W), loc, ALU.mult, ALU.add))
            link(dve.scalar_tensor_tensor(keym, keym, 1.0, valid, ALU.add, ALU.mult))
            dve.tensor_scalar(keym, keym, 1.0, None, ALU.subtract).then_inc(masked, 1)
            dve.wait_ge(turned, 2)
            dve.tensor_copy(locT[:, 0:500], bank(s, 4, 128, 0, 500))
            link(dve.tensor_copy(locT[:, 500:NW], bank(s, 5, 128, 0, 125)))
            for j in range(W):
                dve.tensor_scalar(L[:, :, j], locT, float(j), None, ALU.is_equal).then_inc(hot, 1)
            dve.wait_ge(flag_mm, 1)
            dve.tensor_copy(s.flag[:, :], bank(s, DEG, 128, 0, 1)).then_inc(hot, 1)
            dve.wait_ge(deg_mm, 1)
            dve.tensor_scalar(s.dinvN[:, :], bank(s, DEG, BL, 8, NB), 1.0, None, ALU.add).then_inc(deg_sb, 1)
            dve.wait_ge(kept, 5)
            dve.wait_ge(hot, W + 1)

        @block.scalar
        def _(act):
            act.wait_ge(ident_r, 1)
            act.activation(s.ident16[:, :], s.ident[:, :], ACT.Copy).then_inc(spread, 1)
            act.wait_ge(ident_r, 2)
            act.activation(s.iotaW[:, :, :].rearrange("p c n -> p (c n)"), row0, ACT.Copy).then_inc(spread, 1)
            act.wait_ge(norm_mm, 1)
            act.activation(norm, bank(s, SC, 128, 0, 1), ACT.Copy).then_inc(norm_sb, 1)
            act.wait_ge(folded, 1)
            act.activation(s.X, s.PS[0:HD + 1, 0:2 * BANK], ACT.Copy).then_inc(xy_kept, 1)
            act.wait_ge(folded, 2)
            act.activation(s.Y, s.PS[0:HD + 1, 2 * BANK:4 * BANK], ACT.Copy).then_inc(xy_kept, 1)
            act.wait_ge(divided, NQ)
            act.activation(hi, src, ACT.Copy, scale=1.0 / BL, bias=0.5 / BL - 0.5).then_inc(divided, 1)
            for i, (m, b) in enumerate(((s.loT[:, :], 0), (s.keyT[:, :], 2))):
                act.wait_ge(turned, 2 * i + 1)
                act.activation(m[:, 0:500], bank(s, b, 128, 0, 500), ACT.Copy).then_inc(spread, 1)
                act.activation(m[:, 500:NW], bank(s, b + 1, 128, 0, 125), ACT.Copy).then_inc(spread, 1)
            act.wait_ge(spread, 6)

        @block.tensor
        def _(pe):
            pe.wait_ge(squared, 1)
            pe.wait_ge(consts, 4)
            for k in range(KC):
                mm = pe.matmul(bank(s, SC, 128, 0, 1), sq[:, k, :], s.ones[:, 0:1], start=(k == 0), stop=(k == KC - 1))
            mm.then_inc(norm_mm, 1)
            pe.wait_ge(gains, 4)
            pe.wait_ge(got["wq"], 16)
            pe.wait_ge(got["wo"], 16)
            for m, w, b in ((GkT, wq, 0), (GvT, woT, 2)):
                flat = w.rearrange("p h n -> p (h n)")
                for c in range(2):
                    mm = pe.matmul(bank(s, b + c, HD + 1), m, flat[:, c * BANK:(c + 1) * BANK], start=True, stop=True)
                mm.then_inc(folded, 1)
            pe.wait_ge(sc_r, 1)
            pe.transpose(bank(s, SC, 128, 128, HID), sc.to_broadcast([128, 128]), s.ident[:, :]).then_inc(sc_row, 1)
            pe.wait_ge(xy_kept, 2)
            for i, (m, b) in enumerate(((lo, 0), (locm, 4), (keym, 2))):
                pe.wait_ge(masked, i + 1)
                for q in range(NQ):
                    mm = pe.transpose(bank(s, b + (q == 4), 128, (q % 4) * BL, BL), m[:, q * SLOTS:(q + 1) * SLOTS],
                                      s.ident[0:BL, 0:BL])
                mm.then_inc(turned, 1)
            pe.wait_ge(counted, 1)
            pe.matmul(bank(s, DEG, 128, 0, 1), s.ones[0:BL, :], vsum, start=True, stop=True).then_inc(flag_mm, 1)
            pe.wait_ge(hot, W + 1)
            for b in range(NB):
                mm = pe.matmul(bank(s, DEG, BL, 8 + b, 1), L[:, b * WB:(b + 1) * WB, :].rearrange("p n j -> p (n j)"),
                               ones16[:, 0:1], start=True, stop=True)
            mm.then_inc(deg_mm, 1)


def attention_stats(nc, s):
    t = s.t
    with ExitStack() as ctx:
        def sem(name):
            return semaphore(nc, s, "st_" + name)

        s.used = s.arena_keep
        A1 = HD + 1
        xin = take(s, BL, [U, D])
        xn = take(s, BL, [U, D])
        xnT = take(s, 128, [U, KC * BL])
        st = take(s, BL, [U, 6])
        mv = take(s, BL, [U, 2])
        ve = take(s, BL, [U])
        rstd = take(s, BL, [U])
        sq = take(s, BL, [2, 2 * HEADS, HD + 1])
        ss = take(s, BL, [U, 2 * HEADS])
        rs = take(s, BL, [U, 2 * HEADS])
        kv = take(s, BL, [U * 2 * HEADS, A1])
        KV, TP, HB, AC = [0, 1, 2, 3, 4], 5, 7, 6
        loaded, spilled = [sem(f"x{u}") for u in range(U)], [sem(f"sp{u}") for u in range(U)]
        stats, aggr, ve_r, rstd_r, xn_r = sem("stats"), sem("aggr"), sem("ve"), sem("rstd"), sem("xn")
        tp_r, xnT_r, mm_r, h_hi, h_out = sem("tp"), sem("xnT"), sem("mm"), sem("hhi"), sem("hout")
        sq_r, ss_r, rs_r, kv_r, acc_r, ready, sq_set = (sem(x) for x in ("sq", "ss", "rs", "kv", "acc", "rdy", "sqset"))
        block = ctx.enter_context(nc.Block())

        @block.sync
        def _(sp):
            start_at(sp, [xn_r])

            def load(i, u, r):
                sp.wait_ge(xn_r, at(i) - U)
                sp.dma_start(xin[:, u, :], rows(t["x"], i)).then_inc(loaded[u], 16)

            def spill(i, u, r):
                sp.wait_ge(xnT_r, at(i))
                sp.dma_start(s.xnT_d.rearrange("(b p) c -> b p c", p=128)[bass.ds(i, 1)]
                             .rearrange("a p c -> (a p) c"), xnT[:, u, :]).then_inc(spilled[u], 16)

            pipelined(sp, (0, load), (4, spill))
            for u in range(U):
                sp.wait_ge(spilled[u], 16 * IT + 16)

        @block.vector
        def _(dve):
            start_at(dve, [stats, aggr, ss_r, kv_r, h_out])
            dve.memset(kv[:, :, HD:HD + 1], HD ** -0.5).then_inc(ready, 1)
            dve.memset(sq[:, :, :, HD:HD + 1], HD * EPS).then_inc(ready, 1)
            dve.wait_ge(ready, 2)
            dve.sem_inc(sq_set, 1)

            def statistics(i, u, r):
                dve.wait_ge(loaded[u], r * 16 + 16)
                dve.bn_stats(st[:, u, :], xin[:, u, :]).then_inc(stats, 1)

            def aggregate(i, u, r):
                hold(dve, s.held, (stats, at(i)), (xn_r, at(i) - U))
                dve.bn_aggr(mv[:, u, :], st[:, u, :]).then_inc(aggr, 1)

            def norm(i, u, r):
                dve.wait_ge(rstd_r, at(i))
                dve.wait_ge(tp_r, at(i) - U)
                dve.tensor_scalar(xn[:, u, :], xin[:, u, :], mv[:, u, 0:1], rstd[:, u:u + 1], ALU.subtract,
                                  ALU.mult).then_inc(xn_r, 1)

            def square_sums(i, u, r):
                dve.wait_ge(sq_r, at(i))
                dve.wait_ge(rs_r, at(i) - U)
                dve.tensor_reduce(ss[:, u, :], sq[:, TWO[u]], AX.X, ALU.add).then_inc(ss_r, 1)

            def low_part(i, u, r):
                dve.wait_ge(h_hi, at(i))
                dve.scalar_tensor_tensor(blk(s.h1[:, :, HID:2 * HID], i), bank(s, HB, BL, 0, HID),
                                         s.dinvN[:, bass.ds(i, 1)], blk(s.h1[:, :, 0:HID], i),
                                         ALU.mult, ALU.subtract).then_inc(h_out, 1)

            def normalise(i, u, r):
                dve.wait_ge(rs_r, at(i))
                dve.wait_ge(acc_r, at(i) - U)
                dve.tensor_tensor(kv[:, u * 2 * HEADS:(u + 1) * 2 * HEADS, 0:HD],
                                  bank(s, KV[u], BL).rearrange("p (h d) -> p h d", d=HD),
                                  bc(rs[:, u, :], HD), ALU.mult).then_inc(kv_r, 1)

            pipelined(dve, (1, norm), (0, statistics), (0, aggregate), (3, low_part), (4, normalise), (3, square_sums))

        @block.gpsimd
        def _(pool):
            start_at(pool, [ve_r, rstd_r, rs_r])

            def one_over_std(i, u, r):
                hold(pool, s.held, (aggr, at(i)))
                pool.tensor_scalar(ve[:, u:u + 1], mv[:, u, 1:2], EPS, None, ALU.add).then_inc(ve_r, 1)
                pool.wait_ge(ve_r, at(i))
                pool.wait_ge(xn_r, at(i) - U)
                pool.tensor_tensor(rstd[:, u:u + 1], ve[:, u:u + 1], s.half[0:BL, 0:1], ALU.pow).then_inc(rstd_r, 1)

            def head_factors(i, u, r):
                pool.wait_ge(ss_r, at(i))
                pool.wait_ge(kv_r, at(i) - U)
                pool.tensor_tensor(rs[:, u, :], ss[:, u, :], s.half[0:BL, 0:1].to_broadcast([BL, 2 * HEADS]),
                                   ALU.pow).then_inc(rs_r, 1)

            pipelined(pool, (0, one_over_std), (3, head_factors))

        @block.scalar
        def _(act):
            start_at(act, [xnT_r, sq_r, h_hi])
            act.wait_ge(sq_set, 1)
            start_at(act, spilled, 16)

            def turned(i, u, r):
                act.wait_ge(tp_r, at(i))
                act.wait_ge(mm_r, at(i) - U)
                act.wait_ge(spilled[u], r * 16 + 16)
                act.activation(xnT[:, u, :], bank(s, TP, 128, 0, KC * BL), ACT.Copy).then_inc(xnT_r, 1)

            def squares(i, u, r):
                act.wait_ge(mm_r, at(i))
                act.wait_ge(ss_r, at(i) - before(TWO, u))
                act.activation(sq[:, TWO[u], :, 0:HD], bank(s, KV[u], BL).rearrange("p (h d) -> p h d", d=HD),
                               ACT.Square).then_inc(sq_r, 1)
                act.activation(blk(s.h1[:, :, 0:HID], i), bank(s, HB, BL, 0, HID), ACT.Copy,
                               scale=s.dinvN[:, bass.ds(i, 1)]).then_inc(h_hi, 1)

            pipelined(act, (1, turned), (2, squares))

        @block.tensor
        def _(pe):
            start_at(pe, [tp_r, mm_r, acc_r])
            acc = bank(s, AC, A1, 0, HEADS * A1)

            def turn(i, u, r):
                pe.wait_ge(xn_r, at(i))
                pe.wait_ge(xnT_r, at(i) - 1)
                for k in range(KC):
                    mm = pe.transpose(bank(s, TP, 128, k * BL, BL), xn[:, u, k * 128:(k + 1) * 128],
                                      s.ident[0:BL, 0:BL])
                mm.then_inc(tp_r, 1)

            def project(i, u, r):
                pe.wait_ge(xnT_r, at(i))
                pe.wait_ge(kv_r, at(i) - U)
                for k in range(KC):
                    pe.matmul(bank(s, KV[u], BL), xnT[:, u, k * BL:(k + 1) * BL], s.Wkv[:, k, :],
                              start=(k == 0), stop=(k == KC - 1))
                pe.wait_ge(h_out, at(i) - 1)
                for k in range(KC):
                    mm = pe.matmul(bank(s, HB, BL, 0, HID), xnT[:, u, k * BL:(k + 1) * BL], s.W1[:, k, :],
                                   start=(k == 0), stop=(k == KC - 1))
                mm.then_inc(mm_r, 1)

            def head_sums(i, u, r):
                pe.wait_ge(kv_r, at(i))
                for h in range(HEADS):
                    mm = pe.matmul(acc[:, h * A1:(h + 1) * A1], kv[:, u * 2 * HEADS + h, :],
                                   kv[:, u * 2 * HEADS + HEADS + h, :],
                                   start=isinstance(i, int) and i == 0 and h == 0,
                                   stop=isinstance(i, int) and i == NB - 1, skip_group_check=True)
                mm.then_inc(acc_r, 1)

            pipelined(pe, (1, turn), (2, project), (4, head_sums))


def attention_out(nc, s):
    with ExitStack() as ctx:
        def sem(name):
            return semaphore(nc, s, "ao_" + name)

        s.used = s.arena_keep
        A1 = HD + 1
        K = take(s, A1, [HEADS * A1])
        KX = take(s, A1, [HEADS * D])
        k_r, kx_mm, kx_r, m_mm, m_r = sem("k"), sem("kxmm"), sem("kx"), sem("mmm"), sem("m")
        block = ctx.enter_context(nc.Block())

        @block.scalar
        def _(act):
            act.activation(K, bank(s, 6, A1, 0, HEADS * A1), ACT.Copy, scale=HD / N).then_inc(k_r, 1)
            act.wait_ge(kx_mm, 1)
            act.activation(KX, s.PS[0:A1, 0:2 * BANK], ACT.Copy).then_inc(kx_r, 1)
            act.wait_ge(m_mm, 1)
            act.activation(s.M[:, :, :].rearrange("p k n -> p (k n)"), bank(s, 2), ACT.Copy).then_inc(m_r, 1)
            act.wait_ge(m_r, 1)

        @block.tensor
        def _(pe):
            pe.wait_ge(k_r, 1)
            for h in range(HEADS):
                mm = pe.matmul(s.PS[0:A1, h * D:(h + 1) * D], K[:, h * A1:(h + 1) * A1], s.X[:, h * D:(h + 1) * D],
                               start=True, stop=True)
            mm.then_inc(kx_mm, 1)
            pe.wait_ge(kx_r, 1)
            for k in range(KC):
                for h in range(HEADS):
                    mm = pe.matmul(bank(s, 2, 128, k * D, D), KX[:, h * D + k * 128:h * D + (k + 1) * 128],
                                   s.Y[:, h * D:(h + 1) * D], start=(h == 0), stop=(h == HEADS - 1))
            mm.then_inc(m_mm, 1)


def build_and_convolve(nc, s):
    with ExitStack() as ctx:
        def sem(name):
            return semaphore(nc, s, "bc_" + name)

        hots = s.aggT[:, :].bitcast(F16).rearrange("p (k g c w) -> p k g c w", k=2, g=GROUPS, w=W)
        z = view(s.tail[0:BL, 0:2 * HID], [2, HID])
        hot, used, copied, conv = sem("hot"), sem("used"), sem("copied"), sem("conv")
        biased, scaled, hi_r, lo_r = sem("biased"), sem("scaled"), sem("hi"), sem("lo")
        NCH = len(CH)
        START = [sum(CH[:c]) for c in range(NCH)]
        CONV = 7
        block = ctx.enter_context(nc.Block())

        def turns(eng, turn):
            turn(0, 0, build=True)
            turn(1, 1, build=True)
            turn(2, 0, build=True, convolve=True)
            turn(3, 1, build=True, convolve=True, scale=True)
            with eng.Fori(2, NB // 2) as r:
                turn(2 * r, 0, build=True, convolve=True, scale=True, split=True)
                turn(2 * r + 1, 1, build=True, convolve=True, scale=True, split=True)
            turn(NB - 1, 0, build=True, convolve=True, scale=True, split=True)
            turn(NB, 1, convolve=True, scale=True, split=True)
            turn(NB + 1, 0, convolve=True, scale=True, split=True)
            turn(NB + 2, 1, scale=True, split=True)
            turn(NB + 3, 0, split=True)

        @block.vector
        def _(dve):
            covered = dve.value_load(s.flag[0:1, 0:1])
            with dve.If(covered == E):
                start_at(dve, [used], WB)
                start_at(dve, [biased], 1)
                start_at(dve, [lo_r], 2)

                def turn(t, odd, build=False, convolve=False, scale=False, split=False):
                    for g in range(GROUPS):
                        if build:
                            k = t * WB + g * W
                            dve.wait_ge(used, k + W)
                            dve.tensor_tensor(hots[:, 0, g], s.iotaW[:, :, :],
                                              s.loT[:, bass.ds(k, W)].unsqueeze(1).to_broadcast([128, BL, W]), ALU.is_equal)
                            dve.tensor_tensor(hots[:, 1, g], s.iotaW[:, :, :],
                                              s.keyT[:, bass.ds(k, W)].unsqueeze(1).to_broadcast([128, BL, W]),
                                              ALU.is_equal).then_inc(hot, 1)
                        if split and g == 0:
                            dve.wait_ge(hi_r, t - 3)
                            dve.tensor_tensor(blk(s.h2[:, :, HID:2 * HID], t - 4), z[:, odd], blk(s.h2[:, :, 0:HID], t - 4),
                                              ALU.subtract).then_inc(lo_r, 1)
                        if scale and g == 2:
                            dve.wait_ge(lo_r, t - 2)
                            dve.wait_ge(conv, t - 2)
                            dve.scalar_tensor_tensor(z[:, 1 - odd], bank(s, CONV, BL, 0, HID), s.dinvN[:, bass.ds(t - 3, 1)],
                                                     s.sb1[:, :], ALU.mult, ALU.add).then_inc(biased, 1)

                turns(dve, turn)
                dve.wait_ge(lo_r, NB + 2)
            dve.end_ifs()

        @block.scalar
        def _(act):
            covered = act.value_load(s.flag[0:1, 0:1])
            with act.If(covered == E):
                start_at(act, [copied], NCH)

                def turn(t, odd, build=False, convolve=False, scale=False, split=False):
                    for c in range(NCH):
                        if build:
                            act.wait_ge(used, t * WB + START[c] + CH[c] + WB)
                            src = bank(s, c, BL, 0, CH[c] * BL).rearrange("p (n h w) -> p h n w", n=CH[c], w=W)
                            dst = s.adj[0:BL, bass.ds(t * N, N)].rearrange("p (h d) -> p h d", d=BL)
                            dst = dst[:, :, START[c] * W:(START[c] + CH[c]) * W].rearrange("p h (n w) -> p h n w", w=W)
                            act.activation(dst, src, ACT.Copy).then_inc(copied, 1)
                        if scale and c == 3:
                            act.wait_ge(biased, t - 1)
                            act.activation(z[:, 1 - odd], z[:, 1 - odd], ACT.Relu,
                                           scale=s.dinvN[:, bass.ds(t - 3, 1)]).then_inc(scaled, 1)
                        if scale and c == 4:
                            act.wait_ge(scaled, t - 2)
                            act.activation(blk(s.h2[:, :, 0:HID], t - 3), z[:, 1 - odd], ACT.Copy).then_inc(hi_r, 1)

                turns(act, turn)
                act.wait_ge(hi_r, NB)
            act.end_ifs()

        @block.tensor
        def _(pe):
            covered = pe.value_load(s.flag[0:1, 0:1])
            with pe.If(covered == E):
                dst = bank(s, CONV, BL, 0, HID)

                def turn(t, odd, build=False, convolve=False, scale=False, split=False):
                    h = 0
                    for c in range(NCH):
                        if build:
                            pe.wait_ge(copied, t * NCH + c + 1)
                            for n in range(CH[c]):
                                w = START[c] + n
                                if w % W == 0:
                                    pe.wait_ge(hot, t * GROUPS + w // W + 1)
                                pe.matmul(bank(s, c, BL, n * BL, BL), hots[:, 0, w // W, :, w % W],
                                          hots[:, 1, w // W, :, w % W], start=True, stop=True).then_inc(used, 1)
                        if convolve and c == 2:
                            pe.wait_ge(copied, t * NCH)
                            pe.wait_ge(biased, t - 1)
                        if convolve:
                            while h * (NCH - 2) < (c - 1) * NB:
                                for p in range(2):
                                    pe.matmul(dst, s.adj[0:BL, bass.ds((t - 2) * N + h * BL, BL)],
                                              s.h1[:, h, p * HID:(p + 1) * HID], start=(h == 0 and p == 0), stop=False,
                                              skip_group_check=True)
                                h += 1
                    if convolve:
                        for p in range(2):
                            mm = pe.matmul(dst, s.ident16[0:BL, 0:BL], blk(s.h1[:, :, p * HID:(p + 1) * HID], t - 2),
                                           start=False, stop=(p == 1), skip_group_check=True)
                        mm.then_inc(conv, 1)

                turns(pe, turn)
            pe.end_ifs()


def convolve_again(nc, s):
    t = s.t
    with ExitStack() as ctx:
        def sem(name):
            return semaphore(nc, s, "ca_" + name)

        conv, scaled, rows_mm, rows_kept = sem("conv"), sem("scaled"), sem("rows_mm"), sem("rows_kept")
        adj = s.adj[0:BL, 0:NB * N].rearrange("p (j h d) -> p j h d", j=NB, d=BL)
        s.Wc = view(s.tail[:, 0:KC * INNER], [KC, INNER])
        s.biasC = s.tail[0:BL, KC * INNER:(KC + 1) * INNER]
        tmpb = s.tail[0:BL, (KC + 1) * INNER:(KC + 2) * INNER]
        temp = s.tail[:, (KC + 2) * INNER:(KC + 2) * INNER + FH]
        rtemp = s.tail[:, (KC + 2) * INNER + FH:(KC + 2) * INNER + 2 * FH]
        free = s.h1_flat[:, :].bitcast(F32)
        a = FH * D
        WxT = view(free[0:G, 0:a], [FH, D])
        Wsl = free[0:G, a:a + G]
        bslB = free[:, a + G:a + 2 * G]
        bx = free[0:G, a + 2 * G:a + 2 * G + FH]
        a += 2 * G + FH
        bxB = view(free[0:G, a:a + FH * BL], [FH, BL])
        loads = [
            ("WxT", WxT, t["WxT"].rearrange("(h c) n -> c h n", c=G)),
            ("Wsl", Wsl, t["W_slice"]),
            ("bx", bx, t["bxT"]),
            ("bsl", bslB, t["b_slice"].partition_broadcast(BL)),
            ("temp", temp, t["temp"].partition_broadcast(128)),
        ]
        got = {name: sem("in_" + name) for name, _, _ in loads}
        step, spread, logits, biases, made = sem("step"), sem("spread"), sem("logits"), sem("biases"), sem("made")
        block = ctx.enter_context(nc.Block())

        def heads(ap):
            return ap.rearrange("p (h g) -> p h g", g=G)

        @block.sync
        def _(sp):
            for name, dst, src in loads:
                sp.dma_start(dst, src).then_inc(got[name], 16)

        @block.gpsimd
        def _(pool):
            chain = [0]

            def link(ins):
                chain[0] += 1
                ins.then_inc(step, 1)
                pool.wait_ge(step, chain[0])

            pool.wait_ge(got["temp"], 16)
            link(pool.tensor_scalar(temp, temp, 0.1, 5.0, ALU.max, ALU.min))
            pool.wait_ge(got["bx"], 16)
            pool.tensor_copy(bxB, bc(bx, BL)).then_inc(spread, 1)

        @block.vector
        def _(dve):
            covered = dve.value_load(s.flag[0:1, 0:1])
            with dve.If(covered == E):
                start_at(dve, [scaled], 2)

                def scale(c, b, n):
                    dve.wait_ge(conv, c + 1)
                    dve.wait_ge(rows_kept, c + 1)
                    v = s.aggT[:, bass.ds(c * 4 * BL, n * BL)]
                    dve.scalar_tensor_tensor(v, bank(s, b, 128, 0, n * BL), s.inv_s[:, 0:1], v, ALU.mult,
                                             ALU.mult).then_inc(scaled, 1)

                with dve.Fori(0, 3) as r:
                    scale(2 * r, 0, 4)
                    scale(2 * r + 1, 1, 4)
                scale(6, 0, 1)
                dve.wait_ge(scaled, 9)
            dve.end_ifs()
            dve.wait_ge(spread, 1)
            dve.reciprocal(rtemp, temp).then_inc(made, 1)
            dve.wait_ge(made, 1)
            dve.wait_ge(logits, 1)
            for k in range(KC):
                dve.tensor_tensor(heads(s.Wc[:, k, :]), heads(bank(s, 4 + k)), bc(rtemp, G), ALU.mult).then_inc(made, 1)
            dve.wait_ge(biases, 1)
            dve.wait_ge(got["bsl"], 16)
            dve.tensor_tensor(heads(tmpb), heads(bank(s, 6, BL)), bslB.unsqueeze(1).to_broadcast([BL, FH, G]),
                              ALU.add).then_inc(made, 1)
            dve.wait_ge(made, 4)
            dve.tensor_tensor(heads(s.biasC), heads(tmpb), bc(rtemp[0:BL, :], G), ALU.mult).then_inc(made, 1)
            dve.wait_ge(made, 5)

        @block.scalar
        def _(act):
            covered = act.value_load(s.flag[0:1, 0:1])
            with act.If(covered == E):
                for c in range(7):
                    act.wait_ge(rows_mm, c + 1)
                    n = min(4, NB - 4 * c) * BL
                    act.activation(s.aggT[:, c * 4 * BL:c * 4 * BL + n], bank(s, 2 + c % 6, 128, 0, n),
                                   ACT.Copy).then_inc(rows_kept, 1)
            act.end_ifs()

        @block.tensor
        def _(pe):
            covered = pe.value_load(s.flag[0:1, 0:1])
            with pe.If(covered == E):
                for j in range(NB):
                    if j == NB - 1:
                        pe.wait_ge(rows_kept, 1)
                    mm = pe.transpose(bank(s, 2 + j // 4 % 6, 128, j % 4 * BL, BL), s.dinvN[:, j:j + 1].to_broadcast([BL, 128]),
                                      s.ident[0:BL, 0:BL])
                    if j % 4 == 3 or j == NB - 1:
                        mm.then_inc(rows_mm, 1)

                def sums(c, b, n):
                    pe.wait_ge(scaled, c + 1)
                    for h in range(NB):
                        rhs = adj[:, bass.ds(c * 4, n), h, :] if n > 1 else s.adj[0:BL, (4 * c) * N + h * BL:
                                                                                 (4 * c) * N + (h + 1) * BL]
                        for p in range(2):
                            pe.matmul(bank(s, b, 128, 0, n * BL), s.h2[:, h, p * HID:(p + 1) * HID], rhs,
                                      start=(h == 0 and p == 0), stop=False, skip_group_check=True)
                    for k in range(n):
                        for p in range(2):
                            mm = pe.matmul(bank(s, b, 128, k * BL, BL), blk(s.h2[:, :, p * HID:(p + 1) * HID], c * 4 + k),
                                           s.ident16[0:BL, 0:BL], start=False, stop=(k == n - 1 and p == 1),
                                           skip_group_check=True)
                    mm.then_inc(conv, 1)

                with pe.Fori(0, 3) as r:
                    sums(2 * r, 0, 4)
                    sums(2 * r + 1, 1, 4)
                sums(6, 0, 1)
                pe.wait_ge(rows_kept, 7)
            pe.end_ifs()
            pe.wait_ge(got["WxT"], 16)
            pe.wait_ge(got["Wsl"], 16)
            for k in range(KC):
                for h in range(FH):
                    mm = pe.matmul(bank(s, 4 + k, 128, h * G, G), WxT[:, h, k * 128:(k + 1) * 128], Wsl,
                                   start=True, stop=True)
            mm.then_inc(logits, 1)
            pe.wait_ge(spread, 1)
            for h in range(FH):
                mm = pe.matmul(bank(s, 6, BL, h * G, G), bxB[:, h, :], Wsl, start=True, stop=True)
            mm.then_inc(biases, 1)


def general(nc, s):
    t = s.t
    with ExitStack() as ctx:
        def sem(name):
            return semaphore(nc, s, "ge_" + name)

        s.used = 0
        src = take(s, 128, [GC], I32)
        dst_i = take(s, 128, [GC], I32)
        dst = take(s, 128, [GC])
        iota_i = take(s, 128, [N], I32)
        iota = take(s, 128, [N])
        hot = take(s, 128, [N])
        idx = take(s, 128, [1], I32)
        got = take(s, 128, [HID])
        ratio = take(s, BL, [NB])
        dinv = take(s, BL, [NB])
        rowsT = take(s, 128, [N])
        table = take(s, BL, [NB, HID])
        zeros = take(s, 128, [128])
        CN = [(c * 500, min(500, N - c * 500)) for c in range(7)]
        in_s, iota_r, step, idx_r, got_r = sem("in"), sem("iota"), sem("step"), sem("idx"), sem("got")
        hot_r, mm_r, sums_r, pow_r, cols_r = sem("hot"), sem("mm"), sem("sums"), sem("pow"), sem("cols")
        rows_r, tr_r, table_r, table_d, read, ready = (sem(x) for x in ("rows", "tr", "table", "tabled", "read", "ready"))
        block = ctx.enter_context(nc.Block())

        @block.sync
        def _(sp):
            covered = sp.value_load(s.flag[0:1, 0:1])
            with sp.If(covered != E):
                sp.dma_start(src, t["src_all"]).then_inc(in_s, 16)
                sp.wait_ge(in_s, 16)
                sp.dma_start(dst_i, t["dst_all"]).then_inc(in_s, 16)
                for p in range(2):
                    sp.wait_ge(table_r, p + 1)
                    sp.dma_start(s.table_d.rearrange("(b p) c -> p b c", p=BL), table).then_inc(table_d, 16)
                sp.wait_ge(table_d, 32)
            sp.end_ifs()

        @block.gpsimd
        def _(pool):
            covered = pool.value_load(s.flag[0:1, 0:1])
            with pool.If(covered != E):
                pool.iota(iota_i, pattern=[[1, N]], base=0, channel_multiplier=0).then_inc(iota_r, 1)
                pool.wait_ge(sums_r, 1)
                pool.tensor_tensor(s.aggT[:, :], s.aggT[:, :], s.half[:, 0:1].to_broadcast([128, N]),
                                   ALU.pow).then_inc(pow_r, 1)
                for p in range(2):
                    pool.wait_ge(table_d, 16 * (p + 1))
                    with pool.Fori(0, GC) as c:
                        pool.wait_ge(mm_r, c + 1 + (p + 1) * (GC + 1))
                        pool.tensor_copy(idx, src[:, bass.ds(c, 1)]).then_inc(idx_r, 1)
                        hold(pool, s.held, (idx_r, c + 1 + p * GC))
                        pool.indirect_dma_start(out=got, out_offset=None, in_=s.table_d,
                                                in_offset=bass.IndirectOffsetOnAxis(ap=idx, axis=0)
                                                ).then_inc(got_r, 16)
                        pool.wait_ge(got_r, 16 * (c + 1 + p * GC))
            pool.end_ifs()

        @block.vector
        def _(dve):
            covered = dve.value_load(s.flag[0:1, 0:1])
            with dve.If(covered != E):
                chain = [0]

                def link(ins):
                    chain[0] += 1
                    ins.then_inc(step, 1)
                    dve.wait_ge(step, chain[0])

                dve.wait_ge(in_s, 32)
                dve.wait_ge(iota_r, 1)
                link(dve.tensor_copy(dst, dst_i))
                link(dve.memset(zeros, 0.0))
                link(dve.tensor_copy(iota, iota_i))
                dve.sem_inc(ready, 1)
                for p in range(3):
                    with dve.Fori(0, GC) as c:
                        dve.wait_ge(mm_r, c + 1 + p * (GC + 1))
                        dve.tensor_scalar(hot, iota, dst[:, bass.ds(c, 1)], None, ALU.is_equal).then_inc(hot_r, 1)
                    dve.wait_ge(mm_r, (p + 1) * (GC + 1))
                    if p == 0:
                        for c, (a, n) in enumerate(CN):
                            link(dve.tensor_copy(s.aggT[:, a:a + n], bank(s, c, 128, 0, n)))
                        dve.sem_inc(sums_r, 1)
                        dve.wait_ge(cols_r, 1)
                        link(dve.tensor_copy(dinv, bank(s, 7, BL, 0, NB)))
                        link(dve.reciprocal(ratio, s.dinvN[:, :]))
                        link(dve.tensor_tensor(ratio, ratio, dinv, ALU.mult))
                        link(dve.tensor_tensor(table, s.h1[:, :, 0:HID], s.h1[:, :, HID:2 * HID], ALU.add))
                        link(dve.tensor_tensor(table, table, bc(ratio, HID), ALU.mult))
                        dve.sem_inc(table_r, 1)
                        dve.sem_inc(mm_r, 1)
                    if p == 1:
                        for c, (a, n) in enumerate(CN):
                            link(dve.tensor_copy(rowsT[:, a:a + n], bank(s, c, 128, 0, n)))
                        dve.sem_inc(rows_r, 1)
                        dve.wait_ge(table_d, 16)
                        for b in range(NB):
                            dve.wait_ge(tr_r, b + 1)
                            v = table[:, b, :]
                            link(dve.scalar_tensor_tensor(v, bank(s, 7, BL, 0, HID), dinv[:, b:b + 1], s.sb1[:, :],
                                                          ALU.mult, ALU.add))
                            dve.sem_inc(read, 1)
                            link(dve.tensor_scalar(v, v, 0.0, dinv[:, b:b + 1], ALU.max, ALU.mult))
                        dve.sem_inc(table_r, 1)
                        dve.sem_inc(mm_r, 1)
                    if p == 2:
                        for c, (a, n) in enumerate(CN):
                            v = s.aggT[:, a:a + n]
                            link(dve.scalar_tensor_tensor(v, bank(s, c, 128, 0, n), s.inv_s[:, 0:1], v, ALU.mult, ALU.mult))
            dve.end_ifs()

        @block.tensor
        def _(pe):
            covered = pe.value_load(s.flag[0:1, 0:1])
            with pe.If(covered != E):
                pe.wait_ge(ready, 1)
                pe.sem_inc(mm_r, 1)
                for p in range(3):
                    lhsT = s.ones[:, :] if p == 0 else got
                    if p:
                        pe.wait_ge(mm_r, p * (GC + 1) + 1)
                    for c, (a, n) in enumerate(CN):
                        pe.matmul(bank(s, c, 128, 0, n), zeros, iota[:, a:a + n], start=True, stop=False,
                                  skip_group_check=True)
                    with pe.Fori(0, GC) as k:
                        pe.wait_ge(hot_r, k + 1 + p * GC)
                        if p:
                            pe.wait_ge(got_r, 16 * (k + 1 + (p - 1) * GC))
                        for c, (a, n) in enumerate(CN):
                            mm = pe.matmul(bank(s, c, 128, 0, n), lhsT, hot[:, a:a + n], start=False, stop=False,
                                           skip_group_check=True)
                        mm.then_inc(mm_r, 1)
                    if p == 0:
                        pe.wait_ge(pow_r, 1)
                        for b in range(NB):
                            mm = pe.matmul(bank(s, 7, BL, b, 1), s.aggT[0:1, b * BL:(b + 1) * BL], s.ones[0:1, 0:1],
                                           start=True, stop=True)
                        mm.then_inc(cols_r, 1)
                    if p == 1:
                        pe.wait_ge(rows_r, 1)
                        for b in range(NB):
                            if b:
                                pe.wait_ge(read, b)
                            pe.transpose(bank(s, 7, BL, 0, HID), rowsT[:, b * BL:(b + 1) * BL],
                                         s.ident[:, :]).then_inc(tr_r, 1)
            pe.end_ifs()


def slices(nc, s):
    t = s.t
    with ExitStack() as ctx:
        def sem(name):
            return semaphore(nc, s, "sl_" + name)

        s.used = 0
        s.x2 = take(s, BL, [NB, D])
        s.swT = take(s, 128, [NB, INNER // 128 * BL])
        s.wsum = take(s, BL, [INNER])
        s.UT = take(s, 128, [KC, INNER])
        s.keep = s.used
        agg = take(s, 128, [U, BL])
        xnT = take(s, 128, [U, KC * BL])
        x1 = take(s, BL, [U, D])
        W2 = take(s, 128, [D])
        st = take(s, BL, [U, 6])
        mv = take(s, BL, [U, 2])
        ve = take(s, BL, [U])
        rstd = take(s, BL, [U])
        y = take(s, BL, [U, D])
        yT = take(s, 128, [U, KC * BL])
        lg = take(s, BL, [U, INNER])
        mx = take(s, BL, [U, FH])
        sm = take(s, BL, [U, FH])
        rc = take(s, BL, [U, FH])
        G2, TP, LG, UTB, SWT = 0, [1, 2], [3, 4], 5, 7
        names = ("agg", "w2", "x2", "st", "mv", "ve", "rstd", "y", "tp", "yT", "lgmm", "lg", "mx", "sub", "ex", "sm", "rc",
                 "sw", "swt", "swT", "ut", "acc", "xb")
        (agg_r, w2_r, x2_r, st_r, mv_r, ve_r, rstd_r, y_r, tp_r, yT_r, lgmm_r, lg_r, mx_r, sub_r, ex_r, sm_r, rc_r,
         sw_r, swt_r, swT_r, ut_r, acc_r, xb_r) = sems = [sem(x) for x in names]
        loaded, loaded_t, kept = ([sem(f"{x}{u}") for u in range(U)] for x in ("inx", "int", "keep"))
        in_w2 = sem("inw2")
        zeroed, ut_kept = sem("zeroed"), sem("utkept")
        block = ctx.enter_context(nc.Block())

        def heads(ap):
            return ap.rearrange("p (h g) -> p h g", g=G)

        @block.sync
        def _(sp):
            start_at(sp, sems)
            start_at(sp, kept, 16)
            sp.dma_start(W2, t["W2"]).then_inc(in_w2, 16)

            def load(i, u, r):
                sp.wait_ge(kept[u], r * 16 + 16)
                sp.wait_ge(y_r, at(i) - U)
                sp.dma_start(x1[:, u, :], rows(t["x"], i)).then_inc(loaded[u], 16)
                sp.wait_ge(w2_r, at(i) - U)
                sp.dma_start(xnT[:, u, :], s.xnT_d.rearrange("(b p) c -> b p c", p=128)[bass.ds(i, 1)]
                             .rearrange("a p c -> (a p) c")).then_inc(loaded_t[u], 16)

            def keep(i, u, r):
                sp.wait_ge(x2_r, at(i))
                sp.dma_start(blk(s.x2, i), x1[:, u, :]).then_inc(kept[u], 16)

            pipelined(sp, (0, load), (4, keep))
            for u in range(U):
                sp.wait_ge(kept[u], 16 * IT + 16)

        @block.scalar
        def _(act):
            def static(i, u, r):
                act.wait_ge(w2_r, at(i) - U)
                act.activation(agg[:, u, :], s.aggT[:, bass.ds(i * BL, BL)], ACT.Copy).then_inc(agg_r, 1)

            def turned(i, u, r):
                act.wait_ge(tp_r, at(i))
                act.wait_ge(lgmm_r, at(i) - U)
                act.activation(yT[:, u, :], bank(s, TP[TWO[u]], 128, 0, KC * BL), ACT.Copy).then_inc(yT_r, 1)

            def exponent(i, u, r):
                act.wait_ge(sub_r, at(i))
                act.activation(lg[:, u, :], lg[:, u, :], ACT.Exp).then_inc(ex_r, 1)

            def weights_turned(i, u, r):
                act.wait_ge(swt_r, at(i))
                act.activation(blk(s.swT, i), bank(s, SWT, 128, 0, 4 * BL), ACT.Copy).then_inc(swT_r, 1)

            pipelined(act, (0, static), (1, turned), (4, weights_turned), (2, exponent))
            act.wait_ge(acc_r, NB + U)
            act.activation(s.UT.rearrange("p k n -> p (k n)"), s.PS[:, UTB * BANK:(UTB + 2) * BANK],
                           ACT.Copy).then_inc(ut_kept, 1)
            act.wait_ge(ut_kept, 1)

        @block.vector
        def _(dve):
            def residual(i, u, r):
                dve.wait_ge(w2_r, at(i))
                dve.wait_ge(xb_r, at(i))
                dve.tensor_tensor(x1[:, u, :], bank(s, G2, BL, 0, D), x1[:, u, :], ALU.add).then_inc(x2_r, 1)
                dve.wait_ge(x2_r, at(i))
                dve.bn_stats(st[:, u, :], x1[:, u, :]).then_inc(st_r, 1)
                hold(dve, s.held, (st_r, at(i)), (y_r, at(i) - U))
                dve.bn_aggr(mv[:, u, :], st[:, u, :]).then_inc(mv_r, 1)

            def norm(i, u, r):
                dve.wait_ge(rstd_r, at(i))
                dve.wait_ge(acc_r, at(i) - U)
                dve.tensor_scalar(y[:, u, :], x1[:, u, :], mv[:, u, 0:1], rstd[:, u:u + 1], ALU.subtract,
                                  ALU.mult).then_inc(y_r, 1)

            def logits(i, u, r):
                dve.wait_ge(lgmm_r, at(i))
                dve.wait_ge(ut_r, at(i) - U)
                dve.wait_ge(acc_r, at(i) - U)
                dve.wait_ge(swt_r, at(i) - U)
                dve.tensor_tensor(lg[:, u, :], bank(s, LG[TWO[u]], BL), s.biasC[:, :], ALU.add).then_inc(lg_r, 1)
                dve.wait_ge(lg_r, at(i))
                dve.tensor_reduce(mx[:, u, :], heads(lg[:, u, :]), AX.X, ALU.max).then_inc(mx_r, 1)
                dve.wait_ge(mx_r, at(i))
                dve.tensor_tensor(heads(lg[:, u, :]), heads(lg[:, u, :]), bc(mx[:, u, :], G),
                                  ALU.subtract).then_inc(sub_r, 1)

            def weigh(i, u, r):
                dve.wait_ge(ex_r, at(i))
                dve.tensor_reduce(sm[:, u, :], heads(lg[:, u, :]), AX.X, ALU.add).then_inc(sm_r, 1)
                dve.wait_ge(sm_r, at(i))
                dve.reciprocal(rc[:, u, :], sm[:, u, :]).then_inc(rc_r, 1)
                dve.wait_ge(rc_r, at(i))
                dve.tensor_tensor(heads(lg[:, u, :]), heads(lg[:, u, :]), bc(rc[:, u, :], G),
                                  ALU.mult).then_inc(sw_r, 1)

            pipelined(dve, (3, weigh), (1, norm), (2, logits), (0, residual))

        @block.gpsimd
        def _(pool):
            pool.memset(s.wsum, 0.0).then_inc(zeroed, 1)
            pool.wait_ge(zeroed, 1)

            def add_biases(i, u, r):
                pool.wait_ge(loaded[u], r * 16 + 16)
                pool.tensor_tensor(x1[:, u, :], x1[:, u, :], s.bsum[:, :], ALU.add).then_inc(xb_r, 1)

            def one_over_std(i, u, r):
                hold(pool, s.held, (mv_r, at(i)))
                pool.tensor_scalar(ve[:, u:u + 1], mv[:, u, 1:2], EPS, None, ALU.add).then_inc(ve_r, 1)
                pool.wait_ge(ve_r, at(i))
                pool.wait_ge(y_r, at(i) - U)
                pool.tensor_tensor(rstd[:, u:u + 1], ve[:, u:u + 1], s.half[0:BL, 0:1], ALU.pow).then_inc(rstd_r, 1)

            def total(i, u, r):
                pool.wait_ge(sw_r, at(i))
                pool.wait_ge(ut_r, at(i) - 1)
                pool.tensor_tensor(s.wsum, s.wsum, lg[:, u, :], ALU.add).then_inc(ut_r, 1)

            pipelined(pool, (1, one_over_std), (0, add_biases), (4, total))

        @block.tensor
        def _(pe):
            pe.wait_ge(in_w2, 16)

            def gcn_out(i, u, r):
                pe.wait_ge(agg_r, at(i))
                pe.wait_ge(x2_r, at(i) - 1)
                pe.wait_ge(loaded_t[u], r * 16 + 16)
                for k in range(KC):
                    pe.matmul(bank(s, G2, BL, 0, D), xnT[:, u, k * BL:(k + 1) * BL], s.M[:, k, :], start=(k == 0),
                              stop=False)
                pe.matmul(bank(s, G2, BL, 0, D), agg[:, u, :], W2, start=False, stop=True).then_inc(w2_r, 1)

            def turn(i, u, r):
                pe.wait_ge(y_r, at(i))
                pe.wait_ge(yT_r, at(i) - before(TWO, u))
                for k in range(KC):
                    mm = pe.transpose(bank(s, TP[TWO[u]], 128, k * BL, BL), y[:, u, k * 128:(k + 1) * 128],
                                      s.ident[0:BL, 0:BL])
                mm.then_inc(tp_r, 1)

            def logits(i, u, r):
                pe.wait_ge(yT_r, at(i))
                pe.wait_ge(lg_r, at(i) - before(TWO, u))
                for k in range(KC):
                    mm = pe.matmul(bank(s, LG[TWO[u]], BL), yT[:, u, k * BL:(k + 1) * BL], s.Wc[:, k, :],
                                   start=(k == 0), stop=(k == KC - 1))
                mm.then_inc(lgmm_r, 1)

            def sums(i, u, r):
                pe.wait_ge(sw_r, at(i))
                pe.wait_ge(swT_r, at(i) - 1)
                for c in range(4):
                    mm = pe.transpose(bank(s, SWT, 128, c * BL, BL), lg[:, u, c * 128:(c + 1) * 128],
                                      s.ident[0:BL, 0:BL])
                mm.then_inc(swt_r, 1)
                for k in range(KC):
                    mm = pe.matmul(bank(s, UTB + k), y[:, u, k * 128:(k + 1) * 128], lg[:, u, :],
                                   start=isinstance(i, int) and i == 0, stop=isinstance(i, int) and i == NB - 1,
                                   skip_group_check=True)
                mm.then_inc(acc_r, 1)

            pipelined(pe, (2, logits), (1, turn), (0, gcn_out), (4, sums))


def tokens(nc, s):
    t = s.t
    with ExitStack() as ctx:
        def sem(name):
            return semaphore(nc, s, "to_" + name)

        s.used = s.keep
        s.T = take(s, 128, [4, D])
        s.keep = s.used
        Wfx = take(s, 128, [KC, INNER])
        Wq, Wk, Wv = (take(s, G, [G]) for _ in range(3))
        Wout = take(s, G, [FH, D])
        bfx = take(s, G, [FH])
        nrm = take(s, G, [INNER])
        rn = take(s, G, [INNER])
        tok = take(s, G, [INNER])
        qT, kT, vT = (take(s, G, [INNER]) for _ in range(3))
        sc = take(s, G, [INNER])
        mx = take(s, G, [FH])
        sm = take(s, G, [FH])
        aT = take(s, G, [INNER])
        vW = take(s, G, [FH * D])
        Th = take(s, G, [FH, D])
        loads = [("fx", Wfx, t["W_fx"].rearrange("(k p) n -> p k n", p=128)), ("q", Wq, t["W_q"]), ("k", Wk, t["W_k"]),
                 ("v", Wv, t["W_v"]), ("out", Wout, t["W_out"].rearrange("(h c) n -> c h n", c=G)), ("bfx", bfx, t["bfxT"])]
        got = {n: sem("in" + n) for n, _, _ in loads}
        step, tok_r, qkv_r, ex_r, attn_r, aT_r, vW_r, Th_r = (sem(x) for x in ("s", "tok", "qkv", "ex", "at", "aT", "vW", "Th"))
        m_n, m_t, m_q, m_s, m_a, m_v, m_T, moved = (sem(x) for x in ("mn", "mt", "mq", "ms", "ma", "mv", "mT", "moved"))
        sub_r = sem("sub")
        block = ctx.enter_context(nc.Block())

        def heads(ap):
            return ap.rearrange("p (h g) -> p h g", g=G)

        @block.sync
        def _(sp):
            for n, d, src in loads:
                sp.dma_start(d, src).then_inc(got[n], 16)
            sp.wait_ge(Th_r, 1)
            pairs = Th.rearrange("p (c a) n -> p a c n", a=2)
            for a in range(2):
                sp.dma_start(s.T[a * G:(a + 1) * G, :, :], pairs[:, a, :, :]).then_inc(moved, 16)
            sp.wait_ge(moved, 32)

        @block.vector
        def _(dve):
            chain = [0]

            def link(ins):
                chain[0] += 1
                ins.then_inc(step, 1)
                dve.wait_ge(step, chain[0])

            dve.wait_ge(m_n, 1)
            link(dve.tensor_scalar(rn, bank(s, 0, G), EPS, None, ALU.add))
            link(dve.reciprocal(rn, rn))
            dve.wait_ge(got["bfx"], 16)
            link(dve.tensor_tensor(heads(nrm), heads(bank(s, 0, G)), bc(bfx, G), ALU.mult))
            dve.wait_ge(m_t, 1)
            link(dve.tensor_tensor(nrm, nrm, bank(s, 1, G), ALU.add))
            dve.tensor_tensor(tok, nrm, rn, ALU.mult).then_inc(tok_r, 1)
            dve.wait_ge(m_q, 1)
            for n, d in enumerate((qT, kT, vT)):
                link(dve.tensor_copy(d, bank(s, 2 + n, G)))
            dve.sem_inc(qkv_r, 1)
            dve.wait_ge(m_s, 1)
            link(dve.tensor_scalar(sc, bank(s, 5, G), G ** -0.5, None, ALU.mult))
            link(dve.tensor_reduce(mx, heads(sc), AX.X, ALU.max))
            dve.tensor_tensor(heads(sc), heads(sc), bc(mx, G), ALU.subtract).then_inc(sub_r, 1)
            dve.wait_ge(ex_r, 1)
            link(dve.tensor_reduce(sm, heads(sc), AX.X, ALU.add))
            link(dve.reciprocal(mx, sm))
            dve.tensor_tensor(heads(sc), heads(sc), bc(mx, G), ALU.mult).then_inc(attn_r, 1)
            dve.wait_ge(m_a, 1)
            dve.tensor_copy(aT, bank(s, 6, G)).then_inc(aT_r, 1)

        @block.scalar
        def _(act):
            act.wait_ge(sub_r, 1)
            act.activation(sc, sc, ACT.Exp).then_inc(ex_r, 1)
            act.wait_ge(m_v, 1)
            act.activation(vW, s.PS[0:G, 0:4 * BANK], ACT.Copy).then_inc(vW_r, 1)
            act.wait_ge(m_T, 1)
            act.activation(Th.rearrange("p h n -> p (h n)"), s.PS[0:G, 0:4 * BANK], ACT.Copy).then_inc(Th_r, 1)

        @block.tensor
        def _(pe):
            pe.matmul(bank(s, 0, G), s.ones[0:BL, 0:G], s.wsum, start=True, stop=True).then_inc(m_n, 1)
            pe.wait_ge(got["fx"], 16)
            for h in range(FH):
                for k in range(KC):
                    mm = pe.matmul(bank(s, 1, G, h * G, G), Wfx[:, k, h * G:(h + 1) * G], s.UT[:, k, h * G:(h + 1) * G],
                                   start=(k == 0), stop=(k == KC - 1))
            mm.then_inc(m_t, 1)
            pe.wait_ge(tok_r, 1)
            for n, (w, m) in enumerate((("q", Wq), ("k", Wk), ("v", Wv))):
                pe.wait_ge(got[w], 16)
                mm = pe.matmul(bank(s, 2 + n, G), m, tok, start=True, stop=True)
            mm.then_inc(m_q, 1)
            pe.wait_ge(qkv_r, 1)
            for h in range(FH):
                mm = pe.matmul(bank(s, 5, G, h * G, G), qT[:, h * G:(h + 1) * G], kT[:, h * G:(h + 1) * G],
                               start=True, stop=True)
            mm.then_inc(m_s, 1)
            pe.wait_ge(got["out"], 16)
            for h in range(FH):
                mm = pe.matmul(s.PS[0:G, h * D:(h + 1) * D], vT[:, h * G:(h + 1) * G], Wout[:, h, :],
                               start=True, stop=True)
            mm.then_inc(m_v, 1)
            pe.wait_ge(attn_r, 1)
            for h in range(FH):
                mm = pe.transpose(bank(s, 6, G, h * G, G), sc[:, h * G:(h + 1) * G], s.ident[0:G, 0:G])
            mm.then_inc(m_a, 1)
            pe.wait_ge(aT_r, 1)
            pe.wait_ge(vW_r, 1)
            for h in range(FH):
                mm = pe.matmul(s.PS[0:G, h * D:(h + 1) * D], aT[:, h * G:(h + 1) * G], vW[:, h * D:(h + 1) * D],
                               start=True, stop=True)
            mm.then_inc(m_T, 1)


def output(nc, s):
    with ExitStack() as ctx:
        def sem(name):
            return semaphore(nc, s, "ou_" + name)

        s.used = s.keep
        sw = take(s, 128, [U, 4 * BL])
        o = take(s, BL, [U, D])
        bout = take(s, BL, [D])
        in_b = sem("bout")
        OB = [0, 1]
        mm_r, o_r, xb_r = sem("mm"), sem("o"), sem("xb")
        moved, sent = [sem(f"m{u}") for u in range(U)], [sem(f"s{u}") for u in range(U)]
        block = ctx.enter_context(nc.Block())

        @block.sync
        def _(sp):
            start_at(sp, [mm_r, o_r, xb_r])
            sp.dma_start(bout, s.t["b_out"].partition_broadcast(BL)).then_inc(in_b, 16)
            start_at(sp, sent, 16)

            def static(i, u, r):
                sp.wait_ge(mm_r, at(i) - U)
                sp.dma_start(sw[:, u, :], blk(s.swT, i)).then_inc(moved[u], 16)

            pipelined(sp, (0, static))

        @block.gpsimd
        def _(pool):
            pool.wait_ge(in_b, 16)

            def add_bias(i, u, r):
                pool.tensor_tensor(blk(s.x2, i), blk(s.x2, i), bout, ALU.add).then_inc(xb_r, 1)

            pipelined(pool, (0, add_bias))

        @block.scalar
        def _(act):
            def send(i, u, r):
                act.wait_ge(o_r, at(i))
                act.dma_start(rows(s.out, i), o[:, u, :]).then_inc(sent[u], 16)

            pipelined(act, (0, send))
            for u in range(U):
                act.wait_ge(sent[u], 16 * IT + 16)

        @block.vector
        def _(dve):
            def add(i, u, r):
                dve.wait_ge(mm_r, at(i))
                dve.wait_ge(xb_r, at(i))
                dve.wait_ge(sent[u], r * 16 + 16)
                dve.tensor_tensor(o[:, u, :], bank(s, OB[TWO[u]], BL, 0, D), blk(s.x2, i), ALU.add).then_inc(o_r, 1)

            pipelined(dve, (0, add))

        @block.tensor
        def _(pe):
            def mix(i, u, r):
                pe.wait_ge(moved[u], r * 16 + 16)
                pe.wait_ge(o_r, at(i) - before(TWO, u))
                for c in range(4):
                    mm = pe.matmul(bank(s, OB[TWO[u]], BL, 0, D), sw[:, u, c * BL:(c + 1) * BL], s.T[:, c, :],
                                   start=(c == 0), stop=(c == 3))
                mm.then_inc(mm_r, 1)

            pipelined(pe, (0, mix))


def kernel(x, src, dst, L0_gnn_W1, L0_gnn_b1, L0_gnn_W2, L0_gnn_b2, L0_mix_wq, L0_mix_wk, L0_mix_wv, L0_mix_wo, L0_mix_bo,
           L0_mix_ln_k_g, L0_mix_ln_k_b, L0_mix_ln_v_g, L0_mix_ln_v_b, L0_ffn_W_fx, L0_ffn_b_fx, L0_ffn_W_x, L0_ffn_b_x,
           L0_ffn_W_slice, L0_ffn_b_slice, L0_ffn_W_q, L0_ffn_W_k, L0_ffn_W_v, L0_ffn_W_out, L0_ffn_b_out,
           L0_ffn_temperature):
    import numpy as np
    import concourse.bacc as bacc
    from concourse.bass_utils import run_bass_kernel_spmd

    src, dst = np.asarray(src), np.asarray(dst)
    loops = np.arange(N, dtype=src.dtype)
    pad = np.zeros(GE - E - N, dtype=src.dtype)
    laid = {
        "x": x, "dst": dst,
        "edges": np.stack([src, dst], axis=1).reshape(-1),
        "firsts": dst[::BL],
        "src_all": np.concatenate([src, loops, pad]).reshape(128, GC),
        "dst_all": np.concatenate([dst, loops, pad - 1]).reshape(128, GC),
        "W1": L0_gnn_W1, "b1": L0_gnn_b1, "W2": L0_gnn_W2, "b2": L0_gnn_b2,
        "wq": L0_mix_wq, "wkvT": np.concatenate([np.asarray(L0_mix_wk).T, np.asarray(L0_mix_wv).T], axis=1),
        "woT": np.asarray(L0_mix_wo).T, "bo": L0_mix_bo,
        "ln": np.stack([L0_mix_ln_k_g, L0_mix_ln_k_b, L0_mix_ln_v_g, L0_mix_ln_v_b], axis=1),
        "W_fx": L0_ffn_W_fx, "bfxT": np.asarray(L0_ffn_b_fx).reshape(FH, G).T, "WxT": np.asarray(L0_ffn_W_x).T,
        "bxT": np.asarray(L0_ffn_b_x).reshape(FH, G).T, "W_slice": L0_ffn_W_slice, "b_slice": L0_ffn_b_slice,
        "W_q": L0_ffn_W_q, "W_k": L0_ffn_W_k, "W_v": L0_ffn_W_v, "W_out": L0_ffn_W_out, "b_out": L0_ffn_b_out,
        "temp": np.asarray(L0_ffn_temperature).reshape(FH),
    }
    nc = bacc.Bacc("TRN2", target_bir_lowering=False, num_devices=1)
    arrays, t = {}, {}
    for name, a in laid.items():
        a = np.ascontiguousarray(a)
        arrays["in_" + name] = a
        t[name] = nc.dram_tensor("in_" + name, a.shape, mybir.dt.from_np(a.dtype), kind="ExternalInput").ap()
    out = nc.dram_tensor("out_0", (N, D), F32, kind="ExternalOutput").ap()
    build(nc, t, out)
    return run_bass_kernel_spmd(nc, [arrays], core_ids=[0]).results[0]["out_0"]
```

```python
import concourse.bass as bass
from concourse import mybir
from contextlib import ExitStack

F32 = mybir.dt.float32
F16 = mybir.dt.float16
I32 = mybir.dt.int32
ALU = mybir.AluOpType
ACT = mybir.ActivationFunctionType
AX = mybir.AxisListType

N = 3125
E = 50000
D = 256
HID = 128
BL = 125
NB = N // BL
U = 5
IT = NB // U
KC = D // 128
W = 5
NW = N // W
WB = BL // W
NQ = NW // BL
SLOTS = 128
HEADS, HD = 4, 64
FH, G = 8, 64
INNER = FH * G
BANK = 512
EPS = 1e-5
ROUND = 12582912.0
LIMIT = 16384.0
Y_SCALE = 1024.0
SW_SCALE = 16384.0
CH = [4, 4, 4, 4, 3, 3, 3]
GROUPS = WB // W
TAIL = (KC + 2) * INNER + 2 * FH
GE = 416 * 128
GC = GE // 128


TWO = [0, 1, 0, 1, 0]


def at(i):
    return i + 1 + U


def semaphore(nc, s, name):
    s.phase_semaphores.append(nc.alloc_semaphore(name=name))
    return s.phase_semaphores[-1]


def hold(eng, held, *waits):
    for sem, value in waits:
        eng.wait_ge(sem, value)
    eng.sem_inc(held, 1)


def start_at(eng, sems, n=U):
    for x in sems:
        eng.sem_inc(x, n)


def pipelined(eng, *steps, last=None):
    assert max(lag for lag, _ in steps) < U
    for t in range(U):
        for lag, f in steps:
            if t >= lag:
                f(t - lag, (t - lag) % U, (t - lag) // U)
    with eng.Fori(1, IT) as it:
        for u in range(U):
            for lag, f in steps:
                f(it * U + (u - lag), (u - lag) % U, it + (u - lag) // U)
    for t in range(NB, NB + max(lag for lag, _ in steps)):
        for lag, f in last or steps:
            if t - lag < NB:
                f(t - lag, (t - lag) % U, (t - lag) // U)


def before(slots, u):
    n = len(slots)
    d = 1
    while slots[(u - d) % n] != slots[u]:
        d += 1
    return d


def bc(ap, n):
    return ap.unsqueeze(2).to_broadcast([ap.shape[0], ap.shape[1], n])


def blk(ap, i):
    return ap[:, bass.ds(i, 1), :].rearrange("p a c -> p (a c)")


def rows(dram, i):
    return dram.rearrange("(b p) c -> b p c", p=BL)[bass.ds(i, 1)].rearrange("a p c -> (a p) c")


class Store:
    pass


def build(nc, t, out):
    with ExitStack() as ctx:
        s = Store()
        s.t, s.out = t, out

        def sb(name, shape, dt=F32):
            return ctx.enter_context(nc.sbuf_tensor(name, shape, dt))

        def dram(name, shape, dt=F32):
            return nc.dram_tensor(name, shape, dt, kind="Internal").ap()

        s.xnT_d = dram("xnT_spill", (NB * 128, KC * BL))
        s.table_d = dram("table_spill", (N, HID))
        s.adj = sb("adj", [128, NB * N + 1], F16)
        s.h1_flat = sb("h1_parts", [BL, NB * 2 * HID], F16)
        s.h1 = s.h1_flat[:, :].rearrange("p (b c) -> p b c", b=NB)
        s.h2 = sb("h2_parts", [BL, NB, 2 * HID], F16)
        s.aggT = sb("agg_rows", [128, N])
        s.dinvN = sb("dinv_cols", [BL, NB])
        s.keyT = sb("keyT", [128, NW], F16)
        s.loT = sb("loT", [128, NW], F16)
        s.flag = sb("covered", [128, 1], I32)
        s.ident = sb("ident", [128, 128])
        s.ones = sb("ones", [128, 128])
        s.half = sb("minus_half", [128, 1])
        s.plus = sb("plus_half", [128, 1])
        s.ident16 = sb("ident16", [128, 128], F16)
        s.iotaW = sb("iotaW", [128, BL, W], F16)
        s.sb1 = sb("scaled_b1", [BL, HID])
        s.inv_s = sb("inv_scale", [128, 1])
        s.M = sb("M", [128, KC, D])
        s.bsum = sb("b2_bo", [BL, D])
        s.tail = sb("tail", [128, TAIL])
        s.PS = ctx.enter_context(nc.psum_tensor("PS", [128, 8 * BANK], F32))
        s.held = ctx.enter_context(nc.semaphore("held"))
        s.arena = s.adj[:, :].bitcast(F32)
        s.used = 0

        for phase in (prepare, attention_stats, build_and_convolve, general,
                      convolve_again, slices, tokens_and_output):
            s.phase_semaphores = []
            phase(nc, s)
            nc.clear_and_free_semaphores(s.phase_semaphores)
            nc.all_engine_barrier(sem_only=True)


def take(s, p, shape, dt=F32):
    n = 1
    for a in shape:
        n *= a
    words = n if dt != F16 else (n + 1) // 2
    s.used += words
    assert s.used <= (NB * N + 1) // 2
    return view(s.arena[0:p, s.used - words:s.used], shape, dt)


def view(v, shape, dt=F32):
    n = 1
    for a in shape:
        n *= a
    if dt != F32:
        v = v.bitcast(dt)[:, 0:n]
    if len(shape) == 2:
        v = v.rearrange("p (a b) -> p a b", b=shape[1])
    if len(shape) == 3:
        v = v.rearrange("p (a b c) -> p a b c", b=shape[1], c=shape[2])
    return v


def bank(s, b, p=128, a=0, n=BANK):
    return s.PS[0:p, b * BANK + a:b * BANK + a + n]


def prepare(nc, s):
    t = s.t
    with ExitStack() as ctx:
        def sem(name):
            return semaphore(nc, s, "pr_" + name)

        s.used = 0
        s.Wkv = take(s, 128, [KC, 2 * D])
        s.W1 = take(s, 128, [KC, HID])
        A1 = HD + 1
        end = NB * N // 2
        s.X, s.Y, s.KX = (s.arena[0:A1, end - (i + 1) * HEADS * D:end - i * HEADS * D] for i in range(3))
        s.K = s.arena[0:A1, end - 3 * HEADS * D - HEADS * A1:end - 3 * HEADS * D]
        s.arena_keep = s.used
        sq = take(s, 128, [KC, HID])
        b1B = take(s, BL, [HID])
        b1c = take(s, 128, [1])
        absb = take(s, 128, [1])
        norm = take(s, 128, [1])
        sc = take(s, 128, [1])
        mean = take(s, 128, [KC, 2 * HEADS])
        wq = take(s, HD, [HEADS, D])
        woT = take(s, HD, [HEADS, D])
        ln = take(s, HD, [4])
        GkT = take(s, HD, [HD + 1])
        GvT = take(s, HD, [HD + 1])
        b2B = take(s, BL, [D])
        FC = E // BL
        C = NQ * SLOTS
        row0 = take(s, 128, [BL * W], I32)
        first_i = take(s, BL, [FC], I32)
        first = take(s, BL, [FC])
        t5_i = take(s, BL, [NQ], I32)
        t5 = take(s, BL, [NQ])
        junk = take(s, BL, [FC])
        n1 = take(s, BL, [NQ])
        rowf = take(s, BL, [NQ])
        row_i = take(s, BL, [NQ], I32)
        R = take(s, BL, [NQ, BL], I32)
        n2 = take(s, BL, [NQ])
        at = take(s, BL, [NQ])
        at_i = take(s, BL, [NQ], I32)
        EW = take(s, BL, [NQ, SLOTS * 2], I32)
        src = take(s, BL, [C])
        loc = take(s, BL, [C])
        hi = take(s, BL, [C])
        low_ok = take(s, BL, [C])
        lo = take(s, BL, [C])
        valid = take(s, BL, [C])
        locm = take(s, BL, [C])
        keym = take(s, BL, [C])
        vsum = take(s, BL, [1])
        locT = take(s, 128, [NW], F16)
        L = take(s, 128, [NW, W], F16)
        ones16 = take(s, 128, [128], F16)

        loads = [
            ("first", first_i, t["firsts"].partition_broadcast(BL)),
            ("W1", s.W1, t["W1"].rearrange("(k p) n -> p k n", p=128)),
            ("kv", s.Wkv, t["wkvT"].rearrange("(k p) n -> p k n", p=128)),
            ("ln", ln, t["ln"]),
            ("b1c", b1c, t["b1"].rearrange("(p a) -> p a", a=1)),
            ("wq", wq, t["wq"].rearrange("(h d) n -> d h n", d=HD)),
            ("wo", woT, t["woT"].rearrange("(h d) n -> d h n", d=HD)),
            ("b1", b1B, t["b1"].partition_broadcast(BL)),
            ("b2", b2B, t["b2"].partition_broadcast(BL)),
            ("bo", s.bsum[:, :], t["bo"].partition_broadcast(BL)),
        ]
        got = {name: sem("in_" + name) for name, _, _ in loads}
        thr, zeros, consts, ident_r, spread = sem("thr"), sem("zeros"), sem("consts"), sem("ident"), sem("spread")
        step, squared, norm_mm, norm_sb, norm_pow, sc_r = (sem(x) for x in ("step", "sq", "nmm", "nsb", "npow", "sc"))
        sc_row, gains, folded, xy_kept, kept = sem("scrow"), sem("gains"), sem("folded"), sem("xy"), sem("kept")
        rows_at, rows_in = sem("rowat"), [sem(f"r{q}") for q in range(NQ)]
        edges_at, edges_in = sem("edgeat"), [sem(f"e{q}") for q in range(NQ)]
        divided, masked, turned, counted, flag_mm = sem("div"), sem("mask"), sem("turn"), sem("cnt"), sem("flag")
        hot, loc_r, deg_mm, deg_sb = sem("hot"), sem("loc"), sem("degmm"), sem("degsb")
        SC, DEG = 6, 7
        block = ctx.enter_context(nc.Block())

        @block.sync
        def _(sp):
            for name, dst, src_ in loads:
                sp.dma_start(dst, src_).then_inc(got[name], 16)

        @block.gpsimd
        def _(pool):
            pool.iota(t5_i, pattern=[[W * BL, NQ]], base=0, channel_multiplier=W).then_inc(thr, 1)
            pool.memset(s.ident[:, :], 0.0).then_inc(zeros, 1)
            pool.memset(s.ones[:, :], 1.0).then_inc(consts, 1)
            pool.memset(s.half[:, :], -0.5).then_inc(consts, 1)
            pool.memset(s.plus[:, :], 0.5).then_inc(consts, 1)
            pool.memset(ones16, 1.0).then_inc(consts, 1)
            pool.wait_ge(zeros, 1)
            pool.affine_select(out=s.ident[:, :], in_=s.ident[:, :], compare_op=ALU.not_equal, fill=1.0, base=0,
                               pattern=[[-1, 128]], channel_multiplier=1).then_inc(ident_r, 1)
            pool.iota(row0, pattern=[[1, BL], [0, W]], base=0, channel_multiplier=0).then_inc(ident_r, 1)
            pool.wait_ge(consts, 4)
            pool.wait_ge(rows_at, 1)
            for q in range(NQ):
                pool.indirect_dma_start(out=R[:, q, :], out_offset=None, in_=t["dst"].rearrange("(a b) -> a b", b=BL),
                                        in_offset=bass.IndirectOffsetOnAxis(ap=row_i[:, q:q + 1], axis=0)
                                        ).then_inc(rows_in[q], 16)
            pool.wait_ge(norm_sb, 1)
            pool.tensor_tensor(norm, norm, s.plus[:, 0:1], ALU.pow).then_inc(norm_pow, 1)
            pool.wait_ge(edges_at, 1)
            for q in range(NQ):
                pool.indirect_dma_start(out=EW[:, q, :], out_offset=None, in_=t["edges"].rearrange("(a b) -> a b", a=1),
                                        in_offset=bass.IndirectOffsetOnAxis(ap=at_i[:, q:q + 1], axis=1)
                                        ).then_inc(edges_in[q], 16)

        @block.vector
        def _(dve):
            chain = [0]

            def link(ins):
                chain[0] += 1
                ins.then_inc(step, 1)
                dve.wait_ge(step, chain[0])

            dve.wait_ge(thr, 1)
            link(dve.tensor_copy(t5, t5_i))
            dve.wait_ge(got["first"], 16)
            link(dve.tensor_copy(first, first_i))
            for q in range(NQ):
                link(dve.tensor_scalar(junk, first, t5[:, q:q + 1], 0.0, ALU.is_lt, ALU.add, accum_out=n1[:, q:q + 1]))
            link(dve.tensor_scalar(rowf, n1, 1.0, 0.0, ALU.subtract, ALU.max))
            dve.tensor_copy(row_i, rowf).then_inc(rows_at, 1)

            dve.wait_ge(got["W1"], 16)
            dve.tensor_tensor(sq, s.W1, s.W1, ALU.mult).then_inc(squared, 1)
            dve.wait_ge(got["ln"], 16)
            dve.wait_ge(ident_r, 1)
            for m, a in ((GkT, 0), (GvT, 2)):
                dve.tensor_scalar(m[:, 0:HD], s.ident[0:HD, 0:HD], ln[:, a:a + 1], None, ALU.mult).then_inc(gains, 1)
                dve.tensor_copy(m[:, HD:HD + 1], ln[:, a + 1:a + 2]).then_inc(gains, 1)
            dve.wait_ge(got["kv"], 16)
            kv3 = s.Wkv.rearrange("p k (h d) -> p (k h) d", d=HD)
            m3 = mean.rearrange("p k h -> p (k h)")
            link(dve.tensor_reduce(m3, kv3, AX.X, ALU.add))

            for q in range(NQ):
                dve.wait_ge(rows_in[q], 16)
                link(dve.tensor_scalar(junk[:, 0:BL], R[:, q, :], t5[:, q:q + 1], 0.0, ALU.is_lt, ALU.add,
                                       accum_out=n2[:, q:q + 1]))
            link(dve.scalar_tensor_tensor(at, rowf, float(BL), n2, ALU.mult, ALU.add))
            dve.tensor_scalar(at_i, at, float(E - SLOTS), 2.0, ALU.min, ALU.mult).then_inc(edges_at, 1)

            link(dve.tensor_scalar(m3, m3, -1.0 / HD, None, ALU.mult))
            dve.tensor_tensor(kv3, kv3, bc(m3, HD), ALU.add).then_inc(kept, 1)
            dve.wait_ge(got["b1c"], 16)
            link(dve.tensor_scalar(absb, b1c, -1.0, None, ALU.mult))
            link(dve.tensor_tensor(absb, absb, b1c, ALU.max))
            dve.wait_ge(norm_pow, 1)
            link(dve.scalar_tensor_tensor(norm, norm, 16.0, absb, ALU.mult, ALU.add))
            link(dve.tensor_scalar(s.inv_s[:, :], norm, 1e-20, 1.0 / LIMIT, ALU.max, ALU.mult))
            dve.reciprocal(sc, s.inv_s[:, :]).then_inc(sc_r, 1)
            dve.wait_ge(got["b2"], 16)
            dve.wait_ge(got["bo"], 16)
            dve.tensor_tensor(s.bsum[:, :], s.bsum[:, :], b2B, ALU.add).then_inc(kept, 1)
            dve.wait_ge(sc_row, 1)
            dve.wait_ge(got["b1"], 16)
            dve.tensor_tensor(s.sb1[:, :], b1B, bank(s, SC, BL, 128, HID), ALU.mult).then_inc(kept, 1)
            for k in range(KC):
                dve.tensor_tensor(s.W1[:, k, :], s.W1[:, k, :], bank(s, SC, 128, 128, HID), ALU.mult).then_inc(kept, 1)

            for q in range(NQ):
                dve.wait_ge(edges_in[q], 16)
                pair = EW[:, q, :].rearrange("p (e k) -> p e k", k=2)
                cols = slice(q * SLOTS, (q + 1) * SLOTS)
                dve.tensor_copy(src[:, cols], pair[:, :, 0]).then_inc(divided, 1)
                link(dve.tensor_scalar(loc[:, cols], pair[:, :, 1], t5[:, q:q + 1], None, ALU.subtract))
            link(dve.tensor_scalar(low_ok, loc, 0.0, None, ALU.is_ge))
            link(dve.scalar_tensor_tensor(valid, loc, float(W), low_ok, ALU.is_lt, ALU.mult))
            dve.tensor_reduce(vsum, valid, AX.X, ALU.add).then_inc(counted, 1)
            dve.wait_ge(divided, NQ + 1)
            link(dve.tensor_scalar(hi, hi, ROUND, None, ALU.add))
            link(dve.tensor_scalar(hi, hi, ROUND, None, ALU.subtract))
            dve.scalar_tensor_tensor(lo, hi, -float(BL), src, ALU.mult, ALU.add).then_inc(masked, 1)
            dve.scalar_tensor_tensor(locm, loc, 1.0, valid, ALU.add, ALU.mult).then_inc(masked, 1)
            link(dve.scalar_tensor_tensor(keym, hi, float(W), loc, ALU.mult, ALU.add))
            dve.scalar_tensor_tensor(keym, keym, 1.0, valid, ALU.add, ALU.mult).then_inc(masked, 1)
            dve.wait_ge(turned, 2)
            dve.tensor_scalar(locT[:, 0:500], bank(s, 4, 128, 0, 500), 1.0, None, ALU.subtract).then_inc(loc_r, 1)
            dve.tensor_scalar(locT[:, 500:NW], bank(s, 5, 128, 0, 125), 1.0, None, ALU.subtract).then_inc(loc_r, 1)
            dve.wait_ge(loc_r, 2)
            for j in range(W):
                dve.tensor_scalar(L[:, :, j], locT, float(j), None, ALU.is_equal).then_inc(hot, 1)
            dve.wait_ge(flag_mm, 1)
            dve.tensor_copy(s.flag[:, :], bank(s, DEG, 128, 0, 1)).then_inc(hot, 1)
            dve.wait_ge(deg_mm, 1)
            dve.tensor_scalar(s.dinvN[:, :], bank(s, DEG, BL, 8, NB), 1.0, None, ALU.add).then_inc(deg_sb, 1)
            dve.wait_ge(deg_sb, 1)
            dve.wait_ge(kept, 5)
            dve.wait_ge(hot, W + 1)

        @block.scalar
        def _(act):
            act.wait_ge(ident_r, 1)
            act.activation(s.ident16[:, :], s.ident[:, :], ACT.Copy).then_inc(spread, 1)
            act.wait_ge(ident_r, 2)
            act.activation(s.iotaW[:, :, :].rearrange("p c n -> p (c n)"), row0, ACT.Copy).then_inc(spread, 1)
            act.wait_ge(norm_mm, 1)
            act.activation(norm, bank(s, SC, 128, 0, 1), ACT.Copy).then_inc(norm_sb, 1)
            act.wait_ge(folded, 1)
            act.activation(s.X, s.PS[0:HD + 1, 0:2 * BANK], ACT.Copy).then_inc(xy_kept, 1)
            act.wait_ge(folded, 2)
            act.activation(s.Y, s.PS[0:HD + 1, 2 * BANK:4 * BANK], ACT.Copy).then_inc(xy_kept, 1)
            act.wait_ge(divided, NQ)
            act.activation(hi, src, ACT.Copy, scale=1.0 / BL, bias=0.5 / BL - 0.5).then_inc(divided, 1)
            for i, (m, b) in enumerate(((s.loT[:, :], 0), (s.keyT[:, :], 2))):
                act.wait_ge(turned, 2 * i + 1)
                act.activation(m[:, 0:500], bank(s, b, 128, 0, 500), ACT.Copy, bias=-float(i)).then_inc(spread, 1)
                act.activation(m[:, 500:NW], bank(s, b + 1, 128, 0, 125), ACT.Copy, bias=-float(i)).then_inc(spread, 1)
            act.wait_ge(spread, 6)

        @block.tensor
        def _(pe):
            pe.wait_ge(squared, 1)
            pe.wait_ge(consts, 4)
            for k in range(KC):
                mm = pe.matmul(bank(s, SC, 128, 0, 1), sq[:, k, :], s.ones[:, 0:1], start=(k == 0), stop=(k == KC - 1))
            mm.then_inc(norm_mm, 1)
            pe.wait_ge(gains, 4)
            pe.wait_ge(got["wq"], 16)
            pe.wait_ge(got["wo"], 16)
            for m, w, b in ((GkT, wq, 0), (GvT, woT, 2)):
                flat = w.rearrange("p h n -> p (h n)")
                for c in range(2):
                    mm = pe.matmul(bank(s, b + c, HD + 1), m, flat[:, c * BANK:(c + 1) * BANK], start=True, stop=True)
                mm.then_inc(folded, 1)
            pe.wait_ge(sc_r, 1)
            pe.transpose(bank(s, SC, 128, 128, HID), sc.to_broadcast([128, 128]), s.ident[:, :]).then_inc(sc_row, 1)
            pe.wait_ge(xy_kept, 2)
            for i, (m, b) in enumerate(((lo, 0), (locm, 4), (keym, 2))):
                pe.wait_ge(masked, i + 1)
                for q in range(NQ):
                    mm = pe.transpose(bank(s, b + (q == 4), 128, (q % 4) * BL, BL), m[:, q * SLOTS:(q + 1) * SLOTS],
                                      s.ident[0:BL, 0:BL])
                mm.then_inc(turned, 1)
            pe.wait_ge(counted, 1)
            pe.matmul(bank(s, DEG, 128, 0, 1), s.ones[0:BL, :], vsum, start=True, stop=True).then_inc(flag_mm, 1)
            pe.wait_ge(hot, W + 1)
            for b in range(NB):
                mm = pe.matmul(bank(s, DEG, BL, 8 + b, 1), L[:, b * WB:(b + 1) * WB, :].rearrange("p n j -> p (n j)"),
                               ones16[:, 0:1], start=True, stop=True)
            mm.then_inc(deg_mm, 1)


def attention_stats(nc, s):
    t = s.t
    with ExitStack() as ctx:
        def sem(name):
            return semaphore(nc, s, "st_" + name)

        s.used = s.arena_keep
        A1 = HD + 1
        xin = take(s, BL, [U, D])
        xn = take(s, BL, [U, D])
        xnT = take(s, 128, [U, KC * BL])
        st = take(s, BL, [U, 6])
        mv = take(s, BL, [U, 2])
        ve = take(s, BL, [U])
        rstd = take(s, BL, [U])
        sq = take(s, BL, [2, 2 * HEADS, HD + 1])
        ss = take(s, BL, [U, 2 * HEADS])
        rs = take(s, BL, [U, 2 * HEADS])
        kv = take(s, BL, [U * 2 * HEADS, A1])
        assert s.used <= NB * N // 2 - 3 * HEADS * D - HEADS * A1
        KV, TP, HB, AC = [0, 1, 2, 3, 4], 5, 7, 6
        loaded, spilled = [sem(f"x{u}") for u in range(U)], [sem(f"sp{u}") for u in range(U)]
        stats, aggr, ve_r, rstd_r, xn_r = sem("stats"), sem("aggr"), sem("ve"), sem("rstd"), sem("xn")
        tp_r, xnT_r, mm_r, h_hi, h_out = sem("tp"), sem("xnT"), sem("mm"), sem("hhi"), sem("hout")
        sq_r, ss_r, rs_r, kv_r, acc_r, ready, sq_set, dinv_r = (
            sem(x) for x in ("sq", "ss", "rs", "kv", "acc", "rdy", "sqset", "dinv"))
        block = ctx.enter_context(nc.Block())

        @block.sync
        def _(sp):
            start_at(sp, [xn_r])

            def load(i, u, r):
                sp.wait_ge(xn_r, at(i) - U)
                sp.dma_start(xin[:, u, :], rows(t["x"], i)).then_inc(loaded[u], 16)

            def spill(i, u, r):
                sp.wait_ge(xnT_r, at(i))
                sp.dma_start(s.xnT_d.rearrange("(b p) c -> b p c", p=128)[bass.ds(i, 1)]
                             .rearrange("a p c -> (a p) c"), xnT[:, u, :]).then_inc(spilled[u], 16)

            pipelined(sp, (0, load), (4, spill))
            for u in range(U):
                sp.wait_ge(spilled[u], 16 * IT + 16)

        @block.vector
        def _(dve):
            start_at(dve, [stats, aggr, ss_r, kv_r, h_out])
            dve.memset(kv[:, :, HD:HD + 1], HD ** -0.5).then_inc(ready, 1)
            dve.memset(sq[:, :, :, HD:HD + 1], HD * EPS).then_inc(ready, 1)
            dve.wait_ge(ready, 2)
            dve.sem_inc(sq_set, 1)

            def statistics(i, u, r):
                dve.wait_ge(loaded[u], r * 16 + 16)
                dve.bn_stats(st[:, u, :], xin[:, u, :]).then_inc(stats, 1)

            def aggregate(i, u, r):
                hold(dve, s.held, (stats, at(i)), (xn_r, at(i) - U))
                dve.bn_aggr(mv[:, u, :], st[:, u, :]).then_inc(aggr, 1)

            def norm(i, u, r):
                dve.wait_ge(rstd_r, at(i))
                dve.wait_ge(tp_r, at(i) - U)
                dve.tensor_scalar(xn[:, u, :], xin[:, u, :], mv[:, u, 0:1], rstd[:, u:u + 1], ALU.subtract,
                                  ALU.mult).then_inc(xn_r, 1)

            def square_sums(i, u, r):
                dve.wait_ge(sq_r, at(i))
                dve.wait_ge(rs_r, at(i) - U)
                dve.tensor_reduce(ss[:, u, :], sq[:, TWO[u]], AX.X, ALU.add).then_inc(ss_r, 1)

            def low_part(i, u, r):
                dve.wait_ge(h_hi, at(i))
                dve.scalar_tensor_tensor(blk(s.h1[:, :, HID:2 * HID], i), bank(s, HB, BL, 0, HID),
                                         s.dinvN[:, bass.ds(i, 1)], blk(s.h1[:, :, 0:HID], i),
                                         ALU.mult, ALU.subtract).then_inc(h_out, 1)

            def normalise(i, u, r):
                dve.wait_ge(rs_r, at(i))
                dve.wait_ge(acc_r, at(i) - U)
                dve.tensor_tensor(kv[:, u * 2 * HEADS:(u + 1) * 2 * HEADS, 0:HD],
                                  bank(s, KV[u], BL).rearrange("p (h d) -> p h d", d=HD),
                                  bc(rs[:, u, :], HD), ALU.mult).then_inc(kv_r, 1)

            pipelined(dve, (1, norm), (0, statistics), (0, aggregate), (3, low_part), (4, normalise), (3, square_sums),
                      last=[(1, norm), (3, square_sums), (3, low_part), (4, normalise)])

        @block.gpsimd
        def _(pool):
            pool.tensor_tensor(s.dinvN[:, :], s.dinvN[:, :], s.half[0:BL, 0:1].to_broadcast([BL, NB]),
                               ALU.pow).then_inc(dinv_r, 1)
            pool.wait_ge(dinv_r, 1)
            start_at(pool, [ve_r, rstd_r, rs_r])

            def one_over_std(i, u, r):
                hold(pool, s.held, (aggr, at(i)))
                pool.tensor_scalar(ve[:, u:u + 1], mv[:, u, 1:2], EPS, None, ALU.add).then_inc(ve_r, 1)
                pool.wait_ge(ve_r, at(i))
                pool.wait_ge(xn_r, at(i) - U)
                pool.tensor_tensor(rstd[:, u:u + 1], ve[:, u:u + 1], s.half[0:BL, 0:1], ALU.pow).then_inc(rstd_r, 1)

            def head_factors(i, u, r):
                pool.wait_ge(ss_r, at(i))
                pool.wait_ge(kv_r, at(i) - U)
                pool.tensor_tensor(rs[:, u, :], ss[:, u, :], s.half[0:BL, 0:1].to_broadcast([BL, 2 * HEADS]),
                                   ALU.pow).then_inc(rs_r, 1)

            pipelined(pool, (0, one_over_std), (3, head_factors))

        @block.scalar
        def _(act):
            start_at(act, [xnT_r, sq_r, h_hi])
            act.wait_ge(sq_set, 1)
            act.wait_ge(dinv_r, 1)
            start_at(act, spilled, 16)

            def turned(i, u, r):
                act.wait_ge(tp_r, at(i))
                act.wait_ge(mm_r, at(i) - U)
                act.wait_ge(spilled[u], r * 16 + 16)
                act.activation(xnT[:, u, :], bank(s, TP, 128, 0, KC * BL), ACT.Copy).then_inc(xnT_r, 1)

            def squares(i, u, r):
                act.wait_ge(mm_r, at(i))
                act.wait_ge(ss_r, at(i) - before(TWO, u))
                act.activation(sq[:, TWO[u], :, 0:HD], bank(s, KV[u], BL).rearrange("p (h d) -> p h d", d=HD),
                               ACT.Square).then_inc(sq_r, 1)
                act.activation(blk(s.h1[:, :, 0:HID], i), bank(s, HB, BL, 0, HID), ACT.Copy,
                               scale=s.dinvN[:, bass.ds(i, 1)]).then_inc(h_hi, 1)

            pipelined(act, (1, turned), (2, squares))

        @block.tensor
        def _(pe):
            start_at(pe, [tp_r, mm_r, acc_r])
            acc = bank(s, AC, A1, 0, HEADS * A1)

            def turn(i, u, r):
                pe.wait_ge(xn_r, at(i))
                pe.wait_ge(xnT_r, at(i) - 1)
                for k in range(KC):
                    mm = pe.transpose(bank(s, TP, 128, k * BL, BL), xn[:, u, k * 128:(k + 1) * 128],
                                      s.ident[0:BL, 0:BL])
                mm.then_inc(tp_r, 1)

            def project(i, u, r):
                pe.wait_ge(xnT_r, at(i))
                pe.wait_ge(kv_r, at(i) - U)
                for k in range(KC):
                    pe.matmul(bank(s, KV[u], BL), xnT[:, u, k * BL:(k + 1) * BL], s.Wkv[:, k, :],
                              start=(k == 0), stop=(k == KC - 1))
                pe.wait_ge(h_out, at(i) - 1)
                for k in range(KC):
                    mm = pe.matmul(bank(s, HB, BL, 0, HID), xnT[:, u, k * BL:(k + 1) * BL], s.W1[:, k, :],
                                   start=(k == 0), stop=(k == KC - 1))
                mm.then_inc(mm_r, 1)

            def head_sums(i, u, r):
                pe.wait_ge(kv_r, at(i))
                for h in range(HEADS):
                    mm = pe.matmul(acc[:, h * A1:(h + 1) * A1], kv[:, u * 2 * HEADS + h, :],
                                   kv[:, u * 2 * HEADS + HEADS + h, :],
                                   start=isinstance(i, int) and i == 0 and h == 0,
                                   stop=isinstance(i, int) and i == NB - 1, skip_group_check=True)
                mm.then_inc(acc_r, 1)

            pipelined(pe, (1, turn), (2, project), (4, head_sums))


class Fold:

    def __init__(self, nc, s, prefix):
        self.s = s
        self.k_r, self.kx_mm, self.kx_r, self.m_mm, self.m_r = (
            semaphore(nc, s, prefix + x) for x in ("k", "kxmm", "kx", "mmm", "m"))

    def take_sums(self, act):
        act.activation(self.s.K, bank(self.s, 6, HD + 1, 0, HEADS * (HD + 1)), ACT.Copy, scale=HD / N).then_inc(self.k_r, 1)

    def take_kx(self, act):
        for i in range(2):
            act.wait_ge(self.kx_mm, i + 1)
            act.activation(self.s.KX[:, i * 2 * D:(i + 1) * 2 * D], bank(self.s, 7 - i, HD + 1), ACT.Copy).then_inc(self.kx_r, 1)

    def take_m(self, act):
        act.wait_ge(self.m_mm, 1)
        act.activation(self.s.M[:, :, :].rearrange("p k n -> p (k n)"), bank(self.s, 7), ACT.Copy).then_inc(self.m_r, 1)

    def multiply_kx(self, pe):
        s, A1 = self.s, HD + 1
        pe.wait_ge(self.k_r, 1)
        for h in range(HEADS):
            mm = pe.matmul(bank(s, 7 - h // 2, A1, h % 2 * D, D), s.K[:, h * A1:(h + 1) * A1], s.X[:, h * D:(h + 1) * D],
                           start=True, stop=True)
            if h % 2 == 1:
                mm.then_inc(self.kx_mm, 1)

    def multiply_m(self, pe, k):
        s = self.s
        pe.wait_ge(self.kx_r, 2)
        for h in range(HEADS):
            mm = pe.matmul(bank(s, 7, 128, k * D, D), s.KX[:, h * D + k * 128:h * D + (k + 1) * 128],
                           s.Y[:, h * D:(h + 1) * D], start=(h == 0), stop=(h == HEADS - 1))
        if k == KC - 1:
            mm.then_inc(self.m_mm, 1)


def build_and_convolve(nc, s):
    with ExitStack() as ctx:
        def sem(name):
            return semaphore(nc, s, "bc_" + name)

        hots = s.aggT[:, :].bitcast(F16).rearrange("p (k g c w) -> p k g c w", k=2, g=GROUPS, w=W)
        z = view(s.tail[0:BL, 0:2 * HID], [2, HID])
        hot, used, copied, conv = sem("hot"), sem("used"), sem("copied"), sem("conv")
        biased, scaled, hi_r, lo_r = sem("biased"), sem("scaled"), sem("hi"), sem("lo")
        NCH = len(CH)
        START = [sum(CH[:c]) for c in range(NCH)]
        CONV = 7
        fold = Fold(nc, s, "bc_")
        block = ctx.enter_context(nc.Block())

        def turns(eng, turn):
            turn(0, 0, build=True)
            turn(1, 1, build=True)
            turn(2, 0, build=True, convolve=True)
            turn(3, 1, build=True, convolve=True, scale=True)
            with eng.Fori(1, NB // 4) as r:
                for k in range(4):
                    turn(4 * r + k, k % 2, build=True, convolve=True, scale=True, split=True)
            turn(NB - 1, 0, build=True, convolve=True, scale=True, split=True)
            turn(NB, 1, convolve=True, scale=True, split=True)
            turn(NB + 1, 0, convolve=True, scale=True, split=True)
            turn(NB + 2, 1, scale=True, split=True)
            turn(NB + 3, 0, split=True)

        @block.vector
        def _(dve):
            covered = dve.value_load(s.flag[0:1, 0:1])
            with dve.If(covered == E):
                start_at(dve, [used], WB)
                start_at(dve, [biased], 1)

                def turn(t, odd, build=False, convolve=False, scale=False, split=False):
                    for g in range(GROUPS):
                        if build:
                            k = t * WB + g * W
                            dve.wait_ge(used, k + W)
                            dve.tensor_tensor(hots[:, 0, g], s.iotaW[:, :, :],
                                              s.loT[:, bass.ds(k, W)].unsqueeze(1).to_broadcast([128, BL, W]), ALU.is_equal)
                            dve.tensor_tensor(hots[:, 1, g], s.iotaW[:, :, :],
                                              s.keyT[:, bass.ds(k, W)].unsqueeze(1).to_broadcast([128, BL, W]),
                                              ALU.is_equal).then_inc(hot, 1)
                        if scale and g == 2:
                            dve.wait_ge(lo_r, t - 2)
                            dve.wait_ge(conv, t - 2)
                            dve.scalar_tensor_tensor(z[:, 1 - odd], bank(s, CONV, BL, 0, HID), s.dinvN[:, bass.ds(t - 3, 1)],
                                                     s.sb1[:, :], ALU.mult, ALU.add).then_inc(biased, 1)

                turns(dve, turn)
            dve.end_ifs()

        @block.gpsimd
        def _(pool):
            covered = pool.value_load(s.flag[0:1, 0:1])
            with pool.If(covered == E):
                start_at(pool, [lo_r], 2)

                def turn(t, odd, build=False, convolve=False, scale=False, split=False):
                    if split:
                        pool.wait_ge(hi_r, t - 3)
                        pool.tensor_tensor(blk(s.h2[:, :, HID:2 * HID], t - 4), z[:, odd], blk(s.h2[:, :, 0:HID], t - 4),
                                           ALU.subtract).then_inc(lo_r, 1)

                turns(pool, turn)
                pool.wait_ge(lo_r, NB + 2)
            pool.end_ifs()

        @block.scalar
        def _(act):
            covered = act.value_load(s.flag[0:1, 0:1])
            with act.If(covered == E):
                start_at(act, [copied], NCH)
                fold.take_sums(act)
                fold.take_kx(act)

                def turn(t, odd, build=False, convolve=False, scale=False, split=False):
                    if build and convolve and not scale:
                        fold.take_m(act)
                    for c in range(NCH):
                        if build:
                            act.wait_ge(used, t * WB + START[c] + CH[c] + WB)
                            src = bank(s, c, BL, 0, CH[c] * BL).rearrange("p (n h w) -> p h n w", n=CH[c], w=W)
                            dst = s.adj[0:BL, bass.ds(t * N, N)].rearrange("p (h d) -> p h d", d=BL)
                            dst = dst[:, :, START[c] * W:(START[c] + CH[c]) * W].rearrange("p h (n w) -> p h n w", w=W)
                            act.activation(dst, src, ACT.Copy).then_inc(copied, 1)
                        if scale and c == 3:
                            act.wait_ge(biased, t - 1)
                            act.activation(z[:, 1 - odd], z[:, 1 - odd], ACT.Relu,
                                           scale=s.dinvN[:, bass.ds(t - 3, 1)]).then_inc(scaled, 1)
                        if scale and c == 4:
                            act.wait_ge(scaled, t - 2)
                            act.activation(blk(s.h2[:, :, 0:HID], t - 3), z[:, 1 - odd], ACT.Copy).then_inc(hi_r, 1)

                turns(act, turn)
                act.wait_ge(hi_r, NB)
            act.end_ifs()

        @block.tensor
        def _(pe):
            covered = pe.value_load(s.flag[0:1, 0:1])
            with pe.If(covered == E):
                dst = bank(s, CONV, BL, 0, HID)
                fold.multiply_kx(pe)

                def turn(t, odd, build=False, convolve=False, scale=False, split=False):
                    h = 0
                    for c in range(NCH):
                        if build:
                            if c == NCH - 1:
                                pe.wait_ge(fold.kx_r, 2)
                            pe.wait_ge(copied, t * NCH + c + 1)
                            for n in range(CH[c]):
                                w = START[c] + n
                                if w % W == 0:
                                    pe.wait_ge(hot, t * GROUPS + w // W + 1)
                                pe.matmul(bank(s, c, BL, n * BL, BL), hots[:, 0, w // W, :, w % W],
                                          hots[:, 1, w // W, :, w % W], start=True, stop=True).then_inc(used, 1)
                        if build and not convolve and c == NCH - 1:
                            fold.multiply_m(pe, t)
                        if convolve and c == 2:
                            pe.wait_ge(fold.m_r, 1)
                            pe.wait_ge(copied, t * NCH)
                            pe.wait_ge(biased, t - 1)
                        if convolve:
                            while h * (NCH - 2) < (c - 1) * NB:
                                for p in range(2):
                                    pe.matmul(dst, s.adj[0:BL, bass.ds((t - 2) * N + h * BL, BL)],
                                              s.h1[:, h, p * HID:(p + 1) * HID], start=(h == 0 and p == 0), stop=False,
                                              skip_group_check=True)
                                h += 1
                    if convolve:
                        for p in range(2):
                            mm = pe.matmul(dst, s.ident16[0:BL, 0:BL], blk(s.h1[:, :, p * HID:(p + 1) * HID], t - 2),
                                           start=False, stop=(p == 1), skip_group_check=True)
                        mm.then_inc(conv, 1)

                turns(pe, turn)
            pe.end_ifs()


def convolve_again(nc, s):
    t = s.t
    with ExitStack() as ctx:
        def sem(name):
            return semaphore(nc, s, "ca_" + name)

        conv, scaled, rows_mm, rows_kept = sem("conv"), sem("scaled"), sem("rows_mm"), sem("rows_kept")
        adj = s.adj[0:BL, 0:NB * N].rearrange("p (j h d) -> p j h d", j=NB, d=BL)
        s.Wc = view(s.tail[:, 0:KC * INNER], [KC, INNER])
        s.biasC = s.tail[0:BL, KC * INNER:(KC + 1) * INNER]
        tmpb = s.tail[0:BL, (KC + 1) * INNER:(KC + 2) * INNER]
        temp = s.tail[:, (KC + 2) * INNER:(KC + 2) * INNER + FH]
        rtemp = s.tail[:, (KC + 2) * INNER + FH:(KC + 2) * INNER + 2 * FH]
        free = s.h1_flat[:, :].bitcast(F32)
        a = FH * D
        WxT = view(free[0:G, 0:a], [FH, D])
        Wsl = free[0:G, a:a + G]
        bslB = free[:, a + G:a + 2 * G]
        bx = free[0:G, a + 2 * G:a + 2 * G + FH]
        a += 2 * G + FH
        bxB = view(free[0:G, a:a + FH * BL], [FH, BL])
        loads = [
            ("WxT", WxT, t["WxT"].rearrange("(h c) n -> c h n", c=G)),
            ("Wsl", Wsl, t["W_slice"]),
            ("bx", bx, t["bxT"]),
            ("bsl", bslB, t["b_slice"].partition_broadcast(BL)),
            ("temp", temp, t["temp"].partition_broadcast(128)),
        ]
        got = {name: sem("in_" + name) for name, _, _ in loads}
        step, spread, logits, biases, made = sem("step"), sem("spread"), sem("logits"), sem("biases"), sem("made")
        block = ctx.enter_context(nc.Block())

        def heads(ap):
            return ap.rearrange("p (h g) -> p h g", g=G)

        @block.sync
        def _(sp):
            for name, dst, src in loads:
                sp.dma_start(dst, src).then_inc(got[name], 16)

        @block.gpsimd
        def _(pool):
            chain = [0]

            def link(ins):
                chain[0] += 1
                ins.then_inc(step, 1)
                pool.wait_ge(step, chain[0])

            pool.wait_ge(got["temp"], 16)
            link(pool.tensor_scalar(temp, temp, 0.1, 5.0, ALU.max, ALU.min))
            pool.wait_ge(got["bx"], 16)
            pool.tensor_copy(bxB, bc(bx, BL)).then_inc(spread, 1)

        @block.vector
        def _(dve):
            def scale(c, b, n):
                dve.wait_ge(conv, c + 1)
                dve.wait_ge(rows_kept, c + 1)
                v = s.aggT[:, bass.ds(c * 4 * BL, n * BL)]
                dve.scalar_tensor_tensor(v, bank(s, b, 128, 0, n * BL), s.inv_s[:, 0:1], v, ALU.mult,
                                         ALU.mult).then_inc(scaled, 1)

            covered = dve.value_load(s.flag[0:1, 0:1])
            with dve.If(covered == E):
                start_at(dve, [scaled], 2)

                with dve.Fori(0, 3) as r:
                    scale(2 * r, 0, 4)
                    scale(2 * r + 1, 1, 4)
            dve.end_ifs()
            dve.wait_ge(spread, 1)
            dve.reciprocal(rtemp, temp).then_inc(made, 1)
            dve.wait_ge(made, 1)
            dve.wait_ge(logits, 1)
            for k in range(KC):
                dve.tensor_tensor(heads(s.Wc[:, k, :]), heads(bank(s, 4 + k)), bc(rtemp, G), ALU.mult).then_inc(made, 1)
            dve.wait_ge(biases, 1)
            dve.wait_ge(got["bsl"], 16)
            dve.tensor_tensor(heads(tmpb), heads(bank(s, 6, BL)), bslB.unsqueeze(1).to_broadcast([BL, FH, G]),
                              ALU.add).then_inc(made, 1)
            dve.wait_ge(made, 4)
            dve.tensor_tensor(heads(s.biasC), heads(tmpb), bc(rtemp[0:BL, :], G), ALU.mult).then_inc(made, 1)
            dve.wait_ge(made, 5)
            with dve.If(covered == E):
                scale(6, 0, 1)
                dve.wait_ge(scaled, 9)
            dve.end_ifs()

        @block.scalar
        def _(act):
            covered = act.value_load(s.flag[0:1, 0:1])
            with act.If(covered == E):
                for c in range(7):
                    act.wait_ge(rows_mm, c + 1)
                    n = min(4, NB - 4 * c) * BL
                    act.activation(s.aggT[:, c * 4 * BL:c * 4 * BL + n], bank(s, 2 + c % 6, 128, 0, n),
                                   ACT.Copy).then_inc(rows_kept, 1)
            act.end_ifs()

        @block.tensor
        def _(pe):
            def sums(c, b, n):
                pe.wait_ge(scaled, c + 1)
                for h in range(NB):
                    rhs = adj[:, bass.ds(c * 4, n), h, :] if n > 1 else s.adj[0:BL, (4 * c) * N + h * BL:
                                                                             (4 * c) * N + (h + 1) * BL]
                    for p in range(2):
                        pe.matmul(bank(s, b, 128, 0, n * BL), s.h2[:, h, p * HID:(p + 1) * HID], rhs,
                                  start=(h == 0 and p == 0), stop=False, skip_group_check=True)
                for k in range(n):
                    for p in range(2):
                        mm = pe.matmul(bank(s, b, 128, k * BL, BL), blk(s.h2[:, :, p * HID:(p + 1) * HID], c * 4 + k),
                                       s.ident16[0:BL, 0:BL], start=False, stop=(k == n - 1 and p == 1),
                                       skip_group_check=True)
                mm.then_inc(conv, 1)

            covered = pe.value_load(s.flag[0:1, 0:1])
            with pe.If(covered == E):
                for j in range(NB):
                    if j == NB - 1:
                        pe.wait_ge(rows_kept, 1)
                    mm = pe.transpose(bank(s, 2 + j // 4 % 6, 128, j % 4 * BL, BL), s.dinvN[:, j:j + 1].to_broadcast([BL, 128]),
                                      s.ident[0:BL, 0:BL])
                    if j % 4 == 3 or j == NB - 1:
                        mm.then_inc(rows_mm, 1)

                with pe.Fori(0, 3) as r:
                    sums(2 * r, 0, 4)
                    sums(2 * r + 1, 1, 4)
                pe.wait_ge(rows_kept, 7)
            pe.end_ifs()
            pe.wait_ge(got["WxT"], 16)
            pe.wait_ge(got["Wsl"], 16)
            for k in range(KC):
                for h in range(FH):
                    mm = pe.matmul(bank(s, 4 + k, 128, h * G, G), WxT[:, h, k * 128:(k + 1) * 128], Wsl,
                                   start=True, stop=True)
            mm.then_inc(logits, 1)
            pe.wait_ge(spread, 1)
            for h in range(FH):
                mm = pe.matmul(bank(s, 6, BL, h * G, G), bxB[:, h, :], Wsl, start=True, stop=True)
            mm.then_inc(biases, 1)
            with pe.If(covered == E):
                sums(6, 0, 1)
            pe.end_ifs()


def general(nc, s):
    t = s.t
    with ExitStack() as ctx:
        def sem(name):
            return semaphore(nc, s, "ge_" + name)

        s.used = 0
        src = take(s, 128, [GC], I32)
        dst_i = take(s, 128, [GC], I32)
        dst = take(s, 128, [GC])
        iota_i = take(s, 128, [N], I32)
        iota = take(s, 128, [N])
        hot = take(s, 128, [N])
        idx = take(s, 128, [1], I32)
        got = take(s, 128, [HID])
        ratio = take(s, BL, [NB])
        dinv = take(s, BL, [NB])
        rowsT = take(s, 128, [N])
        table = take(s, BL, [NB, HID])
        zeros = take(s, 128, [128])
        CN = [(c * 500, min(500, N - c * 500)) for c in range(7)]
        in_s, iota_r, step, idx_r, got_r = sem("in"), sem("iota"), sem("step"), sem("idx"), sem("got")
        hot_r, mm_r, sums_r, pow_r, cols_r = sem("hot"), sem("mm"), sem("sums"), sem("pow"), sem("cols")
        rows_r, tr_r, table_r, table_d, read, ready = (sem(x) for x in ("rows", "tr", "table", "tabled", "read", "ready"))
        fold = Fold(nc, s, "ge_")
        block = ctx.enter_context(nc.Block())

        @block.sync
        def _(sp):
            covered = sp.value_load(s.flag[0:1, 0:1])
            with sp.If(covered != E):
                sp.dma_start(src, t["src_all"]).then_inc(in_s, 16)
                sp.wait_ge(in_s, 16)
                sp.dma_start(dst_i, t["dst_all"]).then_inc(in_s, 16)
                for p in range(2):
                    sp.wait_ge(table_r, p + 1)
                    sp.dma_start(s.table_d.rearrange("(b p) c -> p b c", p=BL), table).then_inc(table_d, 16)
                sp.wait_ge(table_d, 32)
            sp.end_ifs()

        @block.gpsimd
        def _(pool):
            covered = pool.value_load(s.flag[0:1, 0:1])
            with pool.If(covered != E):
                pool.iota(iota_i, pattern=[[1, N]], base=0, channel_multiplier=0).then_inc(iota_r, 1)
                pool.wait_ge(sums_r, 1)
                pool.tensor_tensor(s.aggT[:, :], s.aggT[:, :], s.half[:, 0:1].to_broadcast([128, N]),
                                   ALU.pow).then_inc(pow_r, 1)
                for p in range(2):
                    pool.wait_ge(table_d, 16 * (p + 1))
                    with pool.Fori(0, GC) as c:
                        pool.wait_ge(mm_r, c + 1 + (p + 1) * (GC + 1))
                        pool.tensor_copy(idx, src[:, bass.ds(c, 1)]).then_inc(idx_r, 1)
                        hold(pool, s.held, (idx_r, c + 1 + p * GC))
                        pool.indirect_dma_start(out=got, out_offset=None, in_=s.table_d,
                                                in_offset=bass.IndirectOffsetOnAxis(ap=idx, axis=0)
                                                ).then_inc(got_r, 16)
                        pool.wait_ge(got_r, 16 * (c + 1 + p * GC))
            pool.end_ifs()

        @block.scalar
        def _(act):
            covered = act.value_load(s.flag[0:1, 0:1])
            with act.If(covered != E):
                fold.take_sums(act)
                fold.take_kx(act)
                fold.take_m(act)
            act.end_ifs()

        @block.vector
        def _(dve):
            covered = dve.value_load(s.flag[0:1, 0:1])
            with dve.If(covered != E):
                chain = [0]

                def link(ins):
                    chain[0] += 1
                    ins.then_inc(step, 1)
                    dve.wait_ge(step, chain[0])

                dve.wait_ge(in_s, 32)
                dve.wait_ge(iota_r, 1)
                link(dve.tensor_copy(dst, dst_i))
                link(dve.memset(zeros, 0.0))
                link(dve.tensor_copy(iota, iota_i))
                dve.sem_inc(ready, 1)
                for p in range(3):
                    with dve.Fori(0, GC) as c:
                        dve.wait_ge(mm_r, c + 1 + p * (GC + 1))
                        dve.tensor_scalar(hot, iota, dst[:, bass.ds(c, 1)], None, ALU.is_equal).then_inc(hot_r, 1)
                    dve.wait_ge(mm_r, (p + 1) * (GC + 1))
                    if p == 0:
                        for c, (a, n) in enumerate(CN):
                            link(dve.tensor_copy(s.aggT[:, a:a + n], bank(s, c, 128, 0, n)))
                        dve.sem_inc(sums_r, 1)
                        dve.wait_ge(cols_r, 1)
                        link(dve.tensor_copy(dinv, bank(s, 7, BL, 0, NB)))
                        link(dve.reciprocal(ratio, s.dinvN[:, :]))
                        link(dve.tensor_tensor(ratio, ratio, dinv, ALU.mult))
                        link(dve.tensor_tensor(table, s.h1[:, :, 0:HID], s.h1[:, :, HID:2 * HID], ALU.add))
                        link(dve.tensor_tensor(table, table, bc(ratio, HID), ALU.mult))
                        dve.sem_inc(table_r, 1)
                        dve.sem_inc(mm_r, 1)
                    if p == 1:
                        for c, (a, n) in enumerate(CN):
                            link(dve.tensor_copy(rowsT[:, a:a + n], bank(s, c, 128, 0, n)))
                        dve.sem_inc(rows_r, 1)
                        dve.wait_ge(table_d, 16)
                        for b in range(NB):
                            dve.wait_ge(tr_r, b + 1)
                            v = table[:, b, :]
                            link(dve.scalar_tensor_tensor(v, bank(s, 7, BL, 0, HID), dinv[:, b:b + 1], s.sb1[:, :],
                                                          ALU.mult, ALU.add))
                            dve.sem_inc(read, 1)
                            link(dve.tensor_scalar(v, v, 0.0, dinv[:, b:b + 1], ALU.max, ALU.mult))
                        dve.sem_inc(table_r, 1)
                        dve.sem_inc(mm_r, 1)
                    if p == 2:
                        for c, (a, n) in enumerate(CN):
                            v = s.aggT[:, a:a + n]
                            link(dve.scalar_tensor_tensor(v, bank(s, c, 128, 0, n), s.inv_s[:, 0:1], v, ALU.mult, ALU.mult))
            dve.end_ifs()

        @block.tensor
        def _(pe):
            covered = pe.value_load(s.flag[0:1, 0:1])
            with pe.If(covered != E):
                fold.multiply_kx(pe)
                for k in range(KC):
                    fold.multiply_m(pe, k)
                pe.wait_ge(fold.m_r, 1)
                pe.wait_ge(ready, 1)
                pe.sem_inc(mm_r, 1)
                for p in range(3):
                    lhsT = s.ones[:, :] if p == 0 else got
                    if p:
                        pe.wait_ge(mm_r, p * (GC + 1) + 1)
                    for c, (a, n) in enumerate(CN):
                        pe.matmul(bank(s, c, 128, 0, n), zeros, iota[:, a:a + n], start=True, stop=False,
                                  skip_group_check=True)
                    with pe.Fori(0, GC) as k:
                        pe.wait_ge(hot_r, k + 1 + p * GC)
                        if p:
                            pe.wait_ge(got_r, 16 * (k + 1 + (p - 1) * GC))
                        for c, (a, n) in enumerate(CN):
                            mm = pe.matmul(bank(s, c, 128, 0, n), lhsT, hot[:, a:a + n], start=False, stop=False,
                                           skip_group_check=True)
                        mm.then_inc(mm_r, 1)
                    if p == 0:
                        pe.wait_ge(pow_r, 1)
                        for b in range(NB):
                            mm = pe.matmul(bank(s, 7, BL, b, 1), s.aggT[0:1, b * BL:(b + 1) * BL], s.ones[0:1, 0:1],
                                           start=True, stop=True)
                        mm.then_inc(cols_r, 1)
                    if p == 1:
                        pe.wait_ge(rows_r, 1)
                        for b in range(NB):
                            if b:
                                pe.wait_ge(read, b)
                            pe.transpose(bank(s, 7, BL, 0, HID), rowsT[:, b * BL:(b + 1) * BL],
                                         s.ident[:, :]).then_inc(tr_r, 1)
            pe.end_ifs()


def slices(nc, s):
    t = s.t
    with ExitStack() as ctx:
        def sem(name):
            return semaphore(nc, s, "sl_" + name)

        s.used = 0
        s.x2 = take(s, BL, [NB, D])
        s.swT = take(s, 128, [NB, 2 * INNER // 128 * BL], F16)
        s.wsum = take(s, BL, [INNER])
        s.UT = take(s, 128, [KC, INNER])
        s.Wfx = take(s, 128, [KC, INNER])
        s.Wq, s.Wk, s.Wv2 = take(s, G, [G]), take(s, G, [G]), take(s, G, [2 * G])
        s.Wout = take(s, 128, [FH // 2, D])
        s.bfx = take(s, G, [FH])
        s.keep = s.used
        agg = take(s, 128, [U, BL])
        xnT = take(s, 128, [U, KC * BL])
        x1 = take(s, BL, [U, D])
        W2 = take(s, 128, [D])
        st = take(s, BL, [U, 6])
        mv = take(s, BL, [U, 2])
        ve = take(s, BL, [U])
        rstd = take(s, BL, [U])
        y = take(s, BL, [U, D])
        lg = take(s, BL, [U, INNER])
        y16 = take(s, BL, [U, 2 * D], F16)
        yT = take(s, 128, [U, 2 * KC * BL], F16)
        sw16 = take(s, BL, [U, 2 * INNER], F16)
        Wc16 = take(s, 128, [2, KC * INNER], F16)
        top, top1, inv_c, scale_c, inv_l = (take(s, 128, [1]) for _ in range(5))
        mx = take(s, BL, [U, FH])
        sm = take(s, BL, [U, FH])
        rc = take(s, BL, [U, FH])
        G2, TP, LG, UTB, SWT = 0, [1, 2], [3, 4], 5, 7
        names = ("agg", "w2", "x2", "st", "mv", "ve", "rstd", "y", "tp", "yT", "lgmm", "lg", "mx", "sub", "ex", "sm", "rc",
                 "sw", "swt", "swT", "ut", "acc", "xb", "yh", "yl", "swh", "swl")
        (agg_r, w2_r, x2_r, st_r, mv_r, ve_r, rstd_r, y_r, tp_r, yT_r, lgmm_r, lg_r, mx_r, sub_r, ex_r, sm_r, rc_r,
         sw_r, swt_r, swT_r, ut_r, acc_r, xb_r, yh_r, yl_r, swh_r, swl_r) = sems = [sem(x) for x in names]
        loaded, loaded_t, kept = ([sem(f"{x}{u}") for u in range(U)] for x in ("inx", "int", "keep"))
        in_w2 = sem("inw2")
        zeroed, ut_kept, in_tok = sem("zeroed"), sem("utkept"), sem("intok")
        token_loads = [(s.Wfx, t["W_fx"].rearrange("(k p) n -> p k n", p=128)), (s.Wq, t["W_q"]), (s.Wk, t["W_k"]),
                       (s.Wv2[:, 0:G], t["W_v"]), (s.Wv2[:, G:2 * G], t["W_v"]),
                       (s.Wout, t["W_out"].rearrange("(c p) n -> p c n", p=128)), (s.bfx, t["bfxT"])]
        top_r, top_mm, scale_r, wc_hi, wc_lo = sem("top"), sem("topmm"), sem("scale"), sem("wchi"), sem("wclo")
        PARTS = ((0, 0), (0, 1), (1, 0))
        Wc = s.Wc.rearrange("p k n -> p (k n)")
        block = ctx.enter_context(nc.Block())

        def heads(ap):
            return ap.rearrange("p (h g) -> p h g", g=G)

        def transposed(b, n):
            return bank(s, b).bitcast(F16)[:, 0:n * (BL + 1)].rearrange("p (n c) -> p n c", c=BL + 1)[:, :, 0:BL]

        def parts(ap):
            return ap.rearrange("p (n c) -> p n c", c=BL)

        @block.sync
        def _(sp):
            start_at(sp, sems)
            start_at(sp, kept, 16)
            sp.dma_start(W2, t["W2"]).then_inc(in_w2, 16)

            def load(i, u, r):
                sp.wait_ge(kept[u], r * 16 + 16)
                sp.wait_ge(y_r, at(i) - U)
                sp.dma_start(x1[:, u, :], rows(t["x"], i)).then_inc(loaded[u], 16)
                sp.wait_ge(w2_r, at(i) - U)
                sp.dma_start(xnT[:, u, :], s.xnT_d.rearrange("(b p) c -> b p c", p=128)[bass.ds(i, 1)]
                             .rearrange("a p c -> (a p) c")).then_inc(loaded_t[u], 16)

            def keep(i, u, r):
                sp.wait_ge(x2_r, at(i))
                sp.dma_start(blk(s.x2, i), x1[:, u, :]).then_inc(kept[u], 16)

            pipelined(sp, (0, load), (4, keep))
            for dst, src in token_loads:
                sp.dma_start(dst, src).then_inc(in_tok, 16)
            sp.wait_ge(in_tok, 16 * len(token_loads))
            for u in range(U):
                sp.wait_ge(kept[u], 16 * IT + 16)

        @block.scalar
        def _(act):
            def static(i, u, r):
                act.wait_ge(w2_r, at(i) - U)
                act.activation(agg[:, u, :], s.aggT[:, bass.ds(i * BL, BL)], ACT.Copy).then_inc(agg_r, 1)

            def y_high(i, u, r):
                act.wait_ge(y_r, at(i))
                act.wait_ge(acc_r, at(i) - U)
                act.activation(y16[:, u, 0:D], y[:, u, :], ACT.Copy).then_inc(yh_r, 1)

            def turned(i, u, r):
                act.wait_ge(tp_r, at(i))
                act.wait_ge(lgmm_r, at(i) - U)
                act.activation(parts(yT[:, u, :]), transposed(TP[TWO[u]], 2 * KC), ACT.Copy).then_inc(yT_r, 1)

            def weights_high(i, u, r):
                act.wait_ge(sw_r, at(i))
                act.wait_ge(acc_r, at(i) - U)
                act.activation(sw16[:, u, 0:INNER], lg[:, u, :], ACT.Copy).then_inc(swh_r, 1)

            def exponent(i, u, r):
                act.wait_ge(sub_r, at(i))
                act.activation(lg[:, u, :], lg[:, u, :], ACT.Exp).then_inc(ex_r, 1)

            def weights_turned(i, u, r):
                act.wait_ge(swt_r, at(i))
                act.activation(parts(blk(s.swT, i)), transposed(SWT, 8), ACT.Copy).then_inc(swT_r, 1)

            act.wait_ge(scale_r, 1)
            act.activation(Wc16[:, 0, :], Wc, ACT.Copy, scale=scale_c).then_inc(wc_hi, 1)
            pipelined(act, (0, static), (3, weights_high), (1, y_high), (1, turned), (2, exponent), (4, weights_turned))
            act.wait_ge(acc_r, NB + U)
            act.activation(s.UT.rearrange("p k n -> p (k n)"), s.PS[:, UTB * BANK:(UTB + 2) * BANK],
                           ACT.Copy, scale=1.0 / Y_SCALE).then_inc(ut_kept, 1)
            act.wait_ge(ut_kept, 1)

        @block.vector
        def _(dve):
            def residual(i, u, r):
                dve.wait_ge(w2_r, at(i))
                dve.wait_ge(xb_r, at(i))
                dve.tensor_tensor(x1[:, u, :], bank(s, G2, BL, 0, D), x1[:, u, :], ALU.add).then_inc(x2_r, 1)

            def statistics(i, u, r):
                dve.wait_ge(x2_r, at(i))
                dve.bn_stats(st[:, u, :], x1[:, u, :]).then_inc(st_r, 1)

            def aggregate(i, u, r):
                hold(dve, s.held, (st_r, at(i)), (y_r, at(i) - U))
                dve.bn_aggr(mv[:, u, :], st[:, u, :]).then_inc(mv_r, 1)

            def norm(i, u, r):
                dve.wait_ge(rstd_r, at(i))
                dve.wait_ge(yl_r, at(i) - U)
                dve.tensor_scalar(y[:, u, :], x1[:, u, :], mv[:, u, 0:1], rstd[:, u:u + 1], ALU.subtract,
                                  ALU.mult).then_inc(y_r, 1)

            def logits(i, u, r):
                dve.wait_ge(lgmm_r, at(i))
                dve.wait_ge(ut_r, at(i) - U)
                dve.wait_ge(swl_r, at(i) - U)
                dve.scalar_tensor_tensor(lg[:, u, :], bank(s, LG[TWO[u]], BL), inv_l[0:BL, :], s.biasC[:, :], ALU.mult,
                                         ALU.add).then_inc(lg_r, 1)

            def maxima(i, u, r):
                dve.wait_ge(lg_r, at(i))
                dve.tensor_reduce(mx[:, u, :], heads(lg[:, u, :]), AX.X, ALU.max).then_inc(mx_r, 1)

            def less_maxima(i, u, r):
                dve.wait_ge(mx_r, at(i))
                dve.tensor_tensor(heads(lg[:, u, :]), heads(lg[:, u, :]), bc(mx[:, u, :], G),
                                  ALU.subtract).then_inc(sub_r, 1)

            def exponent_sums(i, u, r):
                dve.wait_ge(ex_r, at(i))
                dve.tensor_reduce(sm[:, u, :], heads(lg[:, u, :]), AX.X, ALU.add).then_inc(sm_r, 1)

            def over_sums(i, u, r):
                dve.wait_ge(sm_r, at(i))
                dve.reciprocal(rc[:, u, :], sm[:, u, :]).then_inc(rc_r, 1)

            def weigh(i, u, r):
                dve.wait_ge(rc_r, at(i))
                dve.scalar_tensor_tensor(heads(lg[:, u, :]), heads(lg[:, u, :]), SW_SCALE, bc(rc[:, u, :], G),
                                         ALU.mult, ALU.mult).then_inc(sw_r, 1)

            dve.tensor_reduce(top, Wc, AX.X, ALU.max, apply_absolute_value=True).then_inc(top_r, 1)
            dve.wait_ge(top_mm, 1)
            dve.tensor_reduce(top1[0:1, :], bank(s, SWT, 1, 0, 128), AX.X, ALU.max).then_inc(top_r, 1)
            dve.wait_ge(top_mm, 2)
            dve.tensor_scalar(inv_c, bank(s, SWT, 128, 128, 1), 1e-30, 1.0 / LIMIT, ALU.max, ALU.mult).then_inc(top_r, 1)
            dve.wait_ge(top_r, 3)
            dve.reciprocal(scale_c, inv_c).then_inc(scale_r, 1)
            dve.tensor_scalar(inv_l, inv_c, 1.0 / Y_SCALE, None, ALU.mult).then_inc(top_r, 1)
            dve.wait_ge(top_r, 4)
            dve.wait_ge(wc_hi, 1)
            dve.scalar_tensor_tensor(Wc16[:, 1, :], Wc, scale_c, Wc16[:, 0, :], ALU.mult, ALU.subtract).then_inc(wc_lo, 1)
            pipelined(dve, (3, exponent_sums), (3, over_sums), (3, weigh), (1, norm), (2, logits), (2, maxima),
                      (0, residual), (2, less_maxima), (0, statistics), (0, aggregate))

        @block.gpsimd
        def _(pool):
            pool.memset(s.wsum, 0.0).then_inc(zeroed, 1)
            pool.wait_ge(zeroed, 1)

            def add_biases(i, u, r):
                pool.wait_ge(loaded[u], r * 16 + 16)
                pool.tensor_tensor(x1[:, u, :], x1[:, u, :], s.bsum[:, :], ALU.add).then_inc(xb_r, 1)

            def one_over_std(i, u, r):
                hold(pool, s.held, (mv_r, at(i)))
                pool.tensor_scalar(ve[:, u:u + 1], mv[:, u, 1:2], EPS, Y_SCALE ** -2, ALU.add, ALU.mult).then_inc(ve_r, 1)
                pool.wait_ge(ve_r, at(i))
                pool.wait_ge(y_r, at(i) - U)
                pool.tensor_tensor(rstd[:, u:u + 1], ve[:, u:u + 1], s.half[0:BL, 0:1], ALU.pow).then_inc(rstd_r, 1)

            def y_low(i, u, r):
                pool.wait_ge(yh_r, at(i))
                pool.tensor_tensor(y16[:, u, D:2 * D], y[:, u, :], y16[:, u, 0:D], ALU.subtract).then_inc(yl_r, 1)

            def weights_low(i, u, r):
                pool.wait_ge(swh_r, at(i))
                pool.tensor_tensor(sw16[:, u, INNER:2 * INNER], lg[:, u, :], sw16[:, u, 0:INNER],
                                   ALU.subtract).then_inc(swl_r, 1)

            def total(i, u, r):
                pool.wait_ge(sw_r, at(i))
                pool.wait_ge(ut_r, at(i) - 1)
                pool.tensor_tensor(s.wsum, s.wsum, lg[:, u, :], ALU.add).then_inc(ut_r, 1)

            pipelined(pool, (1, one_over_std), (4, total), (0, add_biases), (1, y_low), (3, weights_low))

        @block.tensor
        def _(pe):
            pe.wait_ge(top_r, 1)
            pe.transpose(bank(s, SWT, 1, 0, 128), top, s.ident[:, :]).then_inc(top_mm, 1)
            pe.wait_ge(top_r, 2)
            pe.matmul(bank(s, SWT, 128, 128, 1), s.ones[0:1, :], top1[0:1, :], start=True, stop=True).then_inc(top_mm, 1)
            pe.wait_ge(in_w2, 16)

            def gcn_out(i, u, r):
                pe.wait_ge(agg_r, at(i))
                pe.wait_ge(x2_r, at(i) - 1)
                pe.wait_ge(loaded_t[u], r * 16 + 16)
                for k in range(KC):
                    pe.matmul(bank(s, G2, BL, 0, D), xnT[:, u, k * BL:(k + 1) * BL], s.M[:, k, :], start=(k == 0),
                              stop=False)
                pe.matmul(bank(s, G2, BL, 0, D), agg[:, u, :], W2, start=False, stop=True).then_inc(w2_r, 1)

            def turn(i, u, r):
                pe.wait_ge(yl_r, at(i))
                pe.wait_ge(yT_r, at(i) - before(TWO, u))
                for k in range(2 * KC):
                    mm = pe.transpose(transposed(TP[TWO[u]], 2 * KC)[:, k, :],
                                      y16[:, u, k * 128:(k + 1) * 128], s.ident16[0:BL, 0:BL])
                mm.then_inc(tp_r, 1)

            def logits(i, u, r):
                pe.wait_ge(yT_r, at(i))
                pe.wait_ge(lg_r, at(i) - before(TWO, u))
                for k in range(KC):
                    for n, (p, q) in enumerate(PARTS):
                        mm = pe.matmul(bank(s, LG[TWO[u]], BL), yT[:, u, (p * KC + k) * BL:(p * KC + k + 1) * BL],
                                       Wc16[:, q, k * INNER:(k + 1) * INNER], start=(k == 0 and n == 0),
                                       stop=(k == KC - 1 and n == 2))
                mm.then_inc(lgmm_r, 1)

            def sums(i, u, r):
                pe.wait_ge(swl_r, at(i))
                pe.wait_ge(swT_r, at(i) - 1)
                for c in range(8):
                    mm = pe.transpose(transposed(SWT, 8)[:, c, :], sw16[:, u, c * 128:(c + 1) * 128],
                                      s.ident16[0:BL, 0:BL])
                mm.then_inc(swt_r, 1)
                for k in range(KC):
                    for n, (p, q) in enumerate(PARTS):
                        mm = pe.matmul(bank(s, UTB + k), y16[:, u, p * D + k * 128:p * D + (k + 1) * 128],
                                       sw16[:, u, q * INNER:(q + 1) * INNER],
                                       start=isinstance(i, int) and i == 0 and n == 0,
                                       stop=isinstance(i, int) and i == NB - 1 and n == 2, skip_group_check=True)
                mm.then_inc(acc_r, 1)

            pe.wait_ge(wc_lo, 1)
            pipelined(pe, (2, logits), (0, gcn_out), (1, turn), (4, sums))


def tokens_and_output(nc, s):
    t = s.t
    with ExitStack() as ctx:
        def sem(name):
            return semaphore(nc, s, "to_" + name)

        s.used = s.keep
        PAIRS = FH // 2
        nrm = take(s, G, [INNER])
        rn = take(s, 128, [PAIRS])
        tok = take(s, G, [INNER])
        qT, kT = (take(s, G, [INNER]) for _ in range(2))
        v2 = take(s, 128, [PAIRS, 128])
        a2 = take(s, 128, [PAIRS, 128])
        sc = take(s, G, [INNER])
        mx = take(s, G, [FH])
        sm = take(s, G, [FH])
        vW = take(s, 128, [PAIRS, D])
        T16 = take(s, 128, [2, PAIRS * D], F16)
        top, top1, inv_T, scale_T, inv_o = (take(s, 128, [1]) for _ in range(5))
        o = take(s, BL, [U, D])
        bout = take(s, BL, [D])
        step, rn_r, tok_r, qk_r, v2_r, ex_r, attn_r, a2_r, vW_r = (
            sem(x) for x in ("s", "rn", "tok", "qk", "v2", "ex", "at", "a2", "vW"))
        m_c, m_n, m_r, m_t, m_q, m_s, m_a, m_v, m_T, zeroed, sub_r = (
            sem(x) for x in ("mc", "mn", "mr", "mt", "mq", "ms", "ma", "mv", "mT", "zero", "sub"))
        in_b, mm_r, o_r, xb_r = sem("bout"), sem("mm"), sem("o"), sem("xb")
        sent = [sem(f"s{u}") for u in range(U)]
        top_r, top_mm, scale_r, T_hi, T_lo = sem("top"), sem("topmm"), sem("scale"), sem("Thi"), sem("Tlo")
        OB = [6, 7]
        block = ctx.enter_context(nc.Block())

        def heads(ap):
            return ap.rearrange("p (h g) -> p h g", g=G)

        def diagonal(ap, a):
            return ap[a * G:(a + 1) * G, :, a * G:(a + 1) * G]

        @block.sync
        def _(sp):
            start_at(sp, [mm_r, o_r, xb_r])
            sp.dma_start(bout, t["b_out"].partition_broadcast(BL)).then_inc(in_b, 16)
            start_at(sp, sent, 16)

        @block.gpsimd
        def _(pool):
            pool.memset(v2, 0.0).then_inc(zeroed, 1)
            pool.memset(a2, 0.0).then_inc(zeroed, 1)
            pool.wait_ge(in_b, 16)

            def add_bias(i, u, r):
                pool.tensor_tensor(blk(s.x2, i), blk(s.x2, i), bout, ALU.add).then_inc(xb_r, 1)

            pipelined(pool, (0, add_bias))

        @block.vector
        def _(dve):
            chain = [0]

            def link(ins):
                chain[0] += 1
                ins.then_inc(step, 1)
                dve.wait_ge(step, chain[0])

            dve.wait_ge(m_c, 1)
            link(dve.tensor_scalar(rn, bank(s, 5, 128, 0, PAIRS), EPS * SW_SCALE, None, ALU.add))
            dve.reciprocal(rn, rn).then_inc(rn_r, 1)
            dve.wait_ge(m_n, 1)
            link(dve.tensor_tensor(heads(nrm), heads(bank(s, 0, G)), bc(s.bfx, G), ALU.mult))
            dve.wait_ge(m_t, 1)
            link(dve.tensor_tensor(nrm, nrm, bank(s, 1, G), ALU.add))
            dve.wait_ge(m_r, 1)
            dve.tensor_tensor(tok, nrm, bank(s, 6, G), ALU.mult).then_inc(tok_r, 1)
            dve.wait_ge(m_q, 1)
            dve.tensor_copy(qT, bank(s, 2, G)).then_inc(qk_r, 1)
            dve.wait_ge(zeroed, 2)
            dve.wait_ge(m_q, 2)
            for a in range(2):
                dve.tensor_copy(diagonal(v2, a), bank(s, 4)[a * G:(a + 1) * G].rearrange(
                    "p (c a g) -> p c a g", a=2, g=G)[:, :, a, :]).then_inc(v2_r, 1)
            dve.wait_ge(m_s, 1)
            link(dve.tensor_scalar(sc, bank(s, 5, G), G ** -0.5, None, ALU.mult))
            link(dve.tensor_reduce(mx, heads(sc), AX.X, ALU.max))
            dve.tensor_tensor(heads(sc), heads(sc), bc(mx, G), ALU.subtract).then_inc(sub_r, 1)
            dve.wait_ge(ex_r, 1)
            link(dve.tensor_reduce(sm, heads(sc), AX.X, ALU.add))
            link(dve.reciprocal(mx, sm))
            dve.tensor_tensor(heads(sc), heads(sc), bc(mx, G), ALU.mult).then_inc(attn_r, 1)
            dve.wait_ge(m_a, 1)
            for a in range(2):
                dve.tensor_copy(diagonal(a2, a), bank(s, 0)[a * G:(a + 1) * G, 0:PAIRS * G].rearrange(
                    "p (c g) -> p c g", g=G)).then_inc(a2_r, 1)
            dve.wait_ge(vW_r, 1)
            dve.tensor_reduce(top, vW.rearrange("p c n -> p (c n)"), AX.X, ALU.max, apply_absolute_value=True).then_inc(top_r, 1)
            dve.wait_ge(top_mm, 1)
            dve.tensor_reduce(top1[0:1, :], bank(s, 1, 1, 0, 128), AX.X, ALU.max).then_inc(top_r, 1)
            dve.wait_ge(top_mm, 2)
            dve.tensor_scalar(inv_T, bank(s, 1, 128, 128, 1), 1e-30, 1.0 / LIMIT, ALU.max, ALU.mult).then_inc(top_r, 1)
            dve.wait_ge(top_r, 3)
            dve.reciprocal(scale_T, inv_T).then_inc(scale_r, 1)
            dve.tensor_scalar(inv_o, inv_T, 1.0 / SW_SCALE, None, ALU.mult).then_inc(top_r, 1)
            dve.wait_ge(top_r, 4)
            for b in range(2):
                dve.wait_ge(T_hi, b + 1)
                dve.scalar_tensor_tensor(T16[:, 1, b * BANK:(b + 1) * BANK], bank(s, 4 + b), scale_T,
                                         T16[:, 0, b * BANK:(b + 1) * BANK], ALU.mult, ALU.subtract).then_inc(T_lo, 1)

            def add(i, u, r):
                dve.wait_ge(mm_r, at(i))
                dve.wait_ge(xb_r, at(i))
                dve.wait_ge(sent[u], r * 16 + 16)
                dve.scalar_tensor_tensor(o[:, u, :], bank(s, OB[TWO[u]], BL, 0, D), inv_o[0:BL, :], blk(s.x2, i), ALU.mult,
                                         ALU.add).then_inc(o_r, 1)

            pipelined(dve, (0, add))

        @block.scalar
        def _(act):
            act.wait_ge(m_q, 1)
            act.activation(kT, bank(s, 3, G), ACT.Copy).then_inc(qk_r, 1)
            act.wait_ge(sub_r, 1)
            act.activation(sc, sc, ACT.Exp).then_inc(ex_r, 1)
            act.wait_ge(m_v, 1)
            act.activation(vW.rearrange("p c n -> p (c n)"), s.PS[:, 2 * BANK:4 * BANK], ACT.Copy).then_inc(vW_r, 1)
            act.wait_ge(scale_r, 1)
            for b in range(2):
                act.wait_ge(m_T, b + 1)
                act.activation(T16[:, 0, b * BANK:(b + 1) * BANK], bank(s, 4 + b), ACT.Copy, scale=scale_T).then_inc(T_hi, 1)

            def send(i, u, r):
                act.wait_ge(o_r, at(i))
                act.dma_start(rows(s.out, i), o[:, u, :]).then_inc(sent[u], 16)

            pipelined(act, (0, send))
            for u in range(U):
                act.wait_ge(sent[u], 16 * IT + 16)

        @block.tensor
        def _(pe):
            for c in range(PAIRS):
                mm = pe.matmul(bank(s, 5, 128, c, 1), s.wsum[:, c * 128:(c + 1) * 128], s.ones[0:BL, 0:1], start=True, stop=True)
            mm.then_inc(m_c, 1)
            pe.matmul(bank(s, 0, G), s.ones[0:BL, 0:G], s.wsum, start=True, stop=True).then_inc(m_n, 1)
            pe.wait_ge(rn_r, 1)
            for c in range(PAIRS):
                mm = pe.transpose(bank(s, 6, G, c * 128, 128), rn[:, c:c + 1].to_broadcast([128, G]), s.ident[:, :])
            mm.then_inc(m_r, 1)
            for h in range(FH):
                for k in range(KC):
                    mm = pe.matmul(bank(s, 1, G, h * G, G), s.Wfx[:, k, h * G:(h + 1) * G], s.UT[:, k, h * G:(h + 1) * G],
                                   start=(k == 0), stop=(k == KC - 1))
            mm.then_inc(m_t, 1)
            pe.wait_ge(tok_r, 1)
            pe.matmul(bank(s, 2, G), s.Wq, tok, start=True, stop=True)
            pe.matmul(bank(s, 3, G), s.Wk, tok, start=True, stop=True).then_inc(m_q, 1)
            pe.matmul(bank(s, 4), s.Wv2, tok, start=True, stop=True).then_inc(m_q, 1)
            pe.wait_ge(qk_r, 2)
            for h in range(FH):
                mm = pe.matmul(bank(s, 5, G, h * G, G), qT[:, h * G:(h + 1) * G], kT[:, h * G:(h + 1) * G],
                               start=True, stop=True)
            mm.then_inc(m_s, 1)
            pe.wait_ge(v2_r, 2)
            for c in range(PAIRS):
                mm = pe.matmul(s.PS[:, 2 * BANK + c * D:2 * BANK + (c + 1) * D], v2[:, c, :], s.Wout[:, c, :],
                               start=True, stop=True)
            mm.then_inc(m_v, 1)
            pe.wait_ge(attn_r, 1)
            for c in range(PAIRS):
                mm = pe.transpose(bank(s, 0, 128, c * G, G), sc[:, c * 128:(c + 1) * 128], s.ident[0:G, 0:G])
            mm.then_inc(m_a, 1)
            pe.wait_ge(a2_r, 2)
            pe.wait_ge(vW_r, 1)
            for c in range(PAIRS):
                if c == 2:
                    pe.wait_ge(top_r, 1)
                    pe.transpose(bank(s, 1, 1, 0, 128), top, s.ident[:, :]).then_inc(top_mm, 1)
                if c == 3:
                    pe.wait_ge(top_r, 2)
                    pe.matmul(bank(s, 1, 128, 128, 1), s.ones[0:1, :], top1[0:1, :], start=True,
                              stop=True).then_inc(top_mm, 1)
                mm = pe.matmul(bank(s, 4 + c // 2, 128, c % 2 * D, D), a2[:, c, :], vW[:, c, :], start=True, stop=True)
                if c % 2 == 1:
                    mm.then_inc(m_T, 1)
            pe.wait_ge(T_lo, 2)

            def mix(i, u, r):
                pe.wait_ge(o_r, at(i) - before(TWO, u))
                w = blk(s.swT, i)
                for c in range(PAIRS):
                    for n, (p, q) in enumerate(((0, 0), (0, 1), (1, 0))):
                        mm = pe.matmul(bank(s, OB[TWO[u]], BL, 0, D), w[:, (p * PAIRS + c) * BL:(p * PAIRS + c + 1) * BL],
                                       T16[:, q, c * D:(c + 1) * D], start=(c == 0 and n == 0),
                                       stop=(c == PAIRS - 1 and n == 2))
                mm.then_inc(mm_r, 1)

            pipelined(pe, (0, mix))


def kernel(x, src, dst, L0_gnn_W1, L0_gnn_b1, L0_gnn_W2, L0_gnn_b2, L0_mix_wq, L0_mix_wk, L0_mix_wv, L0_mix_wo, L0_mix_bo,
           L0_mix_ln_k_g, L0_mix_ln_k_b, L0_mix_ln_v_g, L0_mix_ln_v_b, L0_ffn_W_fx, L0_ffn_b_fx, L0_ffn_W_x, L0_ffn_b_x,
           L0_ffn_W_slice, L0_ffn_b_slice, L0_ffn_W_q, L0_ffn_W_k, L0_ffn_W_v, L0_ffn_W_out, L0_ffn_b_out,
           L0_ffn_temperature):
    import numpy as np
    import concourse.bacc as bacc
    from concourse.bass_utils import run_bass_kernel_spmd

    src, dst = np.asarray(src), np.asarray(dst)
    loops = np.arange(N, dtype=src.dtype)
    pad = np.zeros(GE - E - N, dtype=src.dtype)
    laid = {
        "x": x, "dst": dst,
        "edges": np.stack([src, dst], axis=1).reshape(-1),
        "firsts": dst[::BL],
        "src_all": np.concatenate([src, loops, pad]).reshape(128, GC),
        "dst_all": np.concatenate([dst, loops, pad - 1]).reshape(128, GC),
        "W1": L0_gnn_W1, "b1": L0_gnn_b1, "W2": L0_gnn_W2, "b2": L0_gnn_b2,
        "wq": L0_mix_wq, "wkvT": np.concatenate([np.asarray(L0_mix_wk).T, np.asarray(L0_mix_wv).T], axis=1),
        "woT": np.asarray(L0_mix_wo).T, "bo": L0_mix_bo,
        "ln": np.stack([L0_mix_ln_k_g, L0_mix_ln_k_b, L0_mix_ln_v_g, L0_mix_ln_v_b], axis=1),
        "W_fx": L0_ffn_W_fx, "bfxT": np.asarray(L0_ffn_b_fx).reshape(FH, G).T, "WxT": np.asarray(L0_ffn_W_x).T,
        "bxT": np.asarray(L0_ffn_b_x).reshape(FH, G).T, "W_slice": L0_ffn_W_slice, "b_slice": L0_ffn_b_slice,
        "W_q": L0_ffn_W_q, "W_k": L0_ffn_W_k, "W_v": L0_ffn_W_v, "W_out": L0_ffn_W_out, "b_out": L0_ffn_b_out,
        "temp": np.asarray(L0_ffn_temperature).reshape(FH),
    }
    nc = bacc.Bacc("TRN2", target_bir_lowering=False, num_devices=1)
    arrays, t = {}, {}
    for name, a in laid.items():
        a = np.ascontiguousarray(a)
        arrays["in_" + name] = a
        t[name] = nc.dram_tensor("in_" + name, a.shape, mybir.dt.from_np(a.dtype), kind="ExternalInput").ap()
    out = nc.dram_tensor("out_0", (N, D), F32, kind="ExternalOutput").ap()
    build(nc, t, out)
    return run_bass_kernel_spmd(nc, [arrays], core_ids=[0]).results[0]["out_0"]
```
